# Optimizing a Trainium2 kernel written in Bass

```python
import numpy as np
import jax
import jax.numpy as jnp

def _softmax(x, axis=-1):
    return jax.nn.softmax(x, axis=axis)

def _gelu(x):
    return jax.nn.gelu(x, approximate=True)

def _silu(x):
    return jax.nn.silu(x)

def _sigmoid(x):
    return jax.nn.sigmoid(x)

def _layernorm(x, axis=-1, eps=1e-05):
    m = jnp.mean(x, axis=axis, keepdims=True)
    v = jnp.var(x, axis=axis, keepdims=True)
    return (x - m) / jnp.sqrt(v + eps)

def _scatter_add(tgt, idx, src, axis=0):
    return tgt.at[idx].add(src)

def _segment_sum(src, seg, n):
    return jax.ops.segment_sum(src, seg, n)
kernel_name = 'mk_gps_d1_gnn_r8_33d41a'

def setup_inputs(seed: int=0):
    np.random.seed(seed)
    _w = jnp.asarray

    def _rec_inputs():
        import jax
        import jax.numpy as jnp
        _gk = jax.random.key(seed)
        x = -0.0003713 + 1 * jax.random.normal(jax.random.fold_in(_gk, 1), (6250, 256), jnp.float32)
        src = jax.random.randint(jax.random.fold_in(_gk, 2), (100000,), 0, 6250, jnp.int32)
        dst = jax.random.randint(jax.random.fold_in(_gk, 3), (100000,), 0, 6250, jnp.int32)
        _o = jnp.argsort(dst, stable=True)
        src = src[_o]
        dst = dst[_o]
        return (x, src, dst)
    x, src, dst = _rec_inputs()

    def _L0_gnn_setup():
        import jax, jax.numpy as jnp
        import numpy as np
        N = 6250
        E = 100000
        DIN = 256
        DOUT = 256
        key = jax.random.key(seed)
        k1, k2, k3, k4 = jax.random.split(key, 4)
        x = jax.random.normal(k1, (N, DIN), dtype=jnp.float32)
        src = jax.random.randint(k2, (E,), 0, N, dtype=jnp.int32)
        dst = jax.random.randint(k3, (E,), 0, N, dtype=jnp.int32)
        edge_index = jnp.stack([src, dst])
        gain = 1.414
        limit = gain * np.sqrt(6.0 / (DIN + DOUT))
        W = jax.random.uniform(k4, (DIN, DOUT), dtype=jnp.float32, minval=-limit, maxval=limit)
        return {'x': x, 'W': W, 'edge_index': edge_index}
    _L0_gnn_all = _L0_gnn_setup()
    _L0_gnn_in = {k: v for k, v in _L0_gnn_all.items() if k in ('W',)}
    del _L0_gnn_all

    def _L0_mix_setup():
        import jax, jax.numpy as jnp
        import numpy as np
        D_MODEL = 256
        NUM_HEADS = 8
        DEPTH = D_MODEL // NUM_HEADS
        B, L = (32, 512)

        def _feature_map(x):
            return jax.nn.elu(x) + 1.0
        key = jax.random.key(seed)
        ks = jax.random.split(key, 9)
        sc = 1.0 / np.sqrt(D_MODEL)
        return {'x': jax.random.normal(ks[0], (B, L, D_MODEL), dtype=jnp.float32), 'wq': jax.random.normal(ks[1], (D_MODEL, D_MODEL), dtype=jnp.float32) * sc, 'bq': jnp.zeros((D_MODEL,), dtype=jnp.float32), 'wk': jax.random.normal(ks[2], (D_MODEL, D_MODEL), dtype=jnp.float32) * sc, 'bk': jnp.zeros((D_MODEL,), dtype=jnp.float32), 'wv': jax.random.normal(ks[3], (D_MODEL, D_MODEL), dtype=jnp.float32) * sc, 'bv': jnp.zeros((D_MODEL,), dtype=jnp.float32), 'wo': jax.random.normal(ks[4], (D_MODEL, D_MODEL), dtype=jnp.float32) * sc, 'bo': jnp.zeros((D_MODEL,), dtype=jnp.float32)}
    _L0_mix_all = _L0_mix_setup()
    _L0_mix_in = {k: v for k, v in _L0_mix_all.items() if k in ('wq', 'bq', 'wk', 'bk', 'wv', 'bv', 'wo', 'bo')}
    del _L0_mix_all

    def _L0_ffn_setup():
        import jax, jax.numpy as jnp
        import numpy as np
        TOP_K = 2
        LN_EPS = 1e-05
        key = jax.random.key(seed)
        ks = jax.random.split(key, 8)
        B, S, D, E, H = (16, 1024, 256, 8, 1024)
        x = jax.random.normal(ks[0], (B, S, D), dtype=jnp.float32)
        Wr = jax.random.normal(ks[1], (D, E), dtype=jnp.float32) * 0.1
        br = jnp.zeros((E,), dtype=jnp.float32)
        ln_g = jnp.ones((E, D), dtype=jnp.float32)
        ln_b = jnp.zeros((E, D), dtype=jnp.float32)
        W1 = jax.random.normal(ks[2], (E, D, H), dtype=jnp.float32) * (1.0 / np.sqrt(D))
        b1 = jnp.zeros((E, H), dtype=jnp.float32)
        W2 = jax.random.normal(ks[3], (E, H, D), dtype=jnp.float32) * (1.0 / np.sqrt(H))
        b2 = jnp.zeros((E, D), dtype=jnp.float32)
        return {'x': x, 'Wr': Wr, 'br': br, 'ln_g': ln_g, 'ln_b': ln_b, 'W1': W1, 'b1': b1, 'W2': W2, 'b2': b2}
    _L0_ffn_all = _L0_ffn_setup()
    _L0_ffn_in = {k: v for k, v in _L0_ffn_all.items() if k in ('Wr', 'br', 'ln_g', 'ln_b', 'W1', 'b1', 'W2', 'b2')}
    del _L0_ffn_all
    return {'x': x, 'src': src, 'dst': dst, 'L0_gnn_W': _L0_gnn_in['W'], 'L0_mix_wq': _L0_mix_in['wq'], 'L0_mix_bq': _L0_mix_in['bq'], 'L0_mix_wk': _L0_mix_in['wk'], 'L0_mix_bk': _L0_mix_in['bk'], 'L0_mix_wv': _L0_mix_in['wv'], 'L0_mix_bv': _L0_mix_in['bv'], 'L0_mix_wo': _L0_mix_in['wo'], 'L0_mix_bo': _L0_mix_in['bo'], 'L0_ffn_Wr': _L0_ffn_in['Wr'], 'L0_ffn_br': _L0_ffn_in['br'], 'L0_ffn_ln_g': _L0_ffn_in['ln_g'], 'L0_ffn_ln_b': _L0_ffn_in['ln_b'], 'L0_ffn_W1': _L0_ffn_in['W1'], 'L0_ffn_b1': _L0_ffn_in['b1'], 'L0_ffn_W2': _L0_ffn_in['W2'], 'L0_ffn_b2': _L0_ffn_in['b2']}

def reference(x, src, dst, L0_gnn_W, L0_mix_wq, L0_mix_bq, L0_mix_wk, L0_mix_bk, L0_mix_wv, L0_mix_bv, L0_mix_wo, L0_mix_bo, L0_ffn_Wr, L0_ffn_br, L0_ffn_ln_g, L0_ffn_ln_b, L0_ffn_W1, L0_ffn_b1, L0_ffn_W2, L0_ffn_b2):
    import jax
    import jax.numpy as jnp

    def _L0_gnn_ref(x, W, edge_index):
        import jax, jax.numpy as jnp
        import numpy as np
        N = 6250
        E = 100000
        DIN = 256
        DOUT = 256
        h = x @ W
        n = h.shape[0]
        src, dst = (edge_index[0], edge_index[1])
        mask = (src != dst).astype(h.dtype)
        loops = jnp.arange(n, dtype=src.dtype)
        fsrc = jnp.concatenate([src, loops])
        fdst = jnp.concatenate([dst, loops])
        w_cnt = jnp.concatenate([mask, jnp.ones(n, h.dtype)])
        deg = jax.ops.segment_sum(w_cnt, fdst, num_segments=n)
        dinv = jnp.where(deg > 0, jax.lax.rsqrt(deg), 0.0)
        edge_weight = dinv[fsrc] * dinv[fdst] * w_cnt
        out = jax.ops.segment_sum(edge_weight[:, None] * h[fdst], fsrc, num_segments=n)
        return out

    def _L0_mix_ref(x, wq, bq, wk, bk, wv, bv, wo, bo):
        import jax, jax.numpy as jnp
        import numpy as np
        D_MODEL = 256
        NUM_HEADS = 8
        DEPTH = D_MODEL // NUM_HEADS
        B, L = (32, 512)

        def _feature_map(x):
            return jax.nn.elu(x) + 1.0
        b, l, _ = x.shape
        q = (x @ wq + bq).reshape(b, l, NUM_HEADS, DEPTH)
        k = (x @ wk + bk).reshape(b, l, NUM_HEADS, DEPTH)
        v = (x @ wv + bv).reshape(b, l, NUM_HEADS, DEPTH)
        q = _feature_map(q)
        k = _feature_map(k)
        kv = jnp.einsum('blhd,blhe->bhde', k, v)
        k_sum = jnp.sum(k, axis=1)
        qkv = jnp.einsum('blhd,bhde->blhe', q, kv)
        normalizer = jnp.einsum('blhd,bhd->blh', q, k_sum) + 1e-06
        out = qkv / normalizer[..., None]
        out = out.reshape(b, l, D_MODEL)
        return out @ wo + bo

    def _L0_ffn_ref(x, Wr, br, ln_g, ln_b, W1, b1, W2, b2):
        import jax, jax.numpy as jnp
        import numpy as np
        TOP_K = 2
        LN_EPS = 1e-05
        B, S, D = x.shape
        N = B * S
        xt = x.reshape(N, D)
        logits = xt @ Wr + br
        probs = jax.nn.softmax(logits, axis=-1)
        top_p, top_idx = jax.lax.top_k(probs, TOP_K)
        weights = top_p / top_p.sum(axis=-1, keepdims=True)
        mu = xt.mean(axis=-1, keepdims=True)
        var = ((xt - mu) ** 2).mean(axis=-1, keepdims=True)
        xn = (xt - mu) * jax.lax.rsqrt(var + LN_EPS)
        xe = xn[None, :, :] * ln_g[:, None, :] + ln_b[:, None, :]
        h = jax.nn.gelu(jnp.einsum('end,edh->enh', xe, W1) + b1[:, None, :], approximate=False)
        y = jnp.einsum('enh,ehd->end', h, W2) + b2[:, None, :]
        y_tok = jnp.transpose(y, (1, 0, 2))
        sel = jnp.take_along_axis(y_tok, top_idx[:, :, None], axis=1)
        out = (weights[:, :, None] * sel).sum(axis=1)
        return out.reshape(B, S, D)
    edge_index = jnp.stack([src, dst])
    xn = _layernorm(x, axis=-1)
    x = x + _L0_gnn_ref(xn, L0_gnn_W, edge_index) + _L0_mix_ref(xn[None], L0_mix_wq, L0_mix_bq, L0_mix_wk, L0_mix_bk, L0_mix_wv, L0_mix_bv, L0_mix_wo, L0_mix_bo)[0]
    x = x + _L0_ffn_ref(_layernorm(x, axis=-1)[None], L0_ffn_Wr, L0_ffn_br, L0_ffn_ln_g, L0_ffn_ln_b, L0_ffn_W1, L0_ffn_b1, L0_ffn_W2, L0_ffn_b2)[0]
    return x

_drawn_inputs = setup_inputs


def setup_inputs(seed=0):
    import zlib

    import numpy as np

    out = dict(_drawn_inputs(seed))
    spreads = {'L0_mix_bq': (0.0, 0.8),
     'L0_mix_bk': (0.0, 0.8),
     'L0_mix_bv': (0.0, 0.1),
     'L0_mix_bo': (0.0, 0.1),
     'L0_ffn_br': (0.0, 0.1),
     'L0_ffn_ln_g': (1.0, 0.2),
     'L0_ffn_ln_b': (0.0, 0.1),
     'L0_ffn_b1': (0.0, 0.1),
     'L0_ffn_b2': (0.0, 0.1)}
    factors = {'L0_mix_wq': 3.548}
    for name, (base, spread) in spreads.items():
        noise = np.random.default_rng([zlib.crc32(name.encode()), seed]).standard_normal(out[name].shape)
        drawn = base * np.exp(spread * noise) if base else spread * noise
        out[name] = jnp.asarray(drawn.astype(out[name].dtype))
    for name, factor in factors.items():
        out[name] = (out[name] * factor).astype(out[name].dtype)
    return out
```

```python
import concourse.bass as bass
from concourse import mybir
from contextlib import ExitStack

F32, BF16, I32, I16 = mybir.dt.float32, mybir.dt.bfloat16, mybir.dt.int32, mybir.dt.int16
ALU = mybir.AluOpType
ACT = mybir.ActivationFunctionType
AX = mybir.AxisListType

P = 128
N_NODES = 6250
D = 256
KD = D // P
NT = -(-N_NODES // P)
LAST = N_NODES - (NT - 1) * P
N_EDGES = 100000
DEPTH = 32
LN_EPS = 1e-5

EC = 784
FULL = N_EDGES // P
REST = N_EDGES - FULL * P
HB = EC // NT
ROW = 4
SORTN = 936
GSTEPS = 9
NG = SORTN // (8 * GSTEPS)
GV = 8 * GSTEPS
GR = GV // ROW
RPC = P // ROW
CODE = 13
MASK = (1 << 2 * CODE) - 1
FLAG = 0x40000000
PAD = NT * P
UNROLL = 8
ROWS_MAX = (N_EDGES + (ROW - 1) * NT * P) // ROW
CHUNKS_MAX = (ROWS_MAX + (RPC - 1) * NT) // RPC
STEPS = -(-CHUNKS_MAX // (2 * UNROLL))
CHUNKS = STEPS * 2 * UNROLL
CG = 8
CPAD = CG * P

E = 8
TOPK = 2
H = 1024
KH = H // P
ST = (N_NODES * TOPK - E) // P + E
SLOTS = ST * P
BR = H + D

assert EC % NT == 0 and SORTN % (8 * GSTEPS) == 0 and NT % 2 == 1 and ST % 2 == 1
assert SORTN >= EC + NT * (ROW - 1) and CPAD * RPC >= SORTN // ROW * P + (NT + 1) * (RPC - 1)
assert CHUNKS_MAX <= CHUNKS <= CPAD and PAD < 1 << CODE


class Chain:

    def __init__(self, eng, sem, tick):
        self.eng, self.sem, self.tick = eng, sem, tick
        self.base, self.k, self.i, self.per = 0, 0, None, 0

    def loop(self, i, per):
        self.base, self.k, self.i, self.per = self.base + self.k, 0, i, per

    def end(self, count):
        assert self.k == self.per, (self.k, self.per)
        self.base, self.k, self.i = self.base + self.per * count, 0, None

    def value(self, lag=0):
        n = self.base + self.k - lag
        return n if self.i is None else self.i * self.per + n

    def add(self, ins):
        self.k += 1
        return ins.then_inc(self.sem, 1)

    def sync(self, lag=0):
        when(self.eng, self.tick, self.sem, self.value(lag))

    def link(self, ins):
        self.add(ins)
        self.sync()


def when(eng, tick, sem, value):
    eng.wait_ge(sem, value)
    if not isinstance(value, int):
        eng.sem_inc(tick, 1)


def tiles(eng, body):
    with eng.Fori(0, NT // 2) as i:
        body(i * 2, 0)
        body(i * 2 + 1, 1)
    body(NT - 1, 0)


def chained_tiles(eng, chain, per, body):
    with eng.Fori(0, NT // 2) as i:
        chain.loop(i, 2 * per)
        body(i * 2, 0)
        body(i * 2 + 1, 1)
        chain.end(NT // 2)
    body(NT - 1, 0)


def gps_layer(nc, x, src, dst, src_rest, dst_rest, gnn_w, wq, bq, wkv, bkv, wo, bo,
              wr, br, ln_gT, ln_bT, w1, b1, w2, b2, out):
    ctx = ExitStack()
    with ctx:
        def sb(name, words, dt=F32):
            return ctx.enter_context(nc.sbuf_tensor(name, [P, words], dt))

        def sem(name):
            return ctx.enter_context(nc.semaphore(name))

        def dram(name, shape, dt):
            return nc.dram_tensor(name, shape, dt, kind="Internal").ap()

        table = dram("table", [NT * P, D], F32)
        edge_rows = dram("edge_rows", [CPAD * RPC, ROW], I32)
        chunk_tiles = dram("chunk_tiles", [CPAD], I16)
        slot_x = dram("slot_x", [SLOTS + 2 * P, D], F32)
        slot_y = dram("slot_y", [SLOTS, D], F32)
        bias_rows = dram("bias_rows", [E, 3, BR], BF16)
        slot_experts = dram("slot_experts", [P], I32)

        W1A = sb("W1A", E * KD * H)
        W2A = sb("W2A", E * KH * D)
        ACC = sb("ACC", (NT + 1) * D)
        CONST = sb("CONST", 4 * P)
        SMALL = sb("SMALL", 27 * 50)
        BIG = sb("BIG", 5650)
        S1, S2 = KD * NT * P, NT * D

        def piece(area, at, n, dt=F32):
            words = n if dt in (F32, I32) else (n + 1) // 2
            ap = area[:, at:at + words]
            return ap if dt == F32 else ap.bitcast(dt)

        def grid(area, at, a, b, dt=F32):
            return piece(area, at, a * b, dt).rearrange("p (a b) -> p a b", b=b)

        ident, iota, tri, ones = (CONST[:, k * P:(k + 1) * P] for k in range(4))
        acc = grid(ACC, 0, NT + 1, D)

        def small(k, n=NT, dt=F32):
            return piece(SMALL, 50 * k, n, dt)

        rstd, nmr, mask, dinv, junk = (small(k) for k in range(5))
        gate0, gate1 = small(5), small(6)
        place0, place1 = small(7, NT, I32), small(8, NT, I32)
        bqc, pcol = small(9, KD), piece(SMALL, 452, 1)
        g_s, b_s = grid(SMALL, 454, KD, E), grid(SMALL, 470, KD, E)
        col = [small(k, 50) for k in range(10, 24)]
        rstd2a, rstd2, nmr2 = (small(k) for k in range(24, 27))

        q_all = grid(W1A, 0, KD, NT * P)
        xr = grid(W2A, 0, NT, D)
        oh_lo = [grid(W1A, S1 + s * 1416, HB, P, BF16) for s in range(2)]
        oh_hi = [grid(W1A, S1 + s * 1416 + HB * P // 2, HB, NT, BF16) for s in range(2)]
        bkv_row = W1A[0:1, S1 + 2832:S1 + 2832 + 2 * D]
        bo_row = W1A[0:1, S1 + 3344:S1 + 3344 + D]
        wkv_s, gw_s, wq_s = grid(BIG, 0, KD, 2 * D), grid(BIG, 1024, KD, D), grid(BIG, 1536, KD, D)
        xn = [piece(BIG, 2048 + 256 * s, D) for s in range(2)]
        xnT = [grid(BIG, 2560 + 256 * s, KD, P) for s in range(2)]
        ka, kb, kc = (piece(BIG, 3072 + 256 * k, D) for k in range(3))
        vbuf = grid(BIG, 3840, KD, P + 1)
        srcI, dstI, packed = (piece(W2A, S2 + k * EC, EC, I32) for k in range(3))
        tile_of, lo_of, hi_of = (piece(W2A, S2 + 3 * EC + k * EC // 2, EC, BF16) for k in range(3))
        lookup = grid(W2A, S2, GR, NT + 1)
        tile_cmp = grid(W2A, S2 + 1000, CG, NT)
        eq_scratch = [piece(BIG, 2048 + 400 * s, EC, BF16) for s in range(2)]
        stats_x = grid(BIG, 3072, NT, 6)
        zeros = W2A[:, S2 + 3528:S2 + 3528 + D]
        work = piece(BIG, 4098, SORTN)
        workI = piece(BIG, 4098, SORTN, I32)
        max8 = piece(BIG, 5034, 8)
        sorted_g, sorted_i = piece(BIG, 5042, GV), piece(BIG, 5042, GV, I32)
        stage_raw = piece(BIG, 5114, GV, I32)
        row_tileI, row_tile = piece(BIG, 5186, GR, I32), piece(BIG, 5204, GR)
        row_at, row_k, row_sum = piece(BIG, 5222, GR, I32), piece(BIG, 5240, GR), piece(BIG, 5258, GR)
        NF = SORTN - EC
        fill, fill_flat, fillI = grid(BIG, 5276, NT, ROW - 1), piece(BIG, 5276, NF), piece(BIG, 5428, NF, I32)
        CT_row = BIG[0:CG, 5584:5584 + P // 2].bitcast(I16)
        head_mask, wo_s = piece(W1A, S1, P), grid(W1A, S1 + P, KD, D)
        kv_bd, kvT = grid(W1A, S1 + 640, KD, P), grid(W1A, S1 + 896, KD, P)
        ksum = piece(W1A, S1 + 1152, KD)
        q_neg, q_exp = piece(W1A, S1 + 1200, D), piece(W1A, S1 + 1456, D)
        q_pos, q_den = piece(W1A, S1 + 1712, D), piece(W1A, S1 + 1968, D)
        q_pos_in, q_sc = piece(W1A, S1 + 2224, D), piece(W1A, S1 + 2480, D)
        kv_out = grid(W1A, S1 + 640, KD, D)
        ks_out = grid(W1A, S1 + 2832, KD, P)

        raw, src_u, dst_u, same = (piece(BIG, 1024 * k, CPAD, I32) for k in range(4))
        raw3 = grid(BIG, 0, CG, P, I32)
        lo_f, dst_f, same_f = piece(BIG, 1024, CPAD), piece(BIG, 2048, CPAD), piece(BIG, 3072, CPAD)
        G = [grid(BIG, 2048 * s, UNROLL, D) for s in range(2)]
        dst_T, lo_T = piece(W2A, S2, CHUNKS, I32), piece(W2A, S2 + CHUNKS, CHUNKS)
        OH = [grid(BIG, 4098, UNROLL, P), grid(W2A, S2 + 2 * CHUNKS, UNROLL, P)]
        tile_row = W2A[0:1, S2 + 2976:S2 + 2976 + CPAD // 2].bitcast(I16)
        idx_s = [piece(W2A, S2 + 3784 + 8 * s, UNROLL, I32) for s in range(2)]

        NE = NT * E
        logits, pick0, pick1, both = (grid(BIG, NE * k, NT, E) for k in range(4))
        tmp, rank, totals, runs = (grid(BIG, NE * k, NT, E) for k in range(4, 8))
        x2 = [piece(BIG, 3136 + 256 * s, D) for s in range(2)]
        x2T = [grid(BIG, 3648 + 256 * s, KD, P) for s in range(2)]
        wr_s, br_s = grid(BIG, 4160, KD, E), piece(BIG, 4176, E)
        expert_m8 = grid(BIG, 4192, NT, E)
        exp_tot, exp_tiles, exp_base, slot_e, exp_i = (piece(BIG, 4592 + 16 * k, E) for k in range(5))
        expI, place_s = piece(BIG, 4680, E, I32), [piece(BIG, 4696 + 2 * s, TOPK, I32) for s in range(2)]
        xs2 = [piece(BIG, 4704 + 256 * s, D) for s in range(2)]
        slot_eI = piece(BIG, 4690, 1, I32)
        b_one_flat = piece(BIG, 4500, KD * E * E)
        b_one = piece(BIG, 4500, KD * E * E).rearrange("p (k e m) -> p k e m", k=KD, e=E)
        bias_f, bias_r = BIG[0:E, 0:BR], BIG[0:E, BR:2 * BR]
        bias_b = BIG[0:E, 2 * BR:2 * BR + 3 * BR // 2].bitcast(BF16).rearrange("e (s n) -> e s n", s=3)
        w1_s = W1A[:, :].rearrange("p (e k n) -> p e k n", e=E, k=KD)
        x_in = [piece(BIG, 256 * s, D) for s in range(2)]
        x_inT = [grid(BIG, 512 + 256 * s, KD, P) for s in range(2)]
        hid = [piece(BIG, 1024 + H * s, H) for s in range(2)]
        hidT = grid(BIG, 3072, KH, P)
        y_out = [piece(BIG, 4096, D), piece(ACC, NT * D, D)]
        bias_t = [BIG[0:3, 4352 + 640 * s:4992 + 640 * s].bitcast(BF16) for s in range(2)]
        ones3 = iota[0:3, 0:64].bitcast(BF16)
        expert_row = tri[0:1, 0:P].bitcast(I32)
        y0 = [piece(BIG, 512 * s, D) for s in range(2)]
        y1 = [piece(BIG, 512 * s + 256, D) for s in range(2)]
        o_s = [piece(BIG, 1024 + 256 * s, D) for s in range(2)]
        pair_s = [piece(BIG, 1600 + 2 * s, TOPK, I32) for s in range(2)]

        B = [ctx.enter_context(nc.psum_tensor(f"B{k}", [P, 512], F32)) for k in range(8)]

        tk_v, tk_a, tk_t, tk_g, tk_s = (sem(n) for n in ("tk_v", "tk_a", "tk_t", "tk_g", "tk_s"))
        dve_steps, act_steps, pool_steps = sem("dve_steps"), sem("act_steps"), sem("pool_steps")
        consts_ready = sem("consts_ready")
        pads_set = sem("pads_set")
        edges_in, x_in_s, weights_in = sem("edges_in"), sem("x_in"), sem("weights_in")
        cleared_edges, cleared_slots = sem("cleared_edges"), sem("cleared_slots")
        counts_ready, prefix_ready = sem("counts_ready"), sem("prefix_ready")
        ctile_ready, ctile_T, ctile_row, ctile_out = sem("ctile_ready"), sem("ctile_T"), sem("ctile_row"), sem("ctile_out")
        tile_row_in = sem("tile_row_in")
        bn_done, pairs_ready = sem("bn_done"), sem("pairs_ready")
        oh_ready, oh_free = sem("oh_ready"), sem("oh_free")
        std_in, std_out = sem("std_in"), sem("std_out")
        norm_ready = sem("norm_ready")
        xn_ready, t_ready, xnT_ready = sem("xn_ready"), sem("t_ready"), sem("xnT_ready")
        kv_ready, hq_ready, kvfm_ready, kv_done, proj_out = (
            sem("kv_ready"), sem("hq_ready"), sem("kvfm_ready"), sem("kv_done"), sem("proj_out"))
        sums_done = sem("sums_done")
        stage_ready, scat = sem("stage_ready"), sem("scat")
        table_ready, table_out = sem("table_ready"), sem("table_out")
        wo_in, kvbd_ready, kvT_ps, kvT_ready, kvo_ps, qweights = (
            sem("wo_in"), sem("kvbd_ready"), sem("kvT_ps"), sem("kvT_ready"), sem("kvo_ps"), sem("qweights"))
        q_fm, q_sum, q_norm, q_scaled, q_mixed, q_added = (
            sem("q_fm"), sem("q_sum"), sem("q_norm"), sem("q_scaled"), sem("q_mixed"), sem("q_added"))
        raw_in, unpacked, unp_T, unp_out = sem("raw_in"), sem("unpacked"), sem("unp_T"), sem("unp_out")
        idx_ready, gath, onehot_ready, seg, added = (
            sem("idx_ready"), [sem("gath0"), sem("gath1")], sem("onehot_ready"), sem("seg"), sem("added"))
        w1_in, w2_in, lnb_in, b_one_ready, b1_ps, bias_in, bias_ready, bias_out = (
            sem("w1_in"), sem("w2_in"), sem("lnb_in"), sem("b_one_ready"), sem("b1_ps"), sem("bias_in"),
            sem("bias_ready"), sem("bias_out"))
        w1_scaled = sem("w1_scaled")
        x_done = sem("x_done")
        router_in, norm2_ready = sem("router_in"), sem("norm2_ready")
        x2_ready, x2T_ps, x2T_ready, logit_ps, logit_out = (
            sem("x2_ready"), sem("x2T_ps"), sem("x2T_ready"), sem("logit_ps"), sem("logit_out"))
        pick_ready, gap_ready, gap_exp, ranks_ps, places_ready = (
            sem("pick_ready"), sem("gap_ready"), sem("gap_exp"), sem("ranks_ps"), sem("places_ready"))
        slot_e_ready, slot_e_out, slot_e_in = sem("slot_e_ready"), sem("slot_e_out"), sem("slot_e_in")
        disp_ready, disp = sem("disp_ready"), [sem("disp0"), sem("disp1")]
        ones3_ready = sem("ones3_ready")
        xs_in, xsT_ps, xsT_ready = [sem("xs_in0"), sem("xs_in1")], sem("xsT_ps"), sem("xsT_ready")
        hid_ps, hid_ready, hidT_ps, hidT_ready = sem("hid_ps"), sem("hid_ready"), sem("hidT_ps"), sem("hidT_ready")
        y_ps, y_ready, y_sent = sem("y_ps"), sem("y_ready"), [sem("y_sent0"), sem("y_sent1")]
        pair_ready, pair_in, o_ready, o_sent = (
            sem("pair_ready"), [sem("pair_in0"), sem("pair_in1")], sem("o_ready"), [sem("o_sent0"), sem("o_sent1")])

        block = ctx.enter_context(nc.Block())

        @block.sync
        def _(sp):
            sp.dma_start(srcI[:, 0:FULL], src).then_inc(edges_in, 16)
            sp.dma_start(dstI[:, 0:FULL], dst).then_inc(edges_in, 16)
            sp.wait_ge(pads_set, 1)
            with nc.allow_non_contiguous_dma(reason="one edge per partition"):
                sp.dma_start(srcI[0:REST, FULL:FULL + 1], src_rest).then_inc(edges_in, 16)
                sp.dma_start(dstI[0:REST, FULL:FULL + 1], dst_rest).then_inc(edges_in, 16)
            sp.dma_start(xr[:, 0:NT - 1, :], x[0:(NT - 1) * P, :].rearrange("(t p) d -> p t d", p=P)).then_inc(x_in_s, 16)
            sp.dma_start(xr[0:LAST, NT - 1, :], x[(NT - 1) * P:N_NODES, :]).then_inc(x_in_s, 16)
            sp.dma_start(wkv_s, wkv.rearrange("(k p) n -> p k n", p=P)).then_inc(weights_in, 16)
            sp.dma_start(gw_s, gnn_w.rearrange("(k p) n -> p k n", p=P)).then_inc(weights_in, 16)
            sp.dma_start(wq_s, wq.rearrange("(k p) n -> p k n", p=P)).then_inc(weights_in, 16)
            sp.dma_start(bqc, bq).then_inc(weights_in, 16)
            sp.dma_start(bkv_row, bkv).then_inc(weights_in, 16)
            sp.dma_start(bo_row, bo).then_inc(weights_in, 16)
            sp.wait_ge(consts_ready, 1)
            sp.dma_start(edge_rows.rearrange("(p a) r -> p (a r)", p=P).rearrange("p (m z) -> p m z", z=D),
                         zeros.bitcast(I32).rearrange("p (m z) -> p m z", m=1).to_broadcast([P, CPAD * P // P // D, D])
                         ).then_inc(cleared_edges, 16)
            for k in range(ST // 15):
                sp.dma_start(slot_x[k * 15 * P:(k + 1) * 15 * P, :].rearrange("(p m) z -> p m z", p=P),
                             zeros.rearrange("p (m z) -> p m z", m=1).to_broadcast([P, 15, D])).then_inc(cleared_slots, 16)
            sp.wait_ge(ctile_row, 1)
            sp.dma_start(chunk_tiles.rearrange("(j p) -> j p", p=P), CT_row).then_inc(ctile_out, 16)
            sp.wait_ge(table_ready, 1)
            sp.dma_start(table.rearrange("(t p) d -> p t d", p=P), acc[:, 0:NT, :]).then_inc(table_out, 16)
            sp.dma_start(wo_s, wo.rearrange("(k p) n -> p k n", p=P)).then_inc(wo_in, 16)
            sp.wait_ge(scat, 16 * GR * NG)
            sp.wait_ge(ctile_out, 16)
            sp.dma_start(raw3, edge_rows.rearrange("(j p a) r -> p j (a r)", p=P, a=RPC)).then_inc(raw_in, 16)
            sp.dma_start(tile_row, chunk_tiles.rearrange("(o n) -> o n", o=1)).then_inc(tile_row_in, 16)
            sp.wait_ge(q_added, NT)
            sp.dma_start(w1_s, w1.rearrange("e (k p) n -> p e k n", p=P)).then_inc(w1_in, 16)
            sp.dma_start(g_s, ln_gT.rearrange("(k p) e -> p k e", p=P)).then_inc(lnb_in, 16)
            sp.dma_start(b_s, ln_bT.rearrange("(k p) e -> p k e", p=P)).then_inc(lnb_in, 16)
            sp.wait_ge(cleared_edges, 16)
            sp.wait_ge(cleared_slots, 16 * (ST // 15))
            sp.wait_ge(x_done, 1)
            sp.dma_start(W2A[:, :].rearrange("p (e c n) -> p e c n", e=E, c=KH),
                         w2.rearrange("e (c p) n -> p e c n", p=P)).then_inc(w2_in, 16)
            sp.dma_start(bias_f[:, 0:H], b1).then_inc(bias_in, 16)
            sp.dma_start(bias_f[:, H:BR], b2).then_inc(bias_in, 16)
            sp.wait_ge(bias_ready, 1)
            sp.dma_start(bias_rows, bias_b).then_inc(bias_out, 16)
            sp.wait_ge(bias_out, 16)
            sp.dma_start(wr_s, wr.rearrange("(k p) e -> p k e", p=P)).then_inc(router_in, 16)
            sp.dma_start(br_s, br.to_broadcast([P, E])).then_inc(router_in, 16)
            sp.wait_ge(slot_e_ready, 1)
            with nc.allow_non_contiguous_dma(reason="one expert number per partition"):
                sp.dma_start(slot_experts.rearrange("(p o) -> p o", o=1), slot_eI).then_inc(slot_e_out, 16)
            sp.wait_ge(slot_e_out, 16)
            sp.dma_start(expert_row, slot_experts.rearrange("(o p) -> o p", o=1)).then_inc(slot_e_in, 16)
            sp.wait_ge(slot_e_in, 16)
            for s in range(2):
                sp.wait_ge(disp[s], 32 * ((NT + 1 - s) // 2))

            def expert_tile(t, s):
                e = nc.sync.value_load(expert_row[0:1, t:t + 1] if isinstance(t, int) else expert_row[0:1, bass.ds(t, 1)],
                                       min_val=0, max_val=E - 1)
                if not isinstance(t, int) or t > 1:
                    when(sp, tk_s, xsT_ps, t + 1)
                    when(sp, tk_s, y_ps, t + 1)
                sp.dma_start(x_in[s], slot_x[bass.ds(t * P, P), :]).then_inc(xs_in[s], 16)
                sp.dma_start(bias_t[s], bias_rows[bass.ds(e, 1), :, :].rearrange("o s n -> (o s) n")).then_inc(xs_in[s], 16)

            def send_y(t, s):
                when(sp, tk_s, y_ready, t + 1)
                sp.dma_start(slot_y[bass.ds(t * P, P), :], y_out[s]).then_inc(y_sent[s], 16)

            expert_tile(0, 0)
            with sp.Fori(0, ST // 2) as i:
                for u in range(2):
                    expert_tile(i * 2 + 1 + u, 1 - u)
                    send_y(i * 2 + u, u)
            send_y(ST - 1, 0)

            def send_o(t, s, rows=P):
                when(sp, tk_s, o_ready, t + 2)
                sp.dma_start(out[bass.ds(t * P, rows), :], o_s[s][0:rows, :]).then_inc(o_sent[s], 16)

            with sp.Fori(0, NT // 2) as i:
                send_o(i * 2, 0)
                send_o(i * 2 + 1, 1)
            send_o(NT - 1, 0, LAST)
            sp.wait_ge(o_sent[0], 16 * (NT // 2 + 1))
            sp.wait_ge(o_sent[1], 16 * (NT // 2))
            sp.wait_ge(y_sent[0], 16 * (ST // 2 + 1))
            sp.wait_ge(y_sent[1], 16 * (ST // 2))

        @block.gpsimd
        def _(pool):
            ch = Chain(pool, pool_steps, tk_g)
            ch.add(pool.memset(zeros, 0.0))
            ch.sync()
            pool.sem_inc(consts_ready, 1)
            ch.add(pool.memset(ident, 0.0))
            ch.add(pool.memset(tri, 1.0))
            ch.add(pool.memset(ones, 1.0))
            ch.add(pool.memset(mask, 1.0))
            ch.add(pool.iota(iota, pattern=[[1, P]], base=0, channel_multiplier=0, allow_small_or_imprecise_dtypes=True))
            ch.add(pool.iota(pcol, pattern=[[0, 1]], base=0, channel_multiplier=1, allow_small_or_imprecise_dtypes=True))
            ch.add(pool.iota(junk, pattern=[[0, NT]], base=SLOTS, channel_multiplier=1, allow_small_or_imprecise_dtypes=True))
            ch.sync()
            ch.add(pool.affine_select(out=ident, in_=ident, compare_op=ALU.not_equal, fill=1.0, base=0,
                                      pattern=[[-1, P]], channel_multiplier=1))
            ch.add(pool.affine_select(out=tri, in_=tri, compare_op=ALU.is_gt, fill=0.0, base=0,
                                      pattern=[[1, P]], channel_multiplier=-1))
            ch.add(pool.affine_select(out=mask[:, NT - 1:NT], in_=mask[:, NT - 1:NT], compare_op=ALU.is_ge, fill=0.0,
                                      base=LAST - 1, pattern=[[0, 1]], channel_multiplier=-1))
            ch.sync()
            pool.sem_inc(consts_ready, 1)
            pool.wait_ge(cleared_edges, 16)
            with pool.Fori(0, NG) as g:
                when(pool, tk_g, stage_ready, g + 1)
                for j in range(GR):
                    pool.indirect_dma_start(edge_rows, bass.IndirectOffsetOnAxis(ap=row_at[:, j:j + 1], axis=0),
                                            stage_raw[:, ROW * j:ROW * (j + 1)], None).then_inc(scat, 16)
            pool.wait_ge(table_out, 16)
            with pool.Fori(0, STEPS) as i:
                for h in range(2):
                    when(pool, tk_g, idx_ready, i * 2 + h + 1)
                    for u in range(UNROLL):
                        pool.indirect_dma_start(G[h][:, u, :], None, table,
                                                bass.IndirectOffsetOnAxis(ap=idx_s[h][:, u:u + 1], axis=0)).then_inc(gath[h], 16)
            pool.wait_ge(cleared_slots, 16 * (ST // 15))

            def dispatch(t, s):
                when(pool, tk_g, disp_ready, t + 1)
                for c in range(TOPK):
                    pool.indirect_dma_start(slot_x, bass.IndirectOffsetOnAxis(ap=place_s[s][:, c:c + 1], axis=0),
                                            xs2[s], None).then_inc(disp[s], 16)

            tiles(pool, dispatch)
            pool.wait_ge(y_sent[0], 16 * (ST // 2 + 1))
            pool.wait_ge(y_sent[1], 16 * (ST // 2))

            def combine(t, s):
                when(pool, tk_g, pair_ready, t + 1)
                for c, y in enumerate((y0, y1)):
                    pool.indirect_dma_start(y[s], None, slot_y,
                                            bass.IndirectOffsetOnAxis(ap=pair_s[s][:, c:c + 1], axis=0)).then_inc(pair_in[s], 16)

            tiles(pool, combine)

        @block.vector
        def _(dve):
            ch = Chain(dve, dve_steps, tk_v)

            def tt(o, a, b, op):
                return dve.tensor_tensor(o, a, b, op)

            def ts(o, a, s1, op0, s2=None, op1=ALU.bypass):
                return dve.tensor_scalar(o, a, s1, s2, op0, op1)

            def scan(o, a):
                return dve.tensor_tensor_scan(o, ones[:, 0:a.shape[1]], a, 0.0, ALU.mult, ALU.add)

            ch.add(dve.memset(xr[:, NT - 1, :], 0.0))
            ch.add(dve.memset(srcI[:, FULL:EC], PAD))
            ch.add(dve.memset(dstI[:, FULL:EC], PAD))
            ch.sync()
            dve.sem_inc(pads_set, 1)
            dve.wait_ge(edges_in, 64)
            dve.wait_ge(consts_ready, 2)
            ch.link(ts(packed, srcI, CODE, ALU.logical_shift_left))
            ch.link(tt(packed, packed, dstI, ALU.bitwise_or))
            ch.add(ts(workI[:, 0:EC], packed, MASK, ALU.bitwise_xor, FLAG, ALU.bitwise_or))
            ch.sync()
            ch.link(ts(packed, srcI, 7, ALU.logical_shift_right))
            ch.link(dve.tensor_copy(tile_of, packed))
            ch.link(tt(packed, srcI, dstI, ALU.is_equal))
            ch.link(ts(srcI, dstI, 7, ALU.logical_shift_right))
            ch.add(dve.tensor_copy(hi_of, srcI))
            ch.link(ts(dstI, dstI, P - 1, ALU.bitwise_and))
            ch.link(dve.scalar_tensor_tensor(out=lo_of, in0=packed, scalar=float(2 * P), in1=dstI, op0=ALU.mult, op1=ALU.add))
            cnt, need, nrow, rows_before, rs, nch, cb, off, t0 = col[0:9]
            nI = small(19, 50, I32)

            with dve.Fori(0, NT // 7) as i:
                ch.loop(i, 7)
                for u in range(7):
                    t = i * 7 + u
                    ch.add(dve.tensor_scalar(eq_scratch[u % 2], tile_of, iota[:, bass.ds(t, 1)], None, ALU.is_equal, ALU.add,
                                             accum_out=cnt[:, bass.ds(t, 1)]))
                    ch.sync(1 if u < 6 else 0)
                ch.end(NT // 7)
            ch.sync()
            ch.link(ts(nI[:, 0:NT], cnt[:, 0:NT], float(ROW - 1), ALU.add))
            ch.link(ts(nI[:, 0:NT], nI[:, 0:NT], 2, ALU.logical_shift_right))
            ch.link(dve.tensor_copy(nrow[:, 0:NT], nI[:, 0:NT]))
            ch.add(dve.scalar_tensor_tensor(out=need[:, 0:NT], in0=nrow[:, 0:NT], scalar=float(ROW), in1=cnt[:, 0:NT],
                                            op0=ALU.mult, op1=ALU.subtract))
            ch.link(dve.reduce_sum(t0[:, 0:1], nrow[:, 0:NT], axis=AX.X))
            ch.link(ts(nrow[:, NT:NT + 1], t0[:, 0:1], -1.0, ALU.mult, float(SORTN // ROW), ALU.add))
            dve.sem_inc(counts_ready, 1)
            for j in range(ROW - 1):
                ch.add(ts(fill[:, :, j], need[:, 0:NT], float(j), ALU.is_gt))
            ch.add(ts(t0[:, 0:NT], iota[:, 0:NT], -1.0, ALU.mult, float(NT), ALU.add))
            ch.sync()
            ch.link(tt(fill, fill, t0[:, 0:NT].unsqueeze(2).to_broadcast([P, NT, 3]), ALU.mult))
            ch.add(ts(fill_flat[:, 0:3 * NT], fill_flat[:, 0:3 * NT], -1.0, ALU.mult, float(NT), ALU.add))
            ch.add(dve.memset(fill_flat[:, 3 * NT:NF], float(NT)))
            ch.sync()
            ch.link(ts(fillI, fill_flat, float(P * ((1 << CODE) + 1)), ALU.mult))
            ch.add(ts(workI[:, EC:SORTN], fillI, MASK, ALU.bitwise_xor, FLAG, ALU.bitwise_or))
            dve.wait_ge(prefix_ready, 1)
            ch.link(ts(nI, B[6][:, 64:64 + NT + 1], float(RPC - 1), ALU.add))
            ch.link(ts(nI, nI, 5, ALU.logical_shift_right))
            ch.link(dve.tensor_copy(nch, nI))
            ch.link(scan(cb, nch))
            ch.link(tt(cb, cb, nch, ALU.subtract))
            ch.link(scan(rs, nrow))
            ch.link(tt(rs, rs, nrow, ALU.subtract))
            ch.link(dve.scalar_tensor_tensor(out=off, in0=cb, scalar=float(RPC), in1=rs, op0=ALU.mult, op1=ALU.subtract))
            ch.link(tt(off, off, B[6][:, 0:NT + 1], ALU.add))
            cgrid, ctile = col[9][:, 0:CG], col[10][:, 0:CG]
            ch.link(ts(cgrid, iota[:, 0:CG], float(P), ALU.mult, pcol, ALU.add))
            ch.link(tt(tile_cmp, cgrid.unsqueeze(2).to_broadcast([P, CG, NT]),
                       cb[:, 1:NT + 1].unsqueeze(1).to_broadcast([P, CG, NT]), ALU.is_ge))
            ch.link(dve.tensor_reduce(ctile, tile_cmp, axis=AX.X, op=ALU.add))
            dve.sem_inc(ctile_ready, 1)
            dve.wait_ge(ctile_T, 1)
            ch.link(dve.tensor_copy(CT_row, B[6][0:CG, 128:256]))
            dve.sem_inc(ctile_row, 1)
            dve.wait_ge(x_in_s, 32)
            

            def half_stats(st6):
                mean, var, dm = col[9], col[10], col[11]
                ch.add(tt(mean[:, 0:NT], st6[:, :, 1], st6[:, :, 4], ALU.add))
                ch.add(tt(dm[:, 0:NT], st6[:, :, 1], st6[:, :, 4], ALU.subtract))
                ch.add(tt(var[:, 0:NT], st6[:, :, 2], st6[:, :, 5], ALU.add))
                ch.sync()
                ch.add(ts(mean[:, 0:NT], mean[:, 0:NT], 0.5, ALU.mult))
                ch.add(tt(dm[:, 0:NT], dm[:, 0:NT], dm[:, 0:NT], ALU.mult))
                ch.add(ts(var[:, 0:NT], var[:, 0:NT], 1.0 / D, ALU.mult))
                ch.sync()
                ch.link(dve.scalar_tensor_tensor(out=var[:, 0:NT], in0=dm[:, 0:NT], scalar=0.25, in1=var[:, 0:NT],
                                                 op0=ALU.mult, op1=ALU.add))
                return mean, var

            with dve.Fori(0, NT // 7) as i:
                for u in range(7):
                    t = i * 7 + u
                    dve.bn_stats(stats_x[:, bass.ds(t, 1), :], xr[:, bass.ds(t, 1), :]).then_inc(bn_done, 1)
            dve.wait_ge(bn_done, NT)
            mean, var = half_stats(stats_x)
            ch.link(ts(var[:, 0:NT], var[:, 0:NT], LN_EPS, ALU.add))
            dve.sem_inc(std_in, 1)
            dve.wait_ge(std_out, 1)
            ch.link(dve.reciprocal(rstd, col[12][:, 0:NT]))
            ch.link(dve.scalar_tensor_tensor(out=nmr, in0=mean[:, 0:NT], scalar=-1.0, in1=rstd, op0=ALU.mult, op1=ALU.mult))
            dve.sem_inc(norm_ready, 1)

            def onehots(t, s):
                when(dve, tk_v, oh_free, t + 1)
                lo = lo_of[:, bass.ds(t * HB, HB)].unsqueeze(2).to_broadcast([P, HB, P])
                hi = hi_of[:, bass.ds(t * HB, HB)].unsqueeze(2).to_broadcast([P, HB, NT])
                tt(oh_lo[s], iota.unsqueeze(1).to_broadcast([P, HB, P]), lo, ALU.is_equal)
                tt(oh_hi[s], iota[:, 0:NT].unsqueeze(1).to_broadcast([P, HB, NT]), hi, ALU.is_equal).then_inc(oh_ready, 1)

            tiles(dve, onehots)
            ch.link(dve.tensor_copy(row_k, iota[:, 0:GR]))
            with dve.Fori(0, NG) as g:
                ch.loop(g, 3 * GSTEPS + 8)
                for u in range(GSTEPS):
                    ch.add(dve.max(max8, work))
                    ch.sync()
                    ch.add(dve.match_replace(out=work, in_to_replace=max8, in_values=work, imm_value=0.0))
                    ch.add(dve.tensor_copy(sorted_g[:, 8 * u:8 * u + 8], max8))
                    ch.sync()
                when(dve, tk_v, scat, g * (16 * GR))
                ch.link(ts(stage_raw, sorted_i, MASK, ALU.bitwise_xor, MASK, ALU.bitwise_and))
                ch.link(ts(row_tileI, stage_raw[:, ::ROW], CODE + 7, ALU.logical_shift_right))
                ch.link(dve.tensor_copy(row_tile, row_tileI))
                ch.link(tt(lookup, row_tile.unsqueeze(2).to_broadcast([P, GR, NT + 1]),
                           iota[:, 0:NT + 1].unsqueeze(1).to_broadcast([P, GR, NT + 1]), ALU.is_equal))
                ch.link(tt(lookup, lookup, off.unsqueeze(1).to_broadcast([P, GR, NT + 1]), ALU.mult))
                ch.link(dve.tensor_reduce(row_sum, lookup, axis=AX.X, op=ALU.add))
                ch.link(tt(row_at, row_sum, row_k, ALU.add))
                dve.sem_inc(stage_ready, 1)
                ch.link(ts(row_k, row_k, float(GR), ALU.add))
                ch.end(NG)
            dve.wait_ge(sums_done, 1)
            ch.link(ts(col[9][:, 0:NT], B[5][:, 0:NT], 1.0, ALU.add))
            dve.sem_inc(std_in, 1)
            dve.wait_ge(std_out, 2)
            ch.link(dve.reciprocal(dinv, col[12][:, 0:NT]))
            ch.add(dve.memset(acc[:, NT, :], 0.0))
            ch.link(tt(acc[:, 0:NT, :], acc[:, 0:NT, :], dinv.unsqueeze(2).to_broadcast([P, NT, D]), ALU.mult))
            dve.sem_inc(table_ready, 1)
            ch.link(dve.memset(head_mask, 0.0))
            for b in range(P // DEPTH):
                ch.add(dve.memset(head_mask[b * DEPTH:(b + 1) * DEPTH, b * DEPTH:(b + 1) * DEPTH], 1.0))
            ch.sync()
            for g in range(KD):
                ch.add(tt(kv_bd[:, g, :], B[3 + g][:, 0:P], head_mask, ALU.mult))
                ch.add(dve.tensor_copy(ksum[:, g:g + 1], B[3 + g][:, P:P + 1]))
            ch.sync()
            for g in range(KD):
                ch.add(ts(ks_out[:, g, :], head_mask, ksum[:, g:g + 1], ALU.mult))
            ch.sync()
            dve.sem_inc(kvbd_ready, 1)
            dve.wait_ge(kvT_ps, 1)
            ch.link(dve.tensor_copy(kvT, B[0][:, 0:D].rearrange("p (g n) -> p g n", g=KD)))
            dve.sem_inc(kvT_ready, 1)
            dve.wait_ge(kvo_ps, 1)
            ch.link(dve.tensor_copy(kv_out, B[1][:, :].rearrange("p (g n) -> p g n", g=KD)))
            dve.sem_inc(qweights, 1)

            def attend(t, s):
                when(dve, tk_v, q_fm, t + 1)
                when(dve, tk_v, q_mixed, t)
                ch.link(tt(q_pos, q_pos_in, q_exp, ALU.add))
                dve.sem_inc(q_sum, 1)
                when(dve, tk_v, q_norm, t + 1)
                ch.link(ts(q_den, B[4][:, 0:D], 1e-6, ALU.add))
                ch.link(dve.reciprocal(q_den, q_den))
                ch.link(tt(q_sc, q_pos, q_den, ALU.mult))
                dve.sem_inc(q_scaled, 1)
                when(dve, tk_v, q_mixed, t + 1)
                xt = xr[:, bass.ds(t, 1), :].rearrange("p o d -> p (o d)")
                tt(xt, xt, B[7][:, 0:D], ALU.add).then_inc(q_added, 1)

            chained_tiles(dve, ch, 4, attend)
            dve.wait_ge(raw_in, 16)
            ch.add(ts(src_u, raw, CODE, ALU.logical_shift_right))
            ch.add(ts(dst_u, raw, (1 << CODE) - 1, ALU.bitwise_and))
            ch.sync()
            ch.link(tt(same_f, src_u, dst_u, ALU.is_equal))
            ch.add(ts(dst_f, dst_u, float(NT * P - 1), ALU.min))
            ch.link(ts(raw, src_u, P - 1, ALU.bitwise_and))
            ch.link(dve.scalar_tensor_tensor(out=lo_f, in0=same_f, scalar=float(2 * P), in1=raw, op0=ALU.mult, op1=ALU.add))
            dve.sem_inc(unpacked, 1)
            for k in range(4):
                dve.wait_ge(unp_T, k + 1)
                n = min(512, CHUNKS - 512 * (k % 2))
                to = (dst_T, lo_T)[k // 2]
                ch.add(dve.tensor_copy(to[:, 512 * (k % 2):512 * (k % 2) + n], B[k][:, 0:n]))
            ch.sync()
            dve.sem_inc(unp_out, 1)
            dve.wait_ge(tile_row_in, 16)
            def onehot(i, h):
                when(dve, tk_v, seg, i * 16 + 8 * h)
                tt(OH[h], iota.unsqueeze(1).to_broadcast([P, UNROLL, P]),
                   lo_T[:, bass.ds(i * 16 + 8 * h, UNROLL)].unsqueeze(2).to_broadcast([P, UNROLL, P]),
                   ALU.is_equal).then_inc(onehot_ready, 1)

            with dve.Fori(0, STEPS) as i:
                ch.loop(i, 2 * UNROLL)
                for h in range(2):
                    onehot(i, h)
                    _, at = nc.values_load_multi_w_load_instructions(
                        tile_row[0:1, bass.ds(i * 16 + 8 * h, UNROLL)], engines=[mybir.EngineType.DVE], min_val=0, max_val=NT)
                    when(dve, tk_v, seg, i * 16 + 8 * h + 16)
                    for u in range(UNROLL):
                        a = ACC[:, bass.ds(at[u] * D, D)]
                        ch.add(tt(a, a, B[u // 2][:, (u % 2) * D:(u % 2 + 1) * D], ALU.add))
                        ch.sync()
                    dve.sem_inc(added, 1)
                ch.end(STEPS)
            ch.link(tt(acc[:, 0:NT, :], acc[:, 0:NT, :], dinv.unsqueeze(2).to_broadcast([P, NT, D]), ALU.mult))
            ch.link(tt(acc[:, 0:NT, :], acc[:, 0:NT, :], xr, ALU.add))
            dve.sem_inc(x_done, 1)
            dve.wait_ge(lnb_in, 32)
            ch.link(dve.memset(b_one_flat, 0.0))
            for k in range(KD):
                for e in range(E):
                    ch.add(dve.tensor_copy(b_one[:, k, e, e:e + 1], b_s[:, k, e:e + 1]))
            ch.sync()
            dve.sem_inc(b_one_ready, 1)
            dve.wait_ge(bias_in, 32)
            dve.wait_ge(b1_ps, 1)
            for n in range(2):
                ch.add(tt(bias_f[:, 512 * n:512 * n + 512], bias_f[:, 512 * n:512 * n + 512], B[6 + n][0:E, :], ALU.add))
            ch.sync()
            ch.link(dve.tensor_copy(bias_b[:, 0, :], bias_f))
            ch.link(tt(bias_r, bias_f, bias_b[:, 0, :], ALU.subtract))
            ch.link(dve.tensor_copy(bias_b[:, 1, :], bias_r))
            ch.link(tt(bias_r, bias_r, bias_b[:, 1, :], ALU.subtract))
            ch.link(dve.tensor_copy(bias_b[:, 2, :], bias_r))
            dve.sem_inc(bias_ready, 1)
            dve.wait_ge(bias_out, 16)
            stats2 = grid(BIG, 3136, NT, 6)
            with dve.Fori(0, NT // 7) as i:
                for u in range(7):
                    t = i * 7 + u
                    dve.bn_stats(stats2[:, bass.ds(t, 1), :], acc[:, bass.ds(t, 1), :]).then_inc(bn_done, 1)
            dve.wait_ge(bn_done, 2 * NT)
            mean, var = half_stats(stats2)
            ch.link(ts(col[13][:, 0:NT], var[:, 0:NT], LN_EPS, ALU.add))
            dve.sem_inc(std_in, 1)
            dve.wait_ge(std_out, 3)
            ch.link(dve.reciprocal(rstd, col[12][:, 0:NT]))
            ch.add(dve.scalar_tensor_tensor(out=nmr, in0=mean[:, 0:NT], scalar=-1.0, in1=rstd, op0=ALU.mult, op1=ALU.mult))
            ch.link(tt(col[13][:, 0:NT], rstd, rstd, ALU.mult))
            ch.link(tt(col[13][:, 0:NT], col[13][:, 0:NT], var[:, 0:NT], ALU.mult))
            ch.link(ts(col[13][:, 0:NT], col[13][:, 0:NT], LN_EPS, ALU.add))
            dve.sem_inc(std_in, 1)
            dve.wait_ge(std_out, 4)
            ch.link(dve.reciprocal(rstd2a, col[12][:, 0:NT]))
            ch.link(tt(rstd2, rstd2a, rstd, ALU.mult))
            ch.link(tt(nmr2, rstd2a, nmr, ALU.mult))
            dve.sem_inc(norm2_ready, 1)

            def route(t, s):
                when(dve, tk_v, x2T_ps, t + 1)
                dve.tensor_copy(x2T[s], B[s][:, 0:D].rearrange("p (g n) -> p g n", g=KD)).then_inc(x2T_ready, 1)

            tiles(dve, route)
            dve.wait_ge(logit_out, NT)
            dve.wait_ge(router_in, 32)
            full = [P, NT, E]
            ch.link(tt(logits, logits, br_s.unsqueeze(1).to_broadcast(full), ALU.add))
            ch.add(ts(slot_e, iota[:, 0:E], -float(E), ALU.add))
            ch.sync()
            ch.link(dve.tensor_copy(expert_m8, slot_e.unsqueeze(1).to_broadcast(full)))
            best, which = col[9][:, 0:NT], col[10][:, 0:NT]
            second = col[11][:, 0:NT]
            for k, (top, pick) in enumerate(((best, pick0), (second, pick1))):
                ch.link(dve.tensor_reduce(top, logits, axis=AX.X, op=ALU.max))
                ch.link(tt(tmp, logits, top.unsqueeze(2).to_broadcast(full), ALU.is_equal))
                ch.link(tt(tmp, tmp, expert_m8, ALU.mult))
                ch.link(dve.tensor_reduce(which, tmp, axis=AX.X, op=ALU.min))
                ch.link(tt(pick, expert_m8, which.unsqueeze(2).to_broadcast(full), ALU.is_equal))
                if k == 0:
                    ch.link(dve.scalar_tensor_tensor(out=logits, in0=pick, scalar=-3e38, in1=logits, op0=ALU.mult, op1=ALU.add))
            ch.link(tt(both, pick0, pick1, ALU.add))
            ch.link(tt(both, both, mask.unsqueeze(2).to_broadcast(full), ALU.mult))
            dve.sem_inc(pick_ready, 1)
            ch.link(tt(second, second, best, ALU.subtract))
            dve.sem_inc(gap_ready, 1)
            dve.wait_ge(gap_exp, 1)
            ch.link(ts(gate0, gate1, 1.0, ALU.add))
            ch.link(dve.reciprocal(gate0, gate0))
            ch.link(tt(gate1, gate1, gate0, ALU.mult))
            dve.wait_ge(ranks_ps, 1)
            fl = lambda a: a.rearrange("p t e -> p (t e)")
            ch.add(dve.tensor_copy(fl(rank), B[2][:, 0:NE]))
            ch.add(dve.tensor_copy(fl(totals), B[3][:, 0:NE]))
            ch.sync()
            for e in range(E):
                ch.add(scan(runs[:, :, e], totals[:, :, e]))
            ch.sync()
            ch.link(dve.tensor_copy(exp_tot, runs[:, NT - 1, :]))
            ch.add(tt(runs, runs, totals, ALU.subtract))
            ch.sync()
            ch.link(tt(rank, rank, runs, ALU.add))
            ch.link(ts(expI, exp_tot, float(P - 1), ALU.add))
            ch.link(ts(expI, expI, 7, ALU.logical_shift_right))
            ch.link(dve.tensor_copy(exp_tiles, expI))
            ch.link(scan(exp_i, exp_tiles))
            ch.link(tt(exp_base, exp_i, exp_tiles, ALU.subtract))
            ch.link(ts(slot_e[:, 0:E - 1], exp_i[:, 0:E - 1], pcol, ALU.is_le))
            ch.link(dve.reduce_sum(exp_tot[:, 0:1], slot_e[:, 0:E - 1], axis=AX.X))
            ch.link(dve.tensor_copy(slot_eI, exp_tot[:, 0:1]))
            dve.sem_inc(slot_e_ready, 1)
            ch.link(ts(exp_base, exp_base, float(P), ALU.mult))
            ch.link(tt(rank, rank, exp_base.unsqueeze(1).to_broadcast(full), ALU.add))
            inv = col[12][:, 0:NT]
            ch.link(ts(inv, mask, -1.0, ALU.mult, 1.0, ALU.add))
            ch.link(tt(junk, junk, inv, ALU.mult))
            for c, (pick, place) in enumerate(((pick0, place0), (pick1, place1))):
                pf = col[13][:, 0:NT]
                ch.link(tt(tmp, rank, pick, ALU.mult))
                ch.link(dve.tensor_reduce(pf, tmp, axis=AX.X, op=ALU.add))
                ch.link(tt(pf, pf, mask, ALU.mult))
                ch.link(tt(pf, pf, junk, ALU.add))
                if c:
                    ch.link(dve.scalar_tensor_tensor(out=pf, in0=inv, scalar=float(P), in1=pf, op0=ALU.mult, op1=ALU.add))
                ch.link(dve.tensor_copy(place, pf))
            dve.sem_inc(places_ready, 1)
            ch.link(dve.memset(ones3, 1.0))
            dve.sem_inc(ones3_ready, 1)
            dve.wait_ge(disp[0], 32 * (NT // 2 + 1))
            dve.wait_ge(disp[1], 32 * (NT // 2))
            for place in (place0, place1):
                ch.add(ts(place, place, float(SLOTS - 1), ALU.min))
            ch.sync()
            dve.sem_inc(pairs_ready, 1)

            def front(t, s):
                when(dve, tk_v, xsT_ps, t + 3)
                when(dve, tk_v, hid_ps, t + 1)
                dve.tensor_copy(x_inT[s], B[6][:, 0:D].rearrange("p (g n) -> p g n", g=KD)).then_inc(xsT_ready, 1)

            def back(t, s):
                for g in range(2):
                    when(dve, tk_v, hidT_ps, t * 2 + g + 3)
                    if g == 0:
                        when(dve, tk_v, y_ps, t + 2)
                    dve.tensor_copy(hidT[:, 4 * g:4 * g + 4, :],
                                    B[4 + g][:, :].rearrange("p (g n) -> p g n", g=4)).then_inc(hidT_ready, 1)
                when(dve, tk_v, y_ps, t + 3)
                when(dve, tk_v, y_sent[s], (t - s) * 8)
                dve.tensor_copy(y_out[s], B[7][:, 0:D]).then_inc(y_ready, 1)

            front(0, 0)
            with dve.Fori(0, ST // 2) as i:
                for u in range(2):
                    front(i * 2 + 1 + u, 1 - u)
                    back(i * 2 + u, u)
            back(ST - 1, 0)

            dve.sem_inc(o_ready, 1)

            def combine(t, s):
                when(dve, tk_v, pair_in[s], (t - s) * 16 + 32)
                when(dve, tk_v, o_sent[s], (t - s) * 8)
                at = acc[:, bass.ds(t, 1), :].rearrange("p o d -> p (o d)")
                ch.link(dve.scalar_tensor_tensor(out=o_s[s], in0=y0[s], scalar=gate0[:, bass.ds(t, 1)], in1=at,
                                                 op0=ALU.mult, op1=ALU.add))
                ch.link(dve.scalar_tensor_tensor(out=o_s[s], in0=y1[s], scalar=gate1[:, bass.ds(t, 1)], in1=o_s[s],
                                                 op0=ALU.mult, op1=ALU.add))
                dve.sem_inc(o_ready, 1)

            chained_tiles(dve, ch, 2, combine)

        @block.scalar
        def _(act):
            ch = Chain(act, act_steps, tk_a)

            def cp(o, i, fn=ACT.Copy, **kw):
                return nc.scalar.activation(o, i, fn, **kw)

            act.wait_ge(std_in, 1)
            cp(col[12][:, 0:NT], col[10][:, 0:NT], ACT.Sqrt).then_inc(std_out, 1)
            act.wait_ge(norm_ready, 1)
            act.wait_ge(weights_in, 96)

            def project(t, s):
                xt = xr[:, bass.ds(t, 1), :].rearrange("p o d -> p (o d)")
                cp(xn[s], xt, ACT.Identity, scale=rstd[:, bass.ds(t, 1)], bias=nmr[:, bass.ds(t, 1)]).then_inc(xn_ready, 1)
                when(act, tk_a, t_ready, t + 1)
                cp(xnT[s], B[0][:, 0:D].rearrange("p (g n) -> p g n", g=KD)).then_inc(xnT_ready, 1)
                when(act, tk_a, kv_ready, t + 1)
                when(act, tk_a, kv_done, t)
                ch.add(cp(ka, B[1][:, 0:D], ACT.Relu, scale=-1.0))
                cp(kc, B[1][:, 0:D], ACT.Relu)
                ch.sync()
                cp(kb, ka, ACT.Exp, scale=-1.0)
                m = mask[:, bass.ds(t, 1)]
                cp(vbuf[:, :, 0:P], B[1][:, D:2 * D].rearrange("p (g n) -> p g n", g=KD), scale=m)
                cp(vbuf[:, 0, P:P + 1], m)
                cp(vbuf[:, 1, P:P + 1], m).then_inc(kvfm_ready, 1)
                when(act, tk_a, hq_ready, t + 1)
                cp(acc[:, bass.ds(t, 1), :].rearrange("p o d -> p (o d)"), B[2][:, 0:D])
                for g in range(KD):
                    last = cp(q_all[:, g, bass.ds(t * P, P)], B[2][:, D + g * P:D + (g + 1) * P], ACT.Identity,
                              bias=bqc[:, g:g + 1])
                last.then_inc(proj_out, 1)

            chained_tiles(act, ch, 1, project)
            act.wait_ge(std_in, 2)
            cp(col[12][:, 0:NT], col[9][:, 0:NT], ACT.Sqrt).then_inc(std_out, 1)

            act.wait_ge(qweights, 1)

            def attend(t, s):
                qt = q_all[:, :, bass.ds(t * P, P)]
                g3 = lambda a: a.rearrange("p (g n) -> p g n", g=KD)
                when(act, tk_a, q_sum, t)
                ch.add(cp(g3(q_neg), qt, ACT.Relu, scale=-1.0))
                cp(g3(q_pos_in), qt, ACT.Relu)
                ch.sync()
                cp(q_exp, q_neg, ACT.Exp, scale=-1.0).then_inc(q_fm, 1)

            chained_tiles(act, ch, 1, attend)
            act.wait_ge(unp_out, 1)
            with act.Fori(0, STEPS) as i:
                for h in range(2):
                    when(act, tk_a, seg, i * 16 + 8 * h)
                    act.copy(idx_s[h], dst_T[:, bass.ds(i * 16 + 8 * h, UNROLL)]).then_inc(idx_ready, 1)
            act.wait_ge(b1_ps, 1)
            for e in range(E):
                for k in range(KD):
                    last = cp(w1_s[:, e, k, :], w1_s[:, e, k, :], scale=g_s[:, k, e:e + 1])
            last.then_inc(w1_scaled, 1)
            act.wait_ge(std_in, 3)
            cp(col[12][:, 0:NT], col[13][:, 0:NT], ACT.Sqrt).then_inc(std_out, 1)
            act.wait_ge(std_in, 4)
            cp(col[12][:, 0:NT], col[13][:, 0:NT], ACT.Sqrt).then_inc(std_out, 1)
            act.wait_ge(norm2_ready, 1)

            def route(t, s):
                when(act, tk_a, x2T_ps, t)
                xt = acc[:, bass.ds(t, 1), :].rearrange("p o d -> p (o d)")
                cp(x2[s], xt, ACT.Identity, scale=rstd[:, bass.ds(t, 1)], bias=nmr[:, bass.ds(t, 1)]).then_inc(x2_ready, 1)
                when(act, tk_a, logit_ps, t + 1)
                cp(BIG[:, bass.ds(t * E, E)], B[4 + s][:, 0:E]).then_inc(logit_out, 1)

            tiles(act, route)
            act.wait_ge(gap_ready, 1)
            cp(gate1, col[11][:, 0:NT], ACT.Exp).then_inc(gap_exp, 1)
            act.wait_ge(places_ready, 1)

            def dispatch(t, s):
                when(act, tk_a, disp[s], (t - s) * 16)
                xt = acc[:, bass.ds(t, 1), :].rearrange("p o d -> p (o d)")
                cp(xs2[s], xt, ACT.Identity, scale=rstd2[:, bass.ds(t, 1)], bias=nmr2[:, bass.ds(t, 1)])
                act.copy(place_s[s][:, 0:1], place0[:, bass.ds(t, 1)])
                act.copy(place_s[s][:, 1:2], place1[:, bass.ds(t, 1)]).then_inc(disp_ready, 1)

            tiles(act, dispatch)
            act.wait_ge(disp[0], 32 * (NT // 2 + 1))
            act.wait_ge(disp[1], 32 * (NT // 2))

            def expert(t, s):
                when(act, tk_a, hid_ps, t + 3)
                when(act, tk_a, hidT_ps, t * 2)
                for n in range(2):
                    last = cp(hid[s][:, 512 * n:512 * n + 512], B[2 * s + n][:, :], ACT.Gelu)
                last.then_inc(hid_ready, 1)

            with act.Fori(0, ST // 2) as i:
                expert(i * 2, 0)
                expert(i * 2 + 1, 1)
            expert(ST - 1, 0)

            def pairs(t, s):
                when(act, tk_a, pair_in[s], (t - s) * 16)
                when(act, tk_a, o_ready, t)
                act.copy(pair_s[s][:, 0:1], place0[:, bass.ds(t, 1)])
                act.copy(pair_s[s][:, 1:2], place1[:, bass.ds(t, 1)]).then_inc(pair_ready, 1)

            act.wait_ge(pairs_ready, 1)
            act.wait_ge(y_sent[0], 16 * (ST // 2 + 1))
            act.wait_ge(y_sent[1], 16 * (ST // 2))
            tiles(act, pairs)

        @block.tensor
        def _(pe):
            mm = nc.tensor.matmul
            pe.wait_ge(consts_ready, 2)
            pe.wait_ge(counts_ready, 1)
            mm(B[6][:, 0:NT + 1], tri, col[2], start=True, stop=True)
            mm(B[6][:, 64:64 + NT + 1], ones, col[2], start=True, stop=True).then_inc(prefix_ready, 1)
            pe.wait_ge(ctile_ready, 1)
            nc.tensor.transpose(B[6][0:CG, 128:256], col[10][:, 0:CG], ident).then_inc(ctile_T, 1)
            pe.sem_inc(oh_free, 2)
            pe.wait_ge(weights_in, 96)
            zb = zeros.bitcast(BF16)
            mm(B[3][:, 0:P + 1], zeros[:, 0:P], zeros[:, 0:P + 1], start=True, stop=False)
            mm(B[4][:, 0:P + 1], zeros[:, 0:P], zeros[:, 0:P + 1], start=True, stop=False)
            mm(B[5][:, 0:NT], zb[:, 0:P], zb[:, 0:NT], start=True, stop=False)

            def project(t, s):
                when(pe, tk_t, xn_ready, t + 1)
                for k in range(KD):
                    last = nc.tensor.transpose(B[0][:, k * P:(k + 1) * P], xn[s][:, k * P:(k + 1) * P], ident)
                last.then_inc(t_ready, 1)
                when(pe, tk_t, oh_ready, t + 1)
                for b in range(HB):
                    last = mm(B[5][:, 0:NT], oh_lo[s][:, b, :], oh_hi[s][:, b, :], start=False, stop=False)
                last.then_inc(oh_free, 1)
                when(pe, tk_t, xnT_ready, t + 1)
                when(pe, tk_t, proj_out, t)
                mm(B[1][:, :], ones[0:1, :], bkv_row, start=True, stop=False)
                for k in range(KD):
                    last = mm(B[1][:, :], xnT[s][:, k, :], wkv_s[:, k, :], start=False, stop=k == KD - 1)
                last.then_inc(kv_ready, 1)
                for k in range(KD):
                    mm(B[2][:, 0:D], xnT[s][:, k, :], gw_s[:, k, :], start=k == 0, stop=k == KD - 1)
                for g in range(KD):
                    for k in range(KD):
                        last = mm(B[2][:, D + g * P:D + (g + 1) * P], wq_s[:, k, g * P:(g + 1) * P], xnT[s][:, k, :],
                                  start=k == 0, stop=k == KD - 1)
                last.then_inc(hq_ready, 1)
                when(pe, tk_t, kvfm_ready, t + 1)
                for g in range(KD):
                    for kk in (kb, kc):
                        last = mm(B[3 + g][:, 0:P + 1], kk[:, g * P:(g + 1) * P], vbuf[:, g, :], start=False, stop=False)
                last.then_inc(kv_done, 1)

            tiles(pe, project)
            mm(B[3][:, 0:P + 1], zeros[:, 0:P], zeros[:, 0:P + 1], start=False, stop=True)
            mm(B[4][:, 0:P + 1], zeros[:, 0:P], zeros[:, 0:P + 1], start=False, stop=True)
            mm(B[5][:, 0:NT], zb[:, 0:P], zb[:, 0:NT], start=False, stop=True).then_inc(sums_done, 1)
            pe.wait_ge(kvbd_ready, 1)
            for g in range(KD):
                last = nc.tensor.transpose(B[0][:, g * P:(g + 1) * P], kv_bd[:, g, :], ident)
            last.then_inc(kvT_ps, 1)
            pe.wait_ge(kvT_ready, 1)
            pe.wait_ge(wo_in, 16)
            for g in range(KD):
                last = mm(B[1][:, g * D:(g + 1) * D], kvT[:, g, :], wo_s[:, g, :], start=True, stop=True)
            last.then_inc(kvo_ps, 1)
            pe.wait_ge(qweights, 1)

            def attend(t, s):
                when(pe, tk_t, q_sum, t + 1)
                for g in range(KD):
                    last = mm(B[4][:, g * P:(g + 1) * P], ks_out[:, g, :], q_pos[:, g * P:(g + 1) * P], start=True, stop=True)
                last.then_inc(q_norm, 1)
                when(pe, tk_t, q_scaled, t + 1)
                when(pe, tk_t, q_added, t)
                mm(B[7][:, 0:D], ones[0:1, :], bo_row, start=True, stop=False)
                for g in range(KD):
                    last = mm(B[7][:, 0:D], q_sc[:, g * P:(g + 1) * P], kv_out[:, g, :], start=False, stop=g == KD - 1)
                last.then_inc(q_mixed, 1)

            tiles(pe, attend)
            pe.wait_ge(unpacked, 1)
            for k in range(4):
                f = (dst_f, lo_f)[k // 2]
                for j in range(4):
                    c = (k % 2) * 4 + j
                    last = nc.tensor.transpose(B[k][:, j * P:(j + 1) * P], f[:, c * P:(c + 1) * P], ident)
                last.then_inc(unp_T, 1)
            pe.wait_ge(unp_out, 1)
            pe.sem_inc(seg, UNROLL)
            with pe.Fori(0, STEPS) as i:
                for h in range(2):
                    when(pe, tk_t, gath[h], i * (16 * UNROLL) + 16 * UNROLL)
                    when(pe, tk_t, onehot_ready, i * 2 + h + 1)
                    when(pe, tk_t, added, i * 2 + h)
                    for u in range(UNROLL):
                        mm(B[u // 2][:, (u % 2) * D:(u % 2 + 1) * D], OH[h][:, u, :], G[h][:, u, :],
                           start=True, stop=True).then_inc(seg, 1)
            pe.wait_ge(b_one_ready, 1)
            pe.wait_ge(w1_in, 16)
            for n in range(2):
                for e in range(E):
                    for k in range(KD):
                        last = mm(B[6 + n][0:E, :], b_one[:, k, e, :], w1_s[:, e, k, n * 512:(n + 1) * 512],
                                  start=e == 0 and k == 0, stop=e == E - 1 and k == KD - 1)
            last.then_inc(b1_ps, 1)
            pe.wait_ge(router_in, 32)

            def route(t, s):
                when(pe, tk_t, x2_ready, t + 1)
                for k in range(KD):
                    last = nc.tensor.transpose(B[s][:, k * P:(k + 1) * P], x2[s][:, k * P:(k + 1) * P], ident)
                last.then_inc(x2T_ps, 1)
                when(pe, tk_t, x2T_ready, t + 1)
                for k in range(KD):
                    last = mm(B[4 + s][:, 0:E], x2T[s][:, k, :], wr_s[:, k, :], start=k == 0, stop=k == KD - 1)
                last.then_inc(logit_ps, 1)

            tiles(pe, route)
            pe.wait_ge(pick_ready, 1)
            flat = both.rearrange("p t e -> p (t e)")
            mm(B[2][:, 0:NE], tri, flat, start=True, stop=True)
            mm(B[3][:, 0:NE], ones, flat, start=True, stop=True).then_inc(ranks_ps, 1)
            pe.sem_inc(xsT_ps, 2)
            pe.sem_inc(hid_ps, 2)
            pe.sem_inc(y_ps, 2)
            pe.sem_inc(hidT_ps, 2)
            pe.wait_ge(slot_e_in, 16)
            pe.wait_ge(ones3_ready, 1)
            pe.wait_ge(w1_scaled, 1)
            pe.wait_ge(w2_in, 16)
            pe.wait_ge(bias_out, 16)

            def expert_of(t):
                return nc.tensor.value_load(expert_row[0:1, bass.ds(t, 1)], min_val=0, max_val=E - 1)

            def front(t, s):
                e = expert_of(t)
                when(pe, tk_t, xs_in[s], (t - s) * 16 + 32)
                when(pe, tk_t, xsT_ready, t)
                for k in range(KD):
                    last = nc.tensor.transpose(B[6][:, k * P:(k + 1) * P], x_in[s][:, k * P:(k + 1) * P], ident)
                last.then_inc(xsT_ps, 1)
                when(pe, tk_t, xsT_ready, t + 1)
                if not isinstance(t, int) or t > 1:
                    when(pe, tk_t, hid_ready, t - 1)
                for n in range(2):
                    mm(B[2 * s + n][:, :], ones3, bias_t[s][:, 512 * n:512 * n + 512], start=True, stop=False)
                    for k in range(KD):
                        last = mm(B[2 * s + n][:, :], x_inT[s][:, k, :],
                                  W1A[:, bass.ds(e * (KD * H) + k * H + n * 512, 512)], start=False, stop=k == KD - 1)
                last.then_inc(hid_ps, 1)

            def back(t, s):
                e = expert_of(t)
                when(pe, tk_t, hid_ready, t + 1)
                when(pe, tk_t, hidT_ready, t * 2)
                for g in range(2):
                    for c in range(4):
                        last = nc.tensor.transpose(B[4 + g][:, c * P:(c + 1) * P],
                                                   hid[s][:, (4 * g + c) * P:(4 * g + c + 1) * P], ident)
                    last.then_inc(hidT_ps, 1)
                when(pe, tk_t, y_ready, t)
                mm(B[7][:, 0:D], ones3, bias_t[s][:, H:BR], start=True, stop=False)
                for g in range(2):
                    when(pe, tk_t, hidT_ready, t * 2 + g + 1)
                    for c in range(4):
                        k = 4 * g + c
                        last = mm(B[7][:, 0:D], hidT[:, k, :], W2A[:, bass.ds(e * (KH * D) + k * D, D)],
                                  start=False, stop=k == KH - 1)
                last.then_inc(y_ps, 1)

            front(0, 0)
            with pe.Fori(0, ST // 2) as i:
                for u in range(2):
                    front(i * 2 + 1 + u, 1 - u)
                    back(i * 2 + u, u)
            back(ST - 1, 0)


def kernel(x, src, dst, L0_gnn_W, L0_mix_wq, L0_mix_bq, L0_mix_wk, L0_mix_bk, L0_mix_wv, L0_mix_bv, L0_mix_wo,
           L0_mix_bo, L0_ffn_Wr, L0_ffn_br, L0_ffn_ln_g, L0_ffn_ln_b, L0_ffn_W1, L0_ffn_b1, L0_ffn_W2, L0_ffn_b2):
    import numpy as np
    import concourse.bacc as bacc
    from concourse.bass_utils import run_bass_kernel_spmd

    src, dst = np.asarray(src), np.asarray(dst)
    n = P * FULL
    arrays = {
        "x": x, "src": src[:n].reshape(P, FULL), "dst": dst[:n].reshape(P, FULL),
        "src_rest": src[n:].reshape(REST, 1), "dst_rest": dst[n:].reshape(REST, 1),
        "gnn_w": L0_gnn_W, "wq": L0_mix_wq, "bq": np.asarray(L0_mix_bq).reshape(KD, P).T,
        "wkv": np.concatenate([np.asarray(L0_mix_wk), np.asarray(L0_mix_wv)], axis=1),
        "bkv": np.concatenate([np.asarray(L0_mix_bk), np.asarray(L0_mix_bv)]).reshape(1, 2 * D),
        "wo": L0_mix_wo, "bo": np.asarray(L0_mix_bo).reshape(1, D), "wr": L0_ffn_Wr,
        "br": np.asarray(L0_ffn_br).reshape(1, E), "ln_gT": np.asarray(L0_ffn_ln_g).T, "ln_bT": np.asarray(L0_ffn_ln_b).T,
        "w1": L0_ffn_W1, "b1": L0_ffn_b1, "w2": L0_ffn_W2, "b2": L0_ffn_b2,
    }
    arrays = {"in_" + k: np.ascontiguousarray(a) for k, a in arrays.items()}
    nc = bacc.Bacc("TRN2", target_bir_lowering=False, num_devices=1)
    args = [nc.dram_tensor(k, a.shape, mybir.dt.from_np(a.dtype), kind="ExternalInput").ap() for k, a in arrays.items()]
    out = nc.dram_tensor("out_dram", (N_NODES, D), F32, kind="ExternalOutput").ap()
    gps_layer(nc, *args, out)
    r = run_bass_kernel_spmd(nc, [arrays], core_ids=[0])
    return r.results[0]["out_dram"]
```

```python
import concourse.bass as bass
from concourse import mybir
from contextlib import ExitStack

F32, BF16, I32, I16 = mybir.dt.float32, mybir.dt.bfloat16, mybir.dt.int32, mybir.dt.int16
ALU = mybir.AluOpType
ACT = mybir.ActivationFunctionType
AX = mybir.AxisListType

P = 128
N_NODES = 6250
D = 256
KD = D // P
NT = -(-N_NODES // P)
LAST = N_NODES - (NT - 1) * P
N_EDGES = 100000
DEPTH = 32
LN_EPS = 1e-5

EC = 784
FULL = N_EDGES // P
REST = N_EDGES - FULL * P
TPARTS, TPART = 7, NT // 7
HB = EC // NT
ROW = 4
SORTN = 936
GSTEPS = 9
NG = SORTN // (8 * GSTEPS)
GV = 8 * GSTEPS
GR = GV // ROW
RPC = P // ROW
CODE = 13
MASK = (1 << 2 * CODE) - 1
FLAG = 0x40000000
PAD = NT * P
UNROLL = 8
ROWS_MAX = (N_EDGES + (ROW - 1) * NT * P) // ROW
CHUNKS_MAX = (ROWS_MAX + (RPC - 1) * NT) // RPC
STEPS = -(-CHUNKS_MAX // (2 * UNROLL))
CHUNKS = STEPS * 2 * UNROLL
CG = 8
CPAD = CG * P

E = 8
TOPK = 2
H = 1024
KH = H // P
ST = (N_NODES * TOPK - E) // P + E
SLOTS = ST * P
BR = H + D

assert EC % NT == 0 and SORTN % (8 * GSTEPS) == 0 and NT % 4 == 1 and ST % 2 == 1
assert SORTN >= EC + NT * (ROW - 1) and CPAD * RPC >= SORTN // ROW * P + (NT + 1) * (RPC - 1)
assert CHUNKS_MAX <= CHUNKS <= CPAD and PAD < 1 << CODE


class Chain:

    def __init__(self, eng, sem):
        self.eng, self.sem, self.count = eng, sem, 0

    def add(self, ins):
        self.count += 1
        return ins.then_inc(self.sem, 1)

    def sync(self):
        self.eng.wait_ge(self.sem, self.count)

    def link(self, ins):
        self.add(ins)
        self.sync()


def when(eng, tick, sem, value):
    if not isinstance(value, int):
        eng.wait_ge(sem, value)
        eng.sem_inc(tick, 1)
    elif value > 0:
        eng.wait_ge(sem, value)


def tiles(eng, body, slots=2):
    for t in range(slots):
        body(t, t)
    with eng.Fori(1, NT // slots) as i:
        for s in range(slots):
            body(i * slots + s, s)
    for t in range(NT // slots * slots, NT):
        body(t, t % slots)


def gps_layer(nc, x, src, dst, src_rest, dst_rest, gnn_w, wq, bq, wkv, bkv, wo, bo,
              wr, br, ln_gT, ln_bT, w1, b1, w2, b2, out):
    ctx = ExitStack()
    with ctx:
        def sb(name, words, dt=F32):
            return ctx.enter_context(nc.sbuf_tensor(name, [P, words], dt))

        def sem(name):
            return ctx.enter_context(nc.semaphore(name))

        def dram(name, shape, dt):
            return nc.dram_tensor(name, shape, dt, kind="Internal").ap()

        table = dram("table", [NT * P, D], F32)
        edge_rows = dram("edge_rows", [CPAD * RPC, ROW], I32)
        chunk_tiles = dram("chunk_tiles", [CPAD], I16)
        slot_x = dram("slot_x", [SLOTS + 2 * P, D], F32)
        slot_y = dram("slot_y", [SLOTS, D], F32)
        bias_rows = dram("bias_rows", [E, 3, BR], BF16)
        slot_experts = dram("slot_experts", [P], I32)

        W1A = sb("W1A", E * KD * H)
        W2A = sb("W2A", E * KH * D)
        ACC = sb("ACC", (NT + 1) * D)
        CONST = sb("CONST", 4 * P)
        SMALL = sb("SMALL", 27 * 50)
        BIG = sb("BIG", 5650)
        S1, S2 = KD * NT * P, NT * D

        def piece(area, at, n, dt=F32):
            words = n if dt in (F32, I32) else (n + 1) // 2
            ap = area[:, at:at + words]
            return ap if dt == F32 else ap.bitcast(dt)

        def grid(area, at, a, b, dt=F32):
            return piece(area, at, a * b, dt).rearrange("p (a b) -> p a b", b=b)

        ident, iota, tri, ones = (CONST[:, k * P:(k + 1) * P] for k in range(4))
        acc = grid(ACC, 0, NT + 1, D)

        def small(k, n=NT, dt=F32):
            return piece(SMALL, 50 * k, n, dt)

        rstd, nmr, mask, dinv, junk = (small(k) for k in range(5))
        gate0, gate1 = small(5), small(6)
        place0, place1 = small(7, NT, I32), small(8, NT, I32)
        bqc, pcol = small(9, KD), piece(SMALL, 452, 1)
        g_s, b_s = grid(SMALL, 454, KD, E), grid(SMALL, 470, KD, E)
        col = [small(k, 50) for k in range(10, 24)]
        rstd2a, rstd2, nmr2 = (small(k) for k in range(24, 27))

        q_all = grid(W1A, 0, KD, NT * P)
        xr = grid(W2A, 0, NT, D)
        oh_lo = [grid(W1A, S1 + s * 1416, P, HB, BF16) for s in range(2)]
        oh_hi = [grid(W1A, S1 + s * 1416 + HB * P // 2, NT, HB, BF16) for s in range(2)]
        digits = grid(W2A, S2 + 1400, P, HB, BF16)
        bkv_row = W1A[0:1, S1 + 2832:S1 + 2832 + 2 * D]
        bo_row = W1A[0:1, S1 + 3344:S1 + 3344 + D]
        wkv_s, gw_s, wq_s = grid(BIG, 0, KD, 2 * D), grid(BIG, 1024, KD, D), grid(BIG, 1536, KD, D)
        xn = [piece(BIG, 2048 + 256 * s, D) for s in range(2)]
        xnT = [grid(BIG, 2560 + 256 * s, KD, P) for s in range(2)]
        ka, kb, kc = (piece(BIG, 3072 + 256 * k, D) for k in range(3))
        vbuf = grid(BIG, 3840, KD, P + 1)
        srcI, dstI, packed = (piece(W2A, S2 + k * EC, EC, I32) for k in range(3))
        tile_of, lo_of, hi_of = (piece(W2A, S2 + 3 * EC + k * EC // 2, EC, BF16) for k in range(3))
        lookup = grid(W2A, S2, GR, NT + 1)
        tile_cmp = grid(W2A, S2 + 1000, CG, NT)
        eq_scratch = [piece(BIG, 2048 + 400 * s, EC, BF16) for s in range(2)]
        stats_x = grid(BIG, 3072, NT, 6)
        zeros = W2A[:, S2 + 3528:S2 + 3528 + D]
        work = piece(BIG, 4098, SORTN)
        workI = piece(BIG, 4098, SORTN, I32)
        sorted_g, sorted_i = piece(BIG, 5042, GV), piece(BIG, 5042, GV, I32)
        stage_raw = piece(BIG, 5114, GV, I32)
        row_tileI, row_tile = piece(BIG, 5186, GR, I32), piece(BIG, 5204, GR)
        row_at, row_k, row_sum = piece(BIG, 5222, GR, I32), piece(BIG, 5240, GR), piece(BIG, 5258, GR)
        NF = SORTN - EC
        fill, fill_flat, fillI = grid(BIG, 5276, NT, ROW - 1), piece(BIG, 5276, NF), piece(BIG, 5428, NF, I32)
        CT_row = BIG[0:CG, 5584:5584 + P // 2].bitcast(I16)
        head_mask, wo_s = piece(W1A, S1, P), grid(W1A, S1 + P, KD, D)
        kv_bd, kvT = grid(W1A, S1 + 640, KD, P), grid(W1A, S1 + 896, KD, P)
        ksum = piece(W1A, S1 + 1152, KD)
        q_neg, q_exp = piece(W1A, S1 + 1200, D), piece(W1A, S1 + 1456, D)
        q_pos, q_den = piece(W1A, S1 + 1712, D), piece(W1A, S1 + 1968, D)
        q_pos_in, q_sc = piece(W1A, S1 + 2224, D), piece(W1A, S1 + 2480, D)
        kv_out = grid(W1A, S1 + 640, KD, D)
        ks_out = grid(W1A, S1 + 2832, KD, P)

        raw, src_u, dst_u, same = (piece(BIG, 1024 * k, CPAD, I32) for k in range(4))
        raw3 = grid(BIG, 0, CG, P, I32)
        lo_f, dst_f, same_f = piece(BIG, 1024, CPAD), piece(BIG, 2048, CPAD), piece(BIG, 3072, CPAD)
        G = [grid(BIG, 2048 * s, UNROLL, D) for s in range(2)]
        dst_T, lo_T = piece(W2A, S2, CHUNKS, I32), piece(W2A, S2 + CHUNKS, CHUNKS)
        OH = [grid(BIG, 4098, UNROLL, P), grid(W2A, S2 + 2 * CHUNKS, UNROLL, P)]
        tile_row = W2A[0:1, S2 + 2976:S2 + 2976 + CPAD // 2].bitcast(I16)
        idx_s = [piece(W2A, S2 + 3784 + 8 * s, UNROLL, I32) for s in range(2)]

        NE = NT * E
        logits, pick0, pick1, both = (grid(BIG, NE * k, NT, E) for k in range(4))
        tmp, rank, totals, runs = (grid(BIG, NE * k, NT, E) for k in range(4, 8))
        x2 = [piece(BIG, 3136 + 256 * s, D) for s in range(2)]
        x2T = [grid(BIG, 3648 + 256 * s, KD, P) for s in range(2)]
        wr_s, br_s = grid(BIG, 5448, KD, E), piece(BIG, 5464, E)
        stats2 = grid(BIG, 5150, NT, 6)
        expert_m8 = grid(BIG, 4192, NT, E)
        exp_tot, exp_tiles, exp_base, slot_e, exp_i = (piece(BIG, 4592 + 16 * k, E) for k in range(5))
        expI, place_s = piece(BIG, 4680, E, I32), [piece(BIG, 4696 + 2 * s, TOPK, I32) for s in range(4)]
        xs2 = [piece(BIG, 3136 + 256 * s, D) for s in range(4)]
        slot_eI = piece(BIG, 4690, 1, I32)
        b_one_flat = piece(BIG, 4500, KD * E * E)
        b_one = piece(BIG, 4500, KD * E * E).rearrange("p (k e m) -> p k e m", k=KD, e=E)
        bias_f, bias_r = BIG[0:E, 0:BR], BIG[0:E, BR:2 * BR]
        bias_b = BIG[0:E, 2 * BR:2 * BR + 3 * BR // 2].bitcast(BF16).rearrange("e (s n) -> e s n", s=3)
        w1_s = W1A[:, :].rearrange("p (e k n) -> p e k n", e=E, k=KD)
        x_in = [piece(BIG, 256 * s, D) for s in range(2)]
        x_inT = [grid(BIG, 512 + 256 * s, KD, P) for s in range(2)]
        hid = [piece(BIG, 1024 + H * s, H) for s in range(2)]
        hidT = grid(BIG, 3072, KH, P)
        y_out = [piece(BIG, 4096, D), piece(ACC, NT * D, D)]
        hid_bias = [BIG[0:3, 4352 + H // 2 * s:4352 + H // 2 * (s + 1)].bitcast(BF16) for s in range(2)]
        y_bias = [BIG[0:3, 5376 + D // 2 * s:5376 + D // 2 * (s + 1)].bitcast(BF16) for s in range(2)]
        ones3 = iota[0:3, 0:64].bitcast(BF16)
        expert_row = tri[0:1, 0:P].bitcast(I32)
        y0 = [piece(BIG, 512 * s, D) for s in range(4)]
        y1 = [piece(BIG, 512 * s + 256, D) for s in range(4)]
        o_s = [piece(BIG, 2048 + 256 * s, D) for s in range(4)]
        pair_s = [piece(BIG, 3072 + 2 * s, TOPK, I32) for s in range(4)]

        B = [ctx.enter_context(nc.psum_tensor(f"B{k}", [P, 512], F32)) for k in range(8)]

        tk_v, tk_a, tk_t, tk_g, tk_s = (sem(n) for n in ("tk_v", "tk_a", "tk_t", "tk_g", "tk_s"))
        dve_steps, act_steps, pool_steps = sem("dve_steps"), sem("act_steps"), sem("pool_steps")
        consts_ready = sem("consts_ready")
        pads_set = sem("pads_set")
        edges_in, x_in_s, weights_in = sem("edges_in"), sem("x_in"), sem("weights_in")
        cleared_edges, cleared_slots = sem("cleared_edges"), sem("cleared_slots")
        counts_ready, prefix_ready = sem("counts_ready"), sem("prefix_ready")
        ctile_ready, ctile_T, ctile_row, ctile_out = sem("ctile_ready"), sem("ctile_T"), sem("ctile_row"), sem("ctile_out")
        tile_row_in = sem("tile_row_in")
        bn_done, pairs_ready = sem("bn_done"), sem("pairs_ready")
        oh_ready, oh_free = sem("oh_ready"), sem("oh_free")
        std_in, std_out = sem("std_in"), sem("std_out")
        norm_ready = sem("norm_ready")
        xn_ready, t_ready, xnT_ready = sem("xn_ready"), sem("t_ready"), sem("xnT_ready")
        kv_ready, hq_ready, kvfm_ready, kv_done, proj_out = (
            sem("kv_ready"), sem("hq_ready"), sem("kvfm_ready"), sem("kv_done"), sem("proj_out"))
        sums_done = sem("sums_done")
        stage_ready, scat = sem("stage_ready"), sem("scat")
        table_ready, table_out = sem("table_ready"), sem("table_out")
        wo_in, kvbd_ready, kvT_ps, kvT_ready, kvo_ps, qweights = (
            sem("wo_in"), sem("kvbd_ready"), sem("kvT_ps"), sem("kvT_ready"), sem("kvo_ps"), sem("qweights"))
        q_fm, q_sum, q_norm, q_scaled, q_mixed, q_added = (
            sem("q_fm"), sem("q_sum"), sem("q_norm"), sem("q_scaled"), sem("q_mixed"), sem("q_added"))
        raw_in, unpacked, unp_T, unp_out = sem("raw_in"), sem("unpacked"), sem("unp_T"), sem("unp_out")
        idx_ready, gath, onehot_ready, seg, added = (
            sem("idx_ready"), [sem("gath0"), sem("gath1")], sem("onehot_ready"), sem("seg"), sem("added"))
        w1_in, w2_in, lnb_in, b_one_ready, b1_ps, bias_in, bias_ready, bias_out = (
            sem("w1_in"), sem("w2_in"), sem("lnb_in"), sem("b_one_ready"), sem("b1_ps"), sem("bias_in"),
            sem("bias_ready"), sem("bias_out"))
        w1_scaled = sem("w1_scaled")
        x_done = sem("x_done")
        router_in, norm2_ready = sem("router_in"), sem("norm2_ready")
        x2_ready, x2T_ps, x2T_ready, logit_ps, logit_out = (
            sem("x2_ready"), sem("x2T_ps"), sem("x2T_ready"), sem("logit_ps"), sem("logit_out"))
        pick_ready, gap_ready, gap_exp, ranks_ps, places_ready = (
            sem("pick_ready"), sem("gap_ready"), sem("gap_exp"), sem("ranks_ps"), sem("places_ready"))
        slot_e_ready, slot_e_out, slot_e_in = sem("slot_e_ready"), sem("slot_e_out"), sem("slot_e_in")
        disp_ready, disp = sem("disp_ready"), [sem(f"disp{s}") for s in range(4)]
        ones3_ready = sem("ones3_ready")
        xs_in, xsT_ps, xsT_ready = [sem("xs_in0"), sem("xs_in1")], sem("xsT_ps"), sem("xsT_ready")
        y_bias_in = [sem("y_bias_in0"), sem("y_bias_in1")]
        hid_ps, hid_ready, hidT_ps, hidT_ready = sem("hid_ps"), sem("hid_ready"), sem("hidT_ps"), sem("hidT_ready")
        y_ps, y_ready, y_sent = sem("y_ps"), sem("y_ready"), [sem("y_sent0"), sem("y_sent1")]
        pair_ready, pair_in, o_ready, o_sent = (
            sem("pair_ready"), [sem(f"pair_in{s}") for s in range(4)], sem("o_ready"), [sem(f"o_sent{s}") for s in range(4)])

        block = ctx.enter_context(nc.Block())

        @block.sync
        def _(sp):
            sp.dma_start(srcI[:, 0:FULL], src).then_inc(edges_in, 16)
            sp.dma_start(dstI[:, 0:FULL], dst).then_inc(edges_in, 16)
            sp.wait_ge(pads_set, 1)
            with nc.allow_non_contiguous_dma(reason="one edge per partition"):
                sp.dma_start(srcI[0:REST, FULL:FULL + 1], src_rest).then_inc(edges_in, 16)
                sp.dma_start(dstI[0:REST, FULL:FULL + 1], dst_rest).then_inc(edges_in, 16)
            sp.dma_start(xr[:, 0:NT - 1, :], x[0:(NT - 1) * P, :].rearrange("(t p) d -> p t d", p=P)).then_inc(x_in_s, 16)
            sp.dma_start(xr[0:LAST, NT - 1, :], x[(NT - 1) * P:N_NODES, :]).then_inc(x_in_s, 16)
            sp.dma_start(wkv_s, wkv.rearrange("(k p) n -> p k n", p=P)).then_inc(weights_in, 16)
            sp.dma_start(gw_s, gnn_w.rearrange("(k p) n -> p k n", p=P)).then_inc(weights_in, 16)
            sp.dma_start(wq_s, wq.rearrange("(k p) n -> p k n", p=P)).then_inc(weights_in, 16)
            sp.dma_start(bqc, bq).then_inc(weights_in, 16)
            sp.dma_start(bkv_row, bkv).then_inc(weights_in, 16)
            sp.dma_start(bo_row, bo).then_inc(weights_in, 16)
            sp.wait_ge(consts_ready, 1)
            sp.dma_start(edge_rows.rearrange("(p a) r -> p (a r)", p=P).rearrange("p (m z) -> p m z", z=D),
                         zeros.bitcast(I32).rearrange("p (m z) -> p m z", m=1).to_broadcast([P, CPAD * P // P // D, D])
                         ).then_inc(cleared_edges, 16)
            for k in range(ST // 15):
                sp.dma_start(slot_x[k * 15 * P:(k + 1) * 15 * P, :].rearrange("(p m) z -> p m z", p=P),
                             zeros.rearrange("p (m z) -> p m z", m=1).to_broadcast([P, 15, D])).then_inc(cleared_slots, 16)
            sp.wait_ge(ctile_row, 1)
            sp.dma_start(chunk_tiles.rearrange("(j p) -> j p", p=P), CT_row).then_inc(ctile_out, 16)
            for k in range(TPARTS):
                sp.wait_ge(table_ready, k + 1)
                ts_ = slice(k * TPART, (k + 1) * TPART)
                sp.dma_start(table.rearrange("(t p) d -> p t d", p=P)[:, ts_, :], acc[:, ts_, :]).then_inc(table_out, 16)
            sp.dma_start(wo_s, wo.rearrange("(k p) n -> p k n", p=P)).then_inc(wo_in, 16)
            sp.wait_ge(scat, 16 * GR * NG)
            sp.wait_ge(kv_done, NT)
            sp.wait_ge(ctile_out, 16)
            sp.dma_start(raw3, edge_rows.rearrange("(j p a) r -> p j (a r)", p=P, a=RPC)).then_inc(raw_in, 16)
            sp.dma_start(tile_row, chunk_tiles.rearrange("(o n) -> o n", o=1)).then_inc(tile_row_in, 16)
            sp.wait_ge(q_added, NT)
            sp.dma_start(w1_s, w1.rearrange("e (k p) n -> p e k n", p=P)).then_inc(w1_in, 16)
            sp.dma_start(g_s, ln_gT.rearrange("(k p) e -> p k e", p=P)).then_inc(lnb_in, 16)
            sp.dma_start(b_s, ln_bT.rearrange("(k p) e -> p k e", p=P)).then_inc(lnb_in, 16)
            sp.wait_ge(cleared_edges, 16)
            sp.wait_ge(cleared_slots, 16 * (ST // 15))
            sp.wait_ge(x_done, 1)
            sp.dma_start(W2A[:, :].rearrange("p (e c n) -> p e c n", e=E, c=KH),
                         w2.rearrange("e (c p) n -> p e c n", p=P)).then_inc(w2_in, 16)
            sp.dma_start(bias_f[:, 0:H], b1).then_inc(bias_in, 16)
            sp.dma_start(bias_f[:, H:BR], b2).then_inc(bias_in, 16)
            sp.wait_ge(bias_ready, 1)
            sp.dma_start(bias_rows, bias_b).then_inc(bias_out, 16)
            sp.wait_ge(bias_out, 16)
            sp.dma_start(wr_s, wr.rearrange("(k p) e -> p k e", p=P)).then_inc(router_in, 16)
            sp.dma_start(br_s, br.to_broadcast([P, E])).then_inc(router_in, 16)
            sp.wait_ge(slot_e_ready, 1)
            with nc.allow_non_contiguous_dma(reason="one expert number per partition"):
                sp.dma_start(slot_experts.rearrange("(p o) -> p o", o=1), slot_eI).then_inc(slot_e_out, 16)
            sp.wait_ge(slot_e_out, 16)
            sp.dma_start(expert_row, slot_experts.rearrange("(o p) -> o p", o=1)).then_inc(slot_e_in, 16)
            sp.wait_ge(slot_e_in, 16)
            for s in range(4):
                sp.wait_ge(disp[s], 32 * ((NT + 3 - s) // 4))

            def expert_of(t):
                return nc.sync.value_load(expert_row[0:1, bass.ds(t, 1)], min_val=0, max_val=E - 1)

            def load_x(t, s):
                e = expert_of(t)
                when(sp, tk_s, xsT_ps, t - 1)
                when(sp, tk_s, hid_ps, t - 1)
                sp.dma_start(x_in[s], slot_x[bass.ds(t * P, P), :]).then_inc(xs_in[s], 16)
                sp.dma_start(hid_bias[s], bias_rows[bass.ds(e, 1), :, 0:H].rearrange("o s n -> (o s) n")).then_inc(xs_in[s], 16)

            def load_y_bias(t, s):
                e = expert_of(t)
                when(sp, tk_s, y_ps, t - 1)
                sp.dma_start(y_bias[s], bias_rows[bass.ds(e, 1), :, H:BR].rearrange("o s n -> (o s) n")).then_inc(y_bias_in[s], 16)

            def send_y(t, s):
                when(sp, tk_s, y_ready, t + 1)
                sp.dma_start(slot_y[bass.ds(t * P, P), :], y_out[s]).then_inc(y_sent[s], 16)

            for t in range(2):
                load_x(t, t)
                load_y_bias(t, t)
            load_x(2, 0)
            with sp.Fori(0, (ST - 3) // 2) as i:
                for u in range(2):
                    load_x(i * 2 + u + 3, 1 - u)
                    load_y_bias(i * 2 + u + 2, u)
                    send_y(i * 2 + u, u)
            load_y_bias(ST - 1, 0)
            for t in range(ST - 3, ST):
                send_y(t, t % 2)

            def send_o(t, s):
                rows = LAST if isinstance(t, int) and t == NT - 1 else P
                when(sp, tk_s, o_ready, t + 1)
                sp.dma_start(out[bass.ds(t * P, rows), :], o_s[s][0:rows, :]).then_inc(o_sent[s], 16)

            tiles(sp, send_o, 4)
            for s in range(4):
                sp.wait_ge(o_sent[s], 16 * ((NT + 3 - s) // 4))
            sp.wait_ge(y_sent[0], 16 * (ST // 2 + 1))
            sp.wait_ge(y_sent[1], 16 * (ST // 2))

        @block.gpsimd
        def _(pool):
            ch = Chain(pool, pool_steps)
            ch.add(pool.memset(zeros, 0.0))
            ch.sync()
            pool.sem_inc(consts_ready, 1)
            ch.add(pool.memset(ident, 0.0))
            ch.add(pool.memset(tri, 1.0))
            ch.add(pool.memset(ones, 1.0))
            ch.add(pool.memset(mask, 1.0))
            ch.add(pool.iota(iota, pattern=[[1, P]], base=0, channel_multiplier=0, allow_small_or_imprecise_dtypes=True))
            ch.add(pool.iota(pcol, pattern=[[0, 1]], base=0, channel_multiplier=1, allow_small_or_imprecise_dtypes=True))
            ch.add(pool.iota(junk, pattern=[[0, NT]], base=SLOTS, channel_multiplier=1, allow_small_or_imprecise_dtypes=True))
            ch.sync()
            ch.add(pool.affine_select(out=ident, in_=ident, compare_op=ALU.not_equal, fill=1.0, base=0,
                                      pattern=[[-1, P]], channel_multiplier=1))
            ch.add(pool.affine_select(out=tri, in_=tri, compare_op=ALU.is_gt, fill=0.0, base=0,
                                      pattern=[[1, P]], channel_multiplier=-1))
            ch.add(pool.affine_select(out=mask[:, NT - 1:NT], in_=mask[:, NT - 1:NT], compare_op=ALU.is_ge, fill=0.0,
                                      base=LAST - 1, pattern=[[0, 1]], channel_multiplier=-1))
            ch.sync()
            pool.sem_inc(consts_ready, 1)
            pool.wait_ge(cleared_edges, 16)
            with pool.Fori(0, NG) as g:
                when(pool, tk_g, stage_ready, g + 1)
                for j in range(GR):
                    pool.indirect_dma_start(edge_rows, bass.IndirectOffsetOnAxis(ap=row_at[:, j:j + 1], axis=0),
                                            stage_raw[:, ROW * j:ROW * (j + 1)], None).then_inc(scat, 16)
            pool.wait_ge(table_out, 16 * TPARTS)
            with pool.Fori(0, STEPS) as i:
                for h in range(2):
                    when(pool, tk_g, idx_ready, i * 2 + h + 1)
                    for u in range(UNROLL):
                        pool.indirect_dma_start(G[h][:, u, :], None, table,
                                                bass.IndirectOffsetOnAxis(ap=idx_s[h][:, u:u + 1], axis=0)).then_inc(gath[h], 16)
            pool.wait_ge(cleared_slots, 16 * (ST // 15))

            def dispatch(t, s):
                when(pool, tk_g, disp_ready, t + 1)
                for c in range(TOPK):
                    pool.indirect_dma_start(slot_x, bass.IndirectOffsetOnAxis(ap=place_s[s][:, c:c + 1], axis=0),
                                            xs2[s], None).then_inc(disp[s], 16)

            tiles(pool, dispatch, 4)
            pool.wait_ge(y_sent[0], 16 * (ST // 2 + 1))
            pool.wait_ge(y_sent[1], 16 * (ST // 2))

            def combine(t, s):
                when(pool, tk_g, pair_ready, t + 1)
                for c, y in enumerate((y0, y1)):
                    pool.indirect_dma_start(y[s], None, slot_y,
                                            bass.IndirectOffsetOnAxis(ap=pair_s[s][:, c:c + 1], axis=0)).then_inc(pair_in[s], 16)

            tiles(pool, combine, 4)

        @block.vector
        def _(dve):
            ch = Chain(dve, dve_steps)

            def tt(o, a, b, op):
                return dve.tensor_tensor(o, a, b, op)

            def ts(o, a, s1, op0, s2=None, op1=ALU.bypass):
                return dve.tensor_scalar(o, a, s1, s2, op0, op1)

            def scan(o, a):
                return dve.tensor_tensor_scan(o, ones[:, 0:a.shape[1]], a, 0.0, ALU.mult, ALU.add)

            ch.add(dve.memset(xr[:, NT - 1, :], 0.0))
            ch.add(dve.memset(srcI[:, FULL:EC], PAD))
            ch.add(dve.memset(dstI[:, FULL:EC], PAD))
            ch.sync()
            dve.sem_inc(pads_set, 1)
            dve.wait_ge(edges_in, 64)
            dve.wait_ge(consts_ready, 2)
            ch.link(ts(packed, srcI, CODE, ALU.logical_shift_left))
            ch.link(tt(packed, packed, dstI, ALU.bitwise_or))
            ch.add(ts(workI[:, 0:EC], packed, MASK, ALU.bitwise_xor, FLAG, ALU.bitwise_or))
            ch.sync()
            ch.link(ts(packed, srcI, 7, ALU.logical_shift_right))
            ch.link(dve.tensor_copy(tile_of, packed))
            ch.link(tt(packed, srcI, dstI, ALU.is_equal))
            ch.link(ts(srcI, dstI, 7, ALU.logical_shift_right))
            ch.add(dve.tensor_copy(hi_of, srcI))
            ch.link(ts(dstI, dstI, P - 1, ALU.bitwise_and))
            ch.link(dve.scalar_tensor_tensor(out=lo_of, in0=packed, scalar=float(2 * P), in1=dstI, op0=ALU.mult, op1=ALU.add))
            cnt, need, nrow, rows_before, rs, nch, cb, off, t0 = col[0:9]
            nI = small(19, 50, I32)

            with dve.Fori(0, NT // 7) as i:
                for u in range(7):
                    t = i * 7 + u
                    dve.tensor_scalar(eq_scratch[u % 2], tile_of, iota[:, bass.ds(t, 1)], None, ALU.is_equal, ALU.add,
                                      accum_out=cnt[:, bass.ds(t, 1)])
                    if u != 0:
                        dve.drain()
            ch.link(ts(nI[:, 0:NT], cnt[:, 0:NT], float(ROW - 1), ALU.add))
            ch.link(ts(nI[:, 0:NT], nI[:, 0:NT], 2, ALU.logical_shift_right))
            ch.link(dve.tensor_copy(nrow[:, 0:NT], nI[:, 0:NT]))
            ch.add(dve.scalar_tensor_tensor(out=need[:, 0:NT], in0=nrow[:, 0:NT], scalar=float(ROW), in1=cnt[:, 0:NT],
                                            op0=ALU.mult, op1=ALU.subtract))
            ch.link(dve.reduce_sum(t0[:, 0:1], nrow[:, 0:NT], axis=AX.X))
            ch.link(ts(nrow[:, NT:NT + 1], t0[:, 0:1], -1.0, ALU.mult, float(SORTN // ROW), ALU.add))
            dve.sem_inc(counts_ready, 1)
            for j in range(ROW - 1):
                ch.add(ts(fill[:, :, j], need[:, 0:NT], float(j), ALU.is_gt))
            ch.add(ts(t0[:, 0:NT], iota[:, 0:NT], -1.0, ALU.mult, float(NT), ALU.add))
            ch.sync()
            ch.link(tt(fill, fill, t0[:, 0:NT].unsqueeze(2).to_broadcast([P, NT, 3]), ALU.mult))
            ch.add(ts(fill_flat[:, 0:3 * NT], fill_flat[:, 0:3 * NT], -1.0, ALU.mult, float(NT), ALU.add))
            ch.add(dve.memset(fill_flat[:, 3 * NT:NF], float(NT)))
            ch.sync()
            ch.link(ts(fillI, fill_flat, float(P * ((1 << CODE) + 1)), ALU.mult))
            ch.add(ts(workI[:, EC:SORTN], fillI, MASK, ALU.bitwise_xor, FLAG, ALU.bitwise_or))
            dve.wait_ge(prefix_ready, 1)
            ch.link(ts(nI, B[6][:, 64:64 + NT + 1], float(RPC - 1), ALU.add))
            ch.link(ts(nI, nI, 5, ALU.logical_shift_right))
            ch.link(dve.tensor_copy(nch, nI))
            ch.link(scan(cb, nch))
            ch.link(tt(cb, cb, nch, ALU.subtract))
            ch.link(scan(rs, nrow))
            ch.link(tt(rs, rs, nrow, ALU.subtract))
            ch.link(dve.scalar_tensor_tensor(out=off, in0=cb, scalar=float(RPC), in1=rs, op0=ALU.mult, op1=ALU.subtract))
            ch.link(tt(off, off, B[6][:, 0:NT + 1], ALU.add))
            cgrid, ctile = col[9][:, 0:CG], col[10][:, 0:CG]
            ch.link(ts(cgrid, iota[:, 0:CG], float(P), ALU.mult, pcol, ALU.add))
            ch.link(tt(tile_cmp, cgrid.unsqueeze(2).to_broadcast([P, CG, NT]),
                       cb[:, 1:NT + 1].unsqueeze(1).to_broadcast([P, CG, NT]), ALU.is_ge))
            ch.link(dve.tensor_reduce(ctile, tile_cmp, axis=AX.X, op=ALU.add))
            dve.sem_inc(ctile_ready, 1)
            dve.wait_ge(ctile_T, 1)
            ch.link(dve.tensor_copy(CT_row, B[6][0:CG, 128:256]))
            dve.sem_inc(ctile_row, 1)
            dve.wait_ge(x_in_s, 32)
            

            def half_stats(st6):
                mean, var, dm = col[9], col[10], col[11]
                ch.add(tt(mean[:, 0:NT], st6[:, :, 1], st6[:, :, 4], ALU.add))
                ch.add(tt(dm[:, 0:NT], st6[:, :, 1], st6[:, :, 4], ALU.subtract))
                ch.add(tt(var[:, 0:NT], st6[:, :, 2], st6[:, :, 5], ALU.add))
                ch.sync()
                ch.add(ts(mean[:, 0:NT], mean[:, 0:NT], 0.5, ALU.mult))
                ch.add(tt(dm[:, 0:NT], dm[:, 0:NT], dm[:, 0:NT], ALU.mult))
                ch.add(ts(var[:, 0:NT], var[:, 0:NT], 1.0 / D, ALU.mult))
                ch.sync()
                ch.link(dve.scalar_tensor_tensor(out=var[:, 0:NT], in0=dm[:, 0:NT], scalar=0.25, in1=var[:, 0:NT],
                                                 op0=ALU.mult, op1=ALU.add))
                return mean, var

            with dve.Fori(0, NT // 7) as i:
                for u in range(7):
                    t = i * 7 + u
                    dve.bn_stats(stats_x[:, bass.ds(t, 1), :], xr[:, bass.ds(t, 1), :]).then_inc(bn_done, 1)
            dve.wait_ge(bn_done, NT)
            mean, var = half_stats(stats_x)
            ch.link(ts(var[:, 0:NT], var[:, 0:NT], LN_EPS, ALU.add))
            dve.sem_inc(std_in, 1)
            dve.wait_ge(std_out, 1)
            ch.link(dve.reciprocal(rstd, col[12][:, 0:NT]))
            ch.link(dve.scalar_tensor_tensor(out=nmr, in0=mean[:, 0:NT], scalar=-1.0, in1=rstd, op0=ALU.mult, op1=ALU.mult))
            dve.sem_inc(norm_ready, 1)
            ch.link(dve.tensor_copy(row_k, iota[:, 0:GR]))

            def sort_group(g):
                for u in range(GSTEPS):
                    eight = sorted_g[:, 8 * u:8 * u + 8]
                    dve.max(eight, work)
                    dve.drain()
                    dve.match_replace(out=work, in_to_replace=eight, in_values=work, imm_value=0.0)
                    dve.drain()
                when(dve, tk_v, scat, g * (16 * GR))
                ts(stage_raw, sorted_i, MASK, ALU.bitwise_xor, MASK, ALU.bitwise_and)
                dve.drain()
                ts(row_tileI, stage_raw[:, ::ROW], CODE + 7, ALU.logical_shift_right)
                dve.drain()
                dve.tensor_copy(row_tile, row_tileI)
                dve.drain()
                tt(lookup, row_tile.unsqueeze(2).to_broadcast([P, GR, NT + 1]),
                   iota[:, 0:NT + 1].unsqueeze(1).to_broadcast([P, GR, NT + 1]), ALU.is_equal)
                dve.drain()
                tt(lookup, lookup, off.unsqueeze(1).to_broadcast([P, GR, NT + 1]), ALU.mult)
                dve.drain()
                dve.tensor_reduce(row_sum, lookup, axis=AX.X, op=ALU.add)
                dve.drain()
                tt(row_at, row_sum, row_k, ALU.add).then_inc(stage_ready, 1)
                dve.drain()
                ts(row_k, row_k, float(GR), ALU.add)
                dve.drain()

            sort_group(0)
            with dve.Fori(1, NG) as g:
                sort_group(g)
            ch.link(dve.tensor_copy(digits, iota.unsqueeze(2).to_broadcast([P, P, HB])))

            def onehots(t, s):
                when(dve, tk_v, oh_free, t - 1)
                lo = lo_of[:, bass.ds(t * HB, HB)].unsqueeze(1).to_broadcast([P, P, HB])
                hi = hi_of[:, bass.ds(t * HB, HB)].unsqueeze(1).to_broadcast([P, NT, HB])
                tt(oh_lo[s], digits, lo, ALU.is_equal)
                tt(oh_hi[s], digits[:, 0:NT, :], hi, ALU.is_equal).then_inc(oh_ready, 1)

            tiles(dve, onehots)
            dve.wait_ge(sums_done, 1)
            ch.link(ts(col[9][:, 0:NT], B[5][:, 0:NT], 1.0, ALU.add))
            dve.sem_inc(std_in, 1)
            dve.wait_ge(std_out, 2)
            ch.link(dve.reciprocal(dinv, col[12][:, 0:NT]))
            ch.add(dve.memset(acc[:, NT, :], 0.0))
            for k in range(TPARTS):
                a = acc[:, k * TPART:(k + 1) * TPART, :]
                tt(a, a, dinv[:, k * TPART:(k + 1) * TPART].unsqueeze(2).to_broadcast([P, TPART, D]),
                   ALU.mult).then_inc(table_ready, 1)
            ch.link(dve.memset(head_mask, 0.0))
            for b in range(P // DEPTH):
                ch.add(dve.memset(head_mask[b * DEPTH:(b + 1) * DEPTH, b * DEPTH:(b + 1) * DEPTH], 1.0))
            ch.sync()
            for g in range(KD):
                ch.add(tt(kv_bd[:, g, :], B[3 + g][:, 0:P], head_mask, ALU.mult))
                ch.add(dve.tensor_copy(ksum[:, g:g + 1], B[3 + g][:, P:P + 1]))
            ch.sync()
            for g in range(KD):
                ch.add(ts(ks_out[:, g, :], head_mask, ksum[:, g:g + 1], ALU.mult))
            ch.sync()
            dve.sem_inc(kvbd_ready, 1)
            dve.wait_ge(kvT_ps, 1)
            ch.link(dve.tensor_copy(kvT, B[0][:, 0:D].rearrange("p (g n) -> p g n", g=KD)))
            dve.sem_inc(kvT_ready, 1)
            dve.wait_ge(kvo_ps, 1)
            ch.link(dve.tensor_copy(kv_out, B[1][:, :].rearrange("p (g n) -> p g n", g=KD)))
            dve.sem_inc(qweights, 1)

            def add_terms(t):
                when(dve, tk_v, q_fm, t + 1)
                tt(q_pos, q_pos_in, q_exp, ALU.add).then_inc(q_sum, 1)

            def divide(t):
                when(dve, tk_v, q_norm, t + 1)
                ts(q_den, B[4][:, 0:D], 1e-6, ALU.add)
                dve.drain()
                dve.reciprocal(q_den, q_den)
                dve.drain()
                tt(q_sc, q_pos, q_den, ALU.mult).then_inc(q_scaled, 1)
                dve.drain()

            def add_attention(t):
                when(dve, tk_v, q_mixed, t + 1)
                xt = xr[:, bass.ds(t, 1), :].rearrange("p o d -> p (o d)")
                tt(xt, xt, B[7][:, 0:D], ALU.add).then_inc(q_added, 1)

            dve.wait_ge(raw_in, 16)
            ch.add(ts(src_u, raw, CODE, ALU.logical_shift_right))
            ch.add(ts(dst_u, raw, (1 << CODE) - 1, ALU.bitwise_and))
            ch.sync()
            ch.link(tt(same_f, src_u, dst_u, ALU.is_equal))
            ch.add(ts(dst_f, dst_u, float(NT * P - 1), ALU.min))
            ch.link(ts(raw, src_u, P - 1, ALU.bitwise_and))
            ch.link(dve.scalar_tensor_tensor(out=lo_f, in0=same_f, scalar=float(2 * P), in1=raw, op0=ALU.mult, op1=ALU.add))
            dve.sem_inc(unpacked, 1)
            for k in range(4):
                dve.wait_ge(unp_T, k + 1)
                n = min(512, CHUNKS - 512 * (k % 2))
                to = (dst_T, lo_T)[k // 2]
                ch.add(dve.tensor_copy(to[:, 512 * (k % 2):512 * (k % 2) + n], B[k][:, 0:n]))
            ch.sync()
            dve.sem_inc(unp_out, 1)
            dve.wait_ge(tile_row_in, 16)

            def onehot(n, h):
                when(dve, tk_v, seg, n * 8 - 8)
                tt(OH[h], iota.unsqueeze(1).to_broadcast([P, UNROLL, P]),
                   lo_T[:, bass.ds(n * UNROLL, UNROLL)].unsqueeze(2).to_broadcast([P, UNROLL, P]),
                   ALU.is_equal).then_inc(onehot_ready, 1)

            def add_sums(n):
                _, at = nc.values_load_multi_w_load_instructions(
                    tile_row[0:1, bass.ds(n * UNROLL, UNROLL)], engines=[mybir.EngineType.DVE], min_val=0, max_val=NT)
                when(dve, tk_v, seg, n * 8 + 8)
                for u in range(UNROLL):
                    a = ACC[:, bass.ds(at[u] * D, D)]
                    tt(a, a, B[u // 2][:, (u % 2) * D:(u % 2 + 1) * D], ALU.add)
                    dve.drain()
                dve.sem_inc(added, 1)

            add_terms(0)
            onehot(0, 0)
            onehot(1, 1)
            add_sums(0)
            divide(0)
            with dve.Fori(1, NT) as i:
                add_terms(i)
                onehot(i * 2, 0)
                add_sums(i * 2 - 1)
                add_attention(i - 1)
                onehot(i * 2 + 1, 1)
                add_sums(i * 2)
                divide(i)
            add_attention(NT - 1)
            with dve.Fori(NT, STEPS) as i:
                for h in range(2):
                    onehot(i * 2 + h, h)
                    add_sums(i * 2 + h - 1)
            add_sums(2 * STEPS - 1)
            dve.wait_ge(lnb_in, 32)
            ch.link(dve.memset(b_one_flat, 0.0))
            for k in range(KD):
                for e in range(E):
                    ch.add(dve.tensor_copy(b_one[:, k, e, e:e + 1], b_s[:, k, e:e + 1]))
            ch.sync()
            dve.sem_inc(b_one_ready, 1)
            dve.wait_ge(q_added, NT)

            def residual(t):
                a = acc[:, bass.ds(t, 1), :].rearrange("p o d -> p (o d)")
                xt = xr[:, bass.ds(t, 1), :].rearrange("p o d -> p (o d)")
                return dve.scalar_tensor_tensor(out=a, in0=a, scalar=dinv[:, bass.ds(t, 1)], in1=xt, op0=ALU.mult, op1=ALU.add)

            with dve.Fori(0, NT // 7) as i:
                for u in range(7):
                    residual(i * 7 + u)
                dve.drain()
                for u in range(7):
                    t = i * 7 + u
                    dve.bn_stats(stats2[:, bass.ds(t, 1), :], acc[:, bass.ds(t, 1), :]).then_inc(bn_done, 1)
            dve.sem_inc(x_done, 1)
            dve.wait_ge(bias_in, 32)
            dve.wait_ge(b1_ps, 1)
            for n in range(2):
                ch.add(tt(bias_f[:, 512 * n:512 * n + 512], bias_f[:, 512 * n:512 * n + 512], B[6 + n][0:E, :], ALU.add))
            ch.sync()
            ch.link(dve.tensor_copy(bias_b[:, 0, :], bias_f))
            ch.link(tt(bias_r, bias_f, bias_b[:, 0, :], ALU.subtract))
            ch.link(dve.tensor_copy(bias_b[:, 1, :], bias_r))
            ch.link(tt(bias_r, bias_r, bias_b[:, 1, :], ALU.subtract))
            ch.link(dve.tensor_copy(bias_b[:, 2, :], bias_r))
            dve.sem_inc(bias_ready, 1)
            dve.wait_ge(bn_done, 2 * NT)
            mean, var = half_stats(stats2)
            ch.link(ts(col[13][:, 0:NT], var[:, 0:NT], LN_EPS, ALU.add))
            dve.sem_inc(std_in, 1)
            dve.wait_ge(std_out, 3)
            ch.link(dve.reciprocal(rstd, col[12][:, 0:NT]))
            ch.add(dve.scalar_tensor_tensor(out=nmr, in0=mean[:, 0:NT], scalar=-1.0, in1=rstd, op0=ALU.mult, op1=ALU.mult))
            ch.link(tt(col[13][:, 0:NT], rstd, rstd, ALU.mult))
            ch.link(tt(col[13][:, 0:NT], col[13][:, 0:NT], var[:, 0:NT], ALU.mult))
            ch.link(ts(col[13][:, 0:NT], col[13][:, 0:NT], LN_EPS, ALU.add))
            dve.sem_inc(std_in, 1)
            dve.wait_ge(std_out, 4)
            ch.link(dve.reciprocal(rstd2a, col[12][:, 0:NT]))
            ch.link(tt(rstd2, rstd2a, rstd, ALU.mult))
            ch.link(tt(nmr2, rstd2a, nmr, ALU.mult))
            dve.sem_inc(norm2_ready, 1)
            dve.wait_ge(bias_out, 16)

            def route(t, s):
                when(dve, tk_v, x2T_ps, t + 1)
                when(dve, tk_v, logit_ps, t - 1)
                dve.tensor_copy(x2T[s], B[s][:, 0:D].rearrange("p (g n) -> p g n", g=KD)).then_inc(x2T_ready, 1)

            tiles(dve, route)
            dve.wait_ge(logit_out, NT)
            dve.wait_ge(router_in, 32)
            full = [P, NT, E]
            ch.link(tt(logits, logits, br_s.unsqueeze(1).to_broadcast(full), ALU.add))
            ch.add(ts(slot_e, iota[:, 0:E], -float(E), ALU.add))
            ch.sync()
            ch.link(dve.tensor_copy(expert_m8, slot_e.unsqueeze(1).to_broadcast(full)))
            best, which = col[9][:, 0:NT], col[10][:, 0:NT]
            second = col[11][:, 0:NT]
            for k, (top, pick) in enumerate(((best, pick0), (second, pick1))):
                ch.link(dve.tensor_reduce(top, logits, axis=AX.X, op=ALU.max))
                ch.link(tt(tmp, logits, top.unsqueeze(2).to_broadcast(full), ALU.is_equal))
                ch.link(tt(tmp, tmp, expert_m8, ALU.mult))
                ch.link(dve.tensor_reduce(which, tmp, axis=AX.X, op=ALU.min))
                ch.link(tt(pick, expert_m8, which.unsqueeze(2).to_broadcast(full), ALU.is_equal))
                if k == 0:
                    ch.link(dve.scalar_tensor_tensor(out=logits, in0=pick, scalar=-3e38, in1=logits, op0=ALU.mult, op1=ALU.add))
            ch.link(tt(both, pick0, pick1, ALU.add))
            ch.link(tt(both, both, mask.unsqueeze(2).to_broadcast(full), ALU.mult))
            dve.sem_inc(pick_ready, 1)
            ch.link(tt(second, second, best, ALU.subtract))
            dve.sem_inc(gap_ready, 1)
            dve.wait_ge(gap_exp, 1)
            ch.link(ts(gate0, gate1, 1.0, ALU.add))
            ch.link(dve.reciprocal(gate0, gate0))
            ch.link(tt(gate1, gate1, gate0, ALU.mult))
            dve.wait_ge(ranks_ps, 1)
            fl = lambda a: a.rearrange("p t e -> p (t e)")
            ch.add(dve.tensor_copy(fl(rank), B[2][:, 0:NE]))
            ch.add(dve.tensor_copy(fl(totals), B[3][:, 0:NE]))
            ch.sync()
            for e in range(E):
                ch.add(scan(runs[:, :, e], totals[:, :, e]))
            ch.sync()
            ch.link(dve.tensor_copy(exp_tot, runs[:, NT - 1, :]))
            ch.add(tt(runs, runs, totals, ALU.subtract))
            ch.sync()
            ch.link(tt(rank, rank, runs, ALU.add))
            ch.link(ts(expI, exp_tot, float(P - 1), ALU.add))
            ch.link(ts(expI, expI, 7, ALU.logical_shift_right))
            ch.link(dve.tensor_copy(exp_tiles, expI))
            ch.link(scan(exp_i, exp_tiles))
            ch.link(tt(exp_base, exp_i, exp_tiles, ALU.subtract))
            ch.link(ts(slot_e[:, 0:E - 1], exp_i[:, 0:E - 1], pcol, ALU.is_le))
            ch.link(dve.reduce_sum(exp_tot[:, 0:1], slot_e[:, 0:E - 1], axis=AX.X))
            ch.link(dve.tensor_copy(slot_eI, exp_tot[:, 0:1]))
            dve.sem_inc(slot_e_ready, 1)
            ch.link(ts(exp_base, exp_base, float(P), ALU.mult))
            ch.link(tt(rank, rank, exp_base.unsqueeze(1).to_broadcast(full), ALU.add))
            inv = col[12][:, 0:NT]
            ch.link(ts(inv, mask, -1.0, ALU.mult, 1.0, ALU.add))
            ch.link(tt(junk, junk, inv, ALU.mult))
            for c, (pick, place) in enumerate(((pick0, place0), (pick1, place1))):
                pf = col[13][:, 0:NT]
                ch.link(tt(tmp, rank, pick, ALU.mult))
                ch.link(dve.tensor_reduce(pf, tmp, axis=AX.X, op=ALU.add))
                ch.link(tt(pf, pf, mask, ALU.mult))
                ch.link(tt(pf, pf, junk, ALU.add))
                if c:
                    ch.link(dve.scalar_tensor_tensor(out=pf, in0=inv, scalar=float(P), in1=pf, op0=ALU.mult, op1=ALU.add))
                ch.link(dve.tensor_copy(place, pf))
            dve.sem_inc(places_ready, 1)
            ch.link(dve.memset(ones3, 1.0))
            dve.sem_inc(ones3_ready, 1)
            for s in range(4):
                dve.wait_ge(disp[s], 32 * ((NT + 3 - s) // 4))
            for place in (place0, place1):
                ch.add(ts(place, place, float(SLOTS - 1), ALU.min))
            ch.sync()
            dve.sem_inc(pairs_ready, 1)

            def inputs(t, s):
                when(dve, tk_v, xsT_ps, t + 1)
                when(dve, tk_v, hid_ps, t - 1)
                dve.tensor_copy(x_inT[s], B[6][:, s * D:(s + 1) * D].rearrange("p (g n) -> p g n", g=KD)).then_inc(xsT_ready, 1)

            def hidden(t):
                for g in range(2):
                    when(dve, tk_v, hidT_ps, t * 2 + g + 1)
                    if g == 0:
                        when(dve, tk_v, y_ps, t)
                    dve.tensor_copy(hidT[:, 4 * g:4 * g + 4, :],
                                    B[4 + g][:, :].rearrange("p (g n) -> p g n", g=4)).then_inc(hidT_ready, 1)

            def outputs(t, s):
                when(dve, tk_v, y_ps, t + 1)
                when(dve, tk_v, y_sent[s], (t - s) * 8)
                dve.tensor_copy(y_out[s], B[7][:, 0:D]).then_inc(y_ready, 1)

            def step(t, s):
                hidden(t)
                if not isinstance(t, int) or t + 2 < ST:
                    inputs(t + 2, s)
                outputs(t, s)

            inputs(0, 0)
            inputs(1, 1)
            for t in range(3):
                step(t, t % 2)
            with dve.Fori(1, ST // 2 - 1) as i:
                step(i * 2 + 1, 1)
                step(i * 2 + 2, 0)
            for t in range(ST - 2, ST):
                step(t, t % 2)

            def combine(t, s):
                when(dve, tk_v, pair_in[s], (t - s) * 8 + 32)
                when(dve, tk_v, o_sent[s], (t - s) * 4)
                at = acc[:, bass.ds(t, 1), :].rearrange("p o d -> p (o d)")
                dve.scalar_tensor_tensor(out=o_s[s], in0=y0[s], scalar=gate0[:, bass.ds(t, 1)], in1=at,
                                         op0=ALU.mult, op1=ALU.add)
                dve.drain()
                dve.scalar_tensor_tensor(out=o_s[s], in0=y1[s], scalar=gate1[:, bass.ds(t, 1)], in1=o_s[s],
                                         op0=ALU.mult, op1=ALU.add).then_inc(o_ready, 1)

            tiles(dve, combine, 4)

        @block.scalar
        def _(act):
            ch = Chain(act, act_steps)

            def cp(o, i, fn=ACT.Copy, **kw):
                return nc.scalar.activation(o, i, fn, **kw)

            act.wait_ge(std_in, 1)
            cp(col[12][:, 0:NT], col[10][:, 0:NT], ACT.Sqrt).then_inc(std_out, 1)
            act.wait_ge(norm_ready, 1)
            act.wait_ge(weights_in, 96)

            def normalize(t, s):
                when(act, tk_a, t_ready, t - 1)
                xt = xr[:, bass.ds(t, 1), :].rearrange("p o d -> p (o d)")
                cp(xn[s], xt, ACT.Identity, scale=rstd[:, bass.ds(t, 1)], bias=nmr[:, bass.ds(t, 1)]).then_inc(xn_ready, 1)

            def transposed(t, s):
                when(act, tk_a, t_ready, t + 1)
                when(act, tk_a, hq_ready, t - 1)
                cp(xnT[s], B[0][:, s * D:(s + 1) * D].rearrange("p (g n) -> p g n", g=KD)).then_inc(xnT_ready, 1)

            def keys_values(t):
                when(act, tk_a, kv_ready, t + 1)
                when(act, tk_a, kv_done, t)
                cp(ka, B[1][:, 0:D], ACT.Relu, scale=-1.0)
                cp(kc, B[1][:, 0:D], ACT.Relu)
                act.drain()
                cp(kb, ka, ACT.Exp, scale=-1.0)
                m = mask[:, bass.ds(t, 1)]
                cp(vbuf[:, :, 0:P], B[1][:, D:2 * D].rearrange("p (g n) -> p g n", g=KD), scale=m)
                cp(vbuf[:, 0, P:P + 1], m)
                cp(vbuf[:, 1, P:P + 1], m)
                act.drain()
                act.sem_inc(kvfm_ready, 1)

            def features_queries(t):
                when(act, tk_a, hq_ready, t + 1)
                cp(acc[:, bass.ds(t, 1), :].rearrange("p o d -> p (o d)"), B[2][:, 0:D])
                for g in range(KD):
                    last = cp(q_all[:, g, bass.ds(t * P, P)], B[2][:, D + g * P:D + (g + 1) * P], ACT.Identity,
                              bias=bqc[:, g:g + 1])
                last.then_inc(proj_out, 1)

            def project(t, s):
                normalize(t + 1, 1 - s)
                keys_values(t)
                transposed(t + 1, 1 - s)
                features_queries(t)

            normalize(0, 0)
            transposed(0, 0)
            for t in range(2):
                project(t, t)
            with act.Fori(1, NT // 2) as i:
                for s in range(2):
                    project(i * 2 + s, s)
            keys_values(NT - 1)
            features_queries(NT - 1)
            act.wait_ge(std_in, 2)
            cp(col[12][:, 0:NT], col[9][:, 0:NT], ACT.Sqrt).then_inc(std_out, 1)

            act.wait_ge(qweights, 1)

            def query_terms(t):
                qt = q_all[:, :, bass.ds(t * P, P)]
                g3 = lambda a: a.rearrange("p (g n) -> p g n", g=KD)
                when(act, tk_a, q_sum, t)
                cp(g3(q_neg), qt, ACT.Relu, scale=-1.0)
                cp(g3(q_pos_in), qt, ACT.Relu)
                act.drain()
                cp(q_exp, q_neg, ACT.Exp, scale=-1.0).then_inc(q_fm, 1)

            def indices(n, h):
                when(act, tk_a, seg, n * 8 - 8)
                act.copy(idx_s[h], dst_T[:, bass.ds(n * UNROLL, UNROLL)]).then_inc(idx_ready, 1)

            query_terms(0)
            act.wait_ge(unp_out, 1)
            indices(0, 0)
            indices(1, 1)
            with act.Fori(1, NT) as i:
                query_terms(i)
                for h in range(2):
                    indices(i * 2 + h, h)
            with act.Fori(NT, STEPS) as i:
                for h in range(2):
                    indices(i * 2 + h, h)
            act.wait_ge(b1_ps, 1)
            for e in range(E):
                for k in range(KD):
                    last = cp(w1_s[:, e, k, :], w1_s[:, e, k, :], scale=g_s[:, k, e:e + 1])
            last.then_inc(w1_scaled, 1)
            act.wait_ge(std_in, 3)
            cp(col[12][:, 0:NT], col[13][:, 0:NT], ACT.Sqrt).then_inc(std_out, 1)
            act.wait_ge(std_in, 4)
            cp(col[12][:, 0:NT], col[13][:, 0:NT], ACT.Sqrt).then_inc(std_out, 1)
            act.wait_ge(norm2_ready, 1)

            def normalize2(t, s):
                when(act, tk_a, x2T_ps, t - 1)
                xt = acc[:, bass.ds(t, 1), :].rearrange("p o d -> p (o d)")
                cp(x2[s], xt, ACT.Identity, scale=rstd[:, bass.ds(t, 1)], bias=nmr[:, bass.ds(t, 1)]).then_inc(x2_ready, 1)

            def logits_out(t, s):
                when(act, tk_a, logit_ps, t + 1)
                cp(BIG[:, bass.ds(t * E, E)], B[4 + s][:, 0:E]).then_inc(logit_out, 1)

            act.wait_ge(bias_out, 16)
            normalize2(0, 0)
            normalize2(1, 1)
            for t in range(2):
                normalize2(t + 2, t)
                logits_out(t, t)
            with act.Fori(1, NT // 2 - 1) as i:
                for s in range(2):
                    normalize2(i * 2 + s + 2, s)
                    logits_out(i * 2 + s, s)
            normalize2(NT - 1, 0)
            for t in range(NT - 3, NT):
                logits_out(t, t % 2)
            act.wait_ge(gap_ready, 1)
            cp(gate1, col[11][:, 0:NT], ACT.Exp).then_inc(gap_exp, 1)
            act.wait_ge(places_ready, 1)

            def dispatch(t, s):
                when(act, tk_a, disp[s], (t - s) * 8)
                xt = acc[:, bass.ds(t, 1), :].rearrange("p o d -> p (o d)")
                cp(xs2[s], xt, ACT.Identity, scale=rstd2[:, bass.ds(t, 1)], bias=nmr2[:, bass.ds(t, 1)])
                act.copy(place_s[s][:, 0:1], place0[:, bass.ds(t, 1)])
                act.copy(place_s[s][:, 1:2], place1[:, bass.ds(t, 1)]).then_inc(disp_ready, 1)

            tiles(act, dispatch, 4)
            for s in range(4):
                act.wait_ge(disp[s], 32 * ((NT + 3 - s) // 4))

            def expert(t, s):
                when(act, tk_a, hid_ps, t + 1)
                when(act, tk_a, hidT_ps, t * 2 - 2)
                for n in range(2):
                    last = cp(hid[s][:, 512 * n:512 * n + 512], B[2 * s + n][:, :], ACT.Gelu)
                last.then_inc(hid_ready, 1)

            expert(0, 0)
            expert(1, 1)
            with act.Fori(1, ST // 2) as i:
                expert(i * 2, 0)
                expert(i * 2 + 1, 1)
            expert(ST - 1, 0)

            def pairs(t, s):
                when(act, tk_a, pair_in[s], (t - s) * 8)
                when(act, tk_a, o_ready, t - 3)
                act.copy(pair_s[s][:, 0:1], place0[:, bass.ds(t, 1)])
                act.copy(pair_s[s][:, 1:2], place1[:, bass.ds(t, 1)]).then_inc(pair_ready, 1)

            act.wait_ge(pairs_ready, 1)
            act.wait_ge(y_sent[0], 16 * (ST // 2 + 1))
            act.wait_ge(y_sent[1], 16 * (ST // 2))
            tiles(act, pairs, 4)

        @block.tensor
        def _(pe):
            mm = nc.tensor.matmul
            pe.wait_ge(consts_ready, 2)
            pe.wait_ge(counts_ready, 1)
            mm(B[6][:, 0:NT + 1], tri, col[2], start=True, stop=True)
            mm(B[6][:, 64:64 + NT + 1], ones, col[2], start=True, stop=True).then_inc(prefix_ready, 1)
            pe.wait_ge(ctile_ready, 1)
            nc.tensor.transpose(B[6][0:CG, 128:256], col[10][:, 0:CG], ident).then_inc(ctile_T, 1)
            pe.wait_ge(weights_in, 96)
            zb = zeros.bitcast(BF16)
            mm(B[3][:, 0:P + 1], zeros[:, 0:P], zeros[:, 0:P + 1], start=True, stop=False)
            mm(B[4][:, 0:P + 1], zeros[:, 0:P], zeros[:, 0:P + 1], start=True, stop=False)
            mm(B[5][:, 0:NT], zb[:, 0:P], zb[:, 0:NT], start=True, stop=False)

            def transpose_x(t, s):
                when(pe, tk_t, xn_ready, t + 1)
                when(pe, tk_t, xnT_ready, t - 1)
                for k in range(KD):
                    last = nc.tensor.transpose(B[0][:, s * D + k * P:s * D + (k + 1) * P], xn[s][:, k * P:(k + 1) * P], ident)
                last.then_inc(t_ready, 1)

            def keys_values(t, s):
                when(pe, tk_t, xnT_ready, t + 1)
                when(pe, tk_t, kvfm_ready, t)
                mm(B[1][:, :], ones[0:1, :], bkv_row, start=True, stop=False)
                for k in range(KD):
                    last = mm(B[1][:, :], xnT[s][:, k, :], wkv_s[:, k, :], start=False, stop=k == KD - 1)
                last.then_inc(kv_ready, 1)

            def features_queries(t, s):
                when(pe, tk_t, proj_out, t)
                for k in range(KD):
                    mm(B[2][:, 0:D], xnT[s][:, k, :], gw_s[:, k, :], start=k == 0, stop=k == KD - 1)
                for g in range(KD):
                    for k in range(KD):
                        last = mm(B[2][:, D + g * P:D + (g + 1) * P], wq_s[:, k, g * P:(g + 1) * P], xnT[s][:, k, :],
                                  start=k == 0, stop=k == KD - 1)
                last.then_inc(hq_ready, 1)

            def sum_kv(t):
                when(pe, tk_t, kvfm_ready, t + 1)
                for g in range(KD):
                    for kk in (kb, kc):
                        last = mm(B[3 + g][:, 0:P + 1], kk[:, g * P:(g + 1) * P], vbuf[:, g, :], start=False, stop=False)
                last.then_inc(kv_done, 1)

            def project(t, s):
                keys_values(t, s)
                features_queries(t, s)
                if not isinstance(t, int) or t + 1 < NT:
                    transpose_x(t + 1, 1 - s)
                sum_kv(t)

            transpose_x(0, 0)
            tiles(pe, project)

            def histogram(t, s):
                when(pe, tk_t, oh_ready, t + 1)
                for b in range(HB):
                    last = mm(B[5][:, 0:NT], oh_lo[s][:, :, b], oh_hi[s][:, :, b], start=False, stop=False)
                last.then_inc(oh_free, 1)

            tiles(pe, histogram)
            mm(B[3][:, 0:P + 1], zeros[:, 0:P], zeros[:, 0:P + 1], start=False, stop=True)
            mm(B[4][:, 0:P + 1], zeros[:, 0:P], zeros[:, 0:P + 1], start=False, stop=True)
            mm(B[5][:, 0:NT], zb[:, 0:P], zb[:, 0:NT], start=False, stop=True).then_inc(sums_done, 1)
            pe.wait_ge(kvbd_ready, 1)
            for g in range(KD):
                last = nc.tensor.transpose(B[0][:, g * P:(g + 1) * P], kv_bd[:, g, :], ident)
            last.then_inc(kvT_ps, 1)
            pe.wait_ge(kvT_ready, 1)
            pe.wait_ge(wo_in, 16)
            for g in range(KD):
                last = mm(B[1][:, g * D:(g + 1) * D], kvT[:, g, :], wo_s[:, g, :], start=True, stop=True)
            last.then_inc(kvo_ps, 1)
            pe.wait_ge(qweights, 1)

            pe.wait_ge(unpacked, 1)
            for k in range(4):
                f = (dst_f, lo_f)[k // 2]
                for j in range(4):
                    c = (k % 2) * 4 + j
                    last = nc.tensor.transpose(B[k][:, j * P:(j + 1) * P], f[:, c * P:(c + 1) * P], ident)
                last.then_inc(unp_T, 1)
            pe.wait_ge(unp_out, 1)

            def normalizers(t):
                when(pe, tk_t, q_sum, t + 1)
                for g in range(KD):
                    last = mm(B[4][:, g * P:(g + 1) * P], ks_out[:, g, :], q_pos[:, g * P:(g + 1) * P], start=True, stop=True)
                last.then_inc(q_norm, 1)

            def mix(t):
                when(pe, tk_t, q_scaled, t + 1)
                when(pe, tk_t, q_added, t)
                mm(B[7][:, 0:D], ones[0:1, :], bo_row, start=True, stop=False)
                for g in range(KD):
                    last = mm(B[7][:, 0:D], q_sc[:, g * P:(g + 1) * P], kv_out[:, g, :], start=False, stop=g == KD - 1)
                last.then_inc(q_mixed, 1)

            def sum_chunks(n, h):
                when(pe, tk_t, gath[h], (n - h) * 64 + 16 * UNROLL)
                when(pe, tk_t, onehot_ready, n + 1)
                when(pe, tk_t, added, n)
                for u in range(UNROLL):
                    mm(B[u // 2][:, (u % 2) * D:(u % 2 + 1) * D], OH[h][:, u, :], G[h][:, u, :],
                       start=True, stop=True).then_inc(seg, 1)

            def attend_and_sum(i):
                sum_chunks(i * 2, 0)
                normalizers(i)
                sum_chunks(i * 2 + 1, 1)
                mix(i)

            attend_and_sum(0)
            with pe.Fori(1, NT) as i:
                attend_and_sum(i)
            with pe.Fori(NT, STEPS) as i:
                for h in range(2):
                    sum_chunks(i * 2 + h, h)
            pe.wait_ge(b_one_ready, 1)
            pe.wait_ge(w1_in, 16)
            for n in range(2):
                for e in range(E):
                    for k in range(KD):
                        last = mm(B[6 + n][0:E, :], b_one[:, k, e, :], w1_s[:, e, k, n * 512:(n + 1) * 512],
                                  start=e == 0 and k == 0, stop=e == E - 1 and k == KD - 1)
            last.then_inc(b1_ps, 1)
            pe.wait_ge(router_in, 32)

            def transpose_x2(t, s):
                when(pe, tk_t, x2_ready, t + 1)
                when(pe, tk_t, x2T_ready, t - 1)
                for k in range(KD):
                    last = nc.tensor.transpose(B[s][:, k * P:(k + 1) * P], x2[s][:, k * P:(k + 1) * P], ident)
                last.then_inc(x2T_ps, 1)

            def route(t, s):
                if not isinstance(t, int) or t + 1 < NT:
                    transpose_x2(t + 1, 1 - s)
                when(pe, tk_t, x2T_ready, t + 1)
                when(pe, tk_t, logit_out, t - 1)
                for k in range(KD):
                    last = mm(B[4 + s][:, 0:E], x2T[s][:, k, :], wr_s[:, k, :], start=k == 0, stop=k == KD - 1)
                last.then_inc(logit_ps, 1)

            transpose_x2(0, 0)
            tiles(pe, route)
            pe.wait_ge(pick_ready, 1)
            flat = both.rearrange("p t e -> p (t e)")
            mm(B[2][:, 0:NE], tri, flat, start=True, stop=True)
            mm(B[3][:, 0:NE], ones, flat, start=True, stop=True).then_inc(ranks_ps, 1)
            pe.wait_ge(slot_e_in, 16)
            pe.wait_ge(ones3_ready, 1)
            pe.wait_ge(w1_scaled, 1)
            pe.wait_ge(w2_in, 16)
            pe.wait_ge(bias_out, 16)

            def expert_of(t):
                return nc.tensor.value_load(expert_row[0:1, bass.ds(t, 1)], min_val=0, max_val=E - 1)

            def inputs(t, s):
                when(pe, tk_t, xs_in[s], (t - s) * 16 + 32)
                when(pe, tk_t, xsT_ready, t - 1)
                for k in range(KD):
                    last = nc.tensor.transpose(B[6][:, s * D + k * P:s * D + (k + 1) * P], x_in[s][:, k * P:(k + 1) * P], ident)
                last.then_inc(xsT_ps, 1)

            def first_product(t, s):
                e = expert_of(t)
                when(pe, tk_t, xsT_ready, t + 1)
                when(pe, tk_t, hid_ready, t - 1)
                for n in range(2):
                    mm(B[2 * s + n][:, :], ones3, hid_bias[s][:, 512 * n:512 * n + 512], start=True, stop=False)
                    for k in range(KD):
                        last = mm(B[2 * s + n][:, :], x_inT[s][:, k, :],
                                  W1A[:, bass.ds(e * (KD * H) + k * H + n * 512, 512)], start=False, stop=k == KD - 1)
                last.then_inc(hid_ps, 1)

            def hidden(t, s):
                when(pe, tk_t, hid_ready, t + 1)
                when(pe, tk_t, hidT_ready, t * 2)
                for g in range(2):
                    for c in range(4):
                        last = nc.tensor.transpose(B[4 + g][:, c * P:(c + 1) * P],
                                                   hid[s][:, (4 * g + c) * P:(4 * g + c + 1) * P], ident)
                    last.then_inc(hidT_ps, 1)

            def second_product(t, s):
                e = expert_of(t)
                when(pe, tk_t, y_ready, t)
                when(pe, tk_t, y_bias_in[s], (t - s) * 8 + 16)
                mm(B[7][:, 0:D], ones3, y_bias[s], start=True, stop=False)
                for g in range(2):
                    when(pe, tk_t, hidT_ready, t * 2 + g + 1)
                    for c in range(4):
                        k = 4 * g + c
                        last = mm(B[7][:, 0:D], hidT[:, k, :], W2A[:, bass.ds(e * (KH * D) + k * D, D)],
                                  start=False, stop=k == KH - 1)
                last.then_inc(y_ps, 1)

            def step(t, s):
                hidden(t, s)
                if not isinstance(t, int) or t + 1 < ST:
                    first_product(t + 1, 1 - s)
                if not isinstance(t, int) or t + 2 < ST:
                    inputs(t + 2, s)
                second_product(t, s)

            inputs(0, 0)
            first_product(0, 0)
            inputs(1, 1)
            step(0, 0)
            with pe.Fori(0, ST // 2 - 1) as i:
                step(i * 2 + 1, 1)
                step(i * 2 + 2, 0)
            for t in range(ST - 2, ST):
                step(t, t % 2)


def kernel(x, src, dst, L0_gnn_W, L0_mix_wq, L0_mix_bq, L0_mix_wk, L0_mix_bk, L0_mix_wv, L0_mix_bv, L0_mix_wo,
           L0_mix_bo, L0_ffn_Wr, L0_ffn_br, L0_ffn_ln_g, L0_ffn_ln_b, L0_ffn_W1, L0_ffn_b1, L0_ffn_W2, L0_ffn_b2):
    import numpy as np
    import concourse.bacc as bacc
    from concourse.bass_utils import run_bass_kernel_spmd

    src, dst = np.asarray(src), np.asarray(dst)
    n = P * FULL
    arrays = {
        "x": x, "src": src[:n].reshape(P, FULL), "dst": dst[:n].reshape(P, FULL),
        "src_rest": src[n:].reshape(REST, 1), "dst_rest": dst[n:].reshape(REST, 1),
        "gnn_w": L0_gnn_W, "wq": L0_mix_wq, "bq": np.asarray(L0_mix_bq).reshape(KD, P).T,
        "wkv": np.concatenate([np.asarray(L0_mix_wk), np.asarray(L0_mix_wv)], axis=1),
        "bkv": np.concatenate([np.asarray(L0_mix_bk), np.asarray(L0_mix_bv)]).reshape(1, 2 * D),
        "wo": L0_mix_wo, "bo": np.asarray(L0_mix_bo).reshape(1, D), "wr": L0_ffn_Wr,
        "br": np.asarray(L0_ffn_br).reshape(1, E), "ln_gT": np.asarray(L0_ffn_ln_g).T, "ln_bT": np.asarray(L0_ffn_ln_b).T,
        "w1": L0_ffn_W1, "b1": L0_ffn_b1, "w2": L0_ffn_W2, "b2": L0_ffn_b2,
    }
    arrays = {"in_" + k: np.ascontiguousarray(a) for k, a in arrays.items()}
    nc = bacc.Bacc("TRN2", target_bir_lowering=False, num_devices=1)
    args = [nc.dram_tensor(k, a.shape, mybir.dt.from_np(a.dtype), kind="ExternalInput").ap() for k, a in arrays.items()]
    out = nc.dram_tensor("out_dram", (N_NODES, D), F32, kind="ExternalOutput").ap()
    gps_layer(nc, *args, out)
    r = run_bass_kernel_spmd(nc, [arrays], core_ids=[0])
    return r.results[0]["out_dram"]
```

```python
import concourse.bass as bass
from concourse import mybir
from contextlib import ExitStack

F32, BF16, I32, I16 = mybir.dt.float32, mybir.dt.bfloat16, mybir.dt.int32, mybir.dt.int16
ALU = mybir.AluOpType
ACT = mybir.ActivationFunctionType
AX = mybir.AxisListType

P = 128
N_NODES = 6250
D = 256
KD = D // P
NT = -(-N_NODES // P)
LAST = N_NODES - (NT - 1) * P
N_EDGES = 100000
DEPTH = 32
LN_EPS = 1e-5

EC = 784
FULL = N_EDGES // P
REST = N_EDGES - FULL * P
TPARTS, TPART = 7, NT // 7
HB = EC // NT
ROW = 2
SORTN = 840
GSTEPS = 7
NG = SORTN // (8 * GSTEPS)
GV = 8 * GSTEPS
GR = GV // ROW
RPC = P // ROW
CODE = 13
MASK = (1 << 2 * CODE) - 1
FLAG = 0x40000000
PAD = NT * P
UNROLL = 4
BATCHES = 4
ROWS_MAX = (N_EDGES + (ROW - 1) * NT * P) // ROW
CHUNKS_MAX = (ROWS_MAX + (RPC - 1) * NT) // RPC
STEPS = -(-CHUNKS_MAX // (BATCHES * UNROLL))
CHUNKS = STEPS * BATCHES * UNROLL
CG = 8
CPAD = CG * P

E = 8
TOPK = 2
H = 1024
KH = H // P
ST = (N_NODES * TOPK - E) // P + E
SLOTS = ST * P
OPARTS = [slice(a, b) for a, b in zip((0, 3, 8, 15, 22, 29, 36, 42, 46), (3, 8, 15, 22, 29, 36, 42, 46, NT))]
RG = 7
RSLOT = [u % 4 for u in range(RG)]
RLAG = [next(k for k in range(1, RG + 1) if RSLOT[u - k] == RSLOT[u]) for u in range(RG)]
PICKS = TOPK * NT
PC = 14

assert EC % NT == 0 and SORTN % (8 * GSTEPS) == 0 and NT % 4 == 1 and ST % 2 == 1
CT_DVE = 28
HG = 4
assert NG == 15 and NT == 12 * HG + 1 and HG % 2 == 0 and GSTEPS >= 2 * HG - 1
assert SORTN >= EC + NT * (ROW - 1) and CPAD * RPC >= SORTN // ROW * P + (NT + 1) * (RPC - 1)
assert NT % RG == 0 and STEPS >= NT + 2 + 2 * E // BATCHES and min(RLAG) >= 3
assert PICKS % PC == 0 and PC % 2 == 0 and (PICKS // PC) % 2 == 1 and ST % 4 == 1
assert NT * D < 1 << 15 and NT < STEPS and CHUNKS_MAX <= CHUNKS <= CPAD and PAD < 1 << CODE


class Chain:

    def __init__(self, eng, sem):
        self.eng, self.sem, self.count = eng, sem, 0

    def add(self, ins):
        self.count += 1
        return ins.then_inc(self.sem, 1)

    def sync(self):
        self.eng.wait_ge(self.sem, self.count)

    def link(self, ins):
        self.add(ins)
        self.sync()


def when(eng, tick, sem, value):
    if not isinstance(value, int):
        eng.wait_ge(sem, value)
        eng.sem_inc(tick, 1)
    elif value > 0:
        eng.wait_ge(sem, value)


def tiles(eng, body, slots=2):
    for t in range(slots):
        body(t, t)
    with eng.Fori(1, NT // slots) as i:
        for s in range(slots):
            body(i * slots + s, s)
    for t in range(NT // slots * slots, NT):
        body(t, t % slots)


def gps_layer(nc, x, src, dst, src_rest, dst_rest, gnn_w, wq, bq, wkv, bkv, wo, bo,
              wr, br, ln_gT, ln_bT, w1, b1, w2, b2, out):
    ctx = ExitStack()
    with ctx:
        def sb(name, words, dt=F32):
            return ctx.enter_context(nc.sbuf_tensor(name, [P, words], dt))

        def sem(name):
            return ctx.enter_context(nc.semaphore(name))

        def dram(name, shape, dt):
            return nc.dram_tensor(name, shape, dt, kind="Internal").ap()

        table = dram("table", [NT * P, D], F32)
        edge_rows = dram("edge_rows", [CPAD * RPC, ROW], I32)
        chunk_tiles = dram("chunk_tiles", [CPAD], I16)
        token_x = dram("token_x", [NT * P, D], F32)
        pick_y = dram("pick_y", [PICKS * P + 2 * P, D], F32)
        bias_rows = dram("bias_rows", [E, 3, D], BF16)
        slot_experts = dram("slot_experts", [P], I32)

        W1A = sb("W1A", E * KD * H)
        W2A = sb("W2A", E * KH * D)
        ACC = sb("ACC", (NT + 1) * D)
        CONST = sb("CONST", 4 * P)
        SMALL = sb("SMALL", 27 * 50)
        BIG = sb("BIG", 5650)
        S1, S2 = KD * NT * P, NT * D

        def piece(area, at, n, dt=F32):
            words = n if dt in (F32, I32) else (n + 1) // 2
            ap = area[:, at:at + words]
            return ap if dt == F32 else ap.bitcast(dt)

        def grid(area, at, a, b, dt=F32):
            return piece(area, at, a * b, dt).rearrange("p (a b) -> p a b", b=b)

        ident, iota, tri, ones = (CONST[:, k * P:(k + 1) * P] for k in range(4))
        acc = grid(ACC, 0, NT + 1, D)

        def small(k, n=NT, dt=F32):
            return piece(SMALL, 50 * k, n, dt)

        rstd, nmr, mask, dinv, junk = (small(k) for k in range(5))
        gate0, gate1 = small(5), small(6)
        bqc, pcol = small(9, KD), piece(SMALL, 452, 1)
        g_s, b_s = grid(SMALL, 454, KD, E), grid(SMALL, 470, KD, E)
        col = [small(k, 50) for k in range(10, 24)]
        rstd2a, rstd2, nmr2 = (small(k) for k in range(24, 27))

        q_all = grid(W1A, 0, KD, NT * P)
        xr = grid(W2A, 0, NT, D)
        oh_lo = [grid(W1A, S1 + s * 1416, P, HB, BF16) for s in range(2)]
        oh_hi = [grid(W1A, S1 + s * 1416 + HB * P // 2, NT, HB, BF16) for s in range(2)]
        digits = grid(W2A, S2 + 1400, P, HB, BF16)
        bkv_row = W1A[0:1, S1 + 2832:S1 + 2832 + 2 * D]
        bo_row = W1A[0:1, S1 + 3344:S1 + 3344 + D]
        wkv_s, gw_s, wq_s = grid(BIG, 0, KD, 2 * D), grid(BIG, 1024, KD, D), grid(BIG, 1536, KD, D)
        xn = [piece(BIG, 2048 + 256 * s, D) for s in range(2)]
        xnT = [grid(BIG, 2560 + 256 * s, KD, P) for s in range(2)]
        ka, kb, kc = (piece(BIG, 3072 + 256 * k, D) for k in range(3))
        vbuf = grid(BIG, 3840, KD, P + 1)
        srcI, dstI, packed = (piece(W2A, S2 + k * EC, EC, I32) for k in range(3))
        tile_of, lo_of, hi_of = (piece(W2A, S2 + 3 * EC + k * EC // 2, EC, BF16) for k in range(3))
        lookup = grid(W2A, S2, GR, NT + 1)
        tile_cmp = grid(W2A, S2 + 1000, CG, NT)
        signs, sign_bias = piece(BIG, 3000, NT - CT_DVE + 1), piece(BIG, 3040, NT - CT_DVE + 1)
        sign_scratch = [piece(BIG, 3100 + 400 * s, EC, BF16) for s in range(2)]
        eq_scratch = [piece(BIG, 2048 + 400 * s, EC, BF16) for s in range(2)]
        stats_x = grid(BIG, 3072, NT, 6)
        zeros = W2A[:, S2 + 3528:S2 + 3528 + D]
        work = piece(BIG, 4098, SORTN)
        workI = piece(BIG, 4098, SORTN, I32)
        sorted_g, sorted_i = piece(BIG, 4940, GV), piece(BIG, 4940, GV, I32)
        stage_raw = [piece(BIG, 5000 + 60 * s, GV, I32) for s in range(2)]
        row_at = [piece(BIG, 5120 + 30 * s, GR, I32) for s in range(2)]
        row_tileI, row_tile, row_k, row_sum = piece(BIG, 5180, GR, I32), *(piece(BIG, 5210 + 30 * k, GR) for k in range(3))
        NF = SORTN - EC
        fill, fill_flat, fillI = grid(BIG, 5300, NT, ROW - 1), piece(BIG, 5300, NF), piece(BIG, 5360, NF, I32)
        CT_row = BIG[0:CG, 5584:5584 + P // 2].bitcast(I16)
        head_mask, wo_s = piece(W1A, S1, P), grid(W1A, S1 + P, KD, D)
        NH = P // DEPTH
        kv_ext = grid(W1A, S1 + 640, KD, P + NH)
        ksum = piece(W1A, S1 + 1152, KD)
        q_neg, q_exp, q_relu = (piece(W1A, S1 + 1200 + 256 * k, D) for k in range(3))
        mixed, mixedT = piece(W1A, S1 + 1968, D), grid(W1A, S1 + 2224, KD, P)
        q_den = piece(W1A, S1 + 2480, KD * NH)

        raw, src_u, dst_u, same = (piece(BIG, 1024 * k, CPAD, I32) for k in range(4))
        raw3 = grid(BIG, 0, CG, P, I32)
        lo_f, dst_f, same_f = piece(BIG, 1024, CPAD), piece(BIG, 2048, CPAD), piece(BIG, 3072, CPAD)
        G = [grid(BIG, UNROLL * D * s, UNROLL, D) for s in range(BATCHES)]
        dst_T, lo_neg = piece(W2A, S2, CHUNKS, I32), piece(W2A, S2 + CHUNKS, CHUNKS)
        OH = [grid(area, at + UNROLL * P * s, UNROLL, P) for area, at in ((BIG, 4098), (W2A, S2 + 2 * CHUNKS)) for s in range(2)]
        tile_row = W2A[0:1, S2 + 2976:S2 + 2976 + CPAD // 2].bitcast(I16)
        idx_s = [piece(W2A, S2 + 3784 + UNROLL * s, UNROLL, I32) for s in range(BATCHES)]

        NE = NT * E
        logits, pick0, pick1, both = (grid(BIG, NE * k, NT, E) for k in range(4))
        tmp, rank, totals, runs = (grid(BIG, NE * k, NT, E) for k in range(4, 8))
        x2 = [piece(BIG, 3136 + 256 * s, D) for s in range(4)]
        x2T = [grid(BIG, NE * 4 + 256 * s, KD, P) for s in range(4)]
        wr_s, br_s = grid(BIG, 5448, KD, E), piece(BIG, 5464, E)
        stats2 = grid(BIG, 5150, NT, 6)
        expert_m8 = grid(BIG, 4192, NT, E)
        exp_tot, exp_tiles, exp_base, slot_e, exp_i = (piece(BIG, 4592 + 16 * k, E) for k in range(5))
        expI = piece(BIG, 4680, E, I32)
        xs2 = [piece(BIG, NE + 256 * s, D) for s in range(4)]
        pc_digits = grid(BIG, 0, P, PC, BF16)
        pc_at = [grid(BIG, 896 * (1 + s), P, PC, BF16) for s in range(2)]
        pc_tile = grid(BIG, 2688, ST, PC, BF16)
        pc_tokens = grid(BIG, 3424, 2 * ST, PC, BF16)
        slotI, digitI = piece(BIG, 4900, PICKS, I32), piece(BIG, 5000, PICKS, I32)
        slot_at, slot_tile, pick_col = (piece(BIG, 5100 + 50 * k, PICKS, BF16) for k in range(3))
        row_1, dump_row = piece(BIG, 5250, 1), piece(BIG, 5251, 1)
        zero_row = BIG[0:1, 5260:5260 + ST].bitcast(BF16)
        row_f, tok_f, unused, unused_at, parity = (piece(BIG, 2688 + 110 * k, ST) for k in range(5))
        slot_token, x_idx = piece(SMALL, 700, ST, I32), [piece(SMALL, 810 + s, 1, I32) for s in range(4)]
        slot_row, y_idx = piece(SMALL, 0, ST, I32), [piece(SMALL, 814 + s, 1, I32) for s in range(4)]
        slot_eI = piece(BIG, 4690, 1, I32)
        b_one_flat = piece(BIG, 5122, KD * E * E)
        b_one = b_one_flat.rearrange("p (k e m) -> p k e m", k=KD, e=E)
        b1_rows = [BIG[0:E, at:at + H // 2] for at in (2592, 4544)]
        bias_f, bias_r = BIG[0:E, 4160:4160 + D], BIG[0:E, 4160 + D:4160 + 2 * D]
        bias_b = BIG[0:E, 4160 + 2 * D:4160 + 2 * D + 3 * D // 2].bitcast(BF16).rearrange("e (s n) -> e s n", s=3)
        hid_bias, b1_s = piece(SMALL, 500, E * KH), piece(SMALL, 600, E * KH)
        w1_s = W1A[:, :].rearrange("p (e k n) -> p e k n", e=E, k=KD)
        x_in = [piece(area, at + 256 * s, D) for area, at in ((BIG, 0), (SMALL, 820)) for s in range(2)]
        x_inT = [grid(BIG, 512 + 256 * s, KD, P) for s in range(2)]
        w1_now = grid(BIG, 1024, KD, H)
        hidT = [grid(BIG, 3072 + H * s, KH, P) for s in range(2)]
        y_out = [piece(BIG, 5120, D), piece(ACC, NT * D, D)]
        y_bias = [BIG[0:3, 5376 + D // 2 * s:5376 + D // 2 * (s + 1)].bitcast(BF16) for s in range(2)]
        ones3 = iota[0:3, 0:64].bitcast(BF16)
        expert_row = tri[0:1, 0:P].bitcast(I32)
        y_first, y_second = grid(W1A, 0, NT, D), grid(W2A, 0, NT, D)

        B = [ctx.enter_context(nc.psum_tensor(f"B{k}", [P, 512], F32)) for k in range(8)]

        tk_v, tk_a, tk_t, tk_g, tk_s = (sem(n) for n in ("tk_v", "tk_a", "tk_t", "tk_g", "tk_s"))
        dve_steps, act_steps, pool_steps = sem("dve_steps"), sem("act_steps"), sem("pool_steps")
        consts_ready = sem("consts_ready")
        pads_set = sem("pads_set")
        edges_in, x_in_s, weights_in = sem("edges_in"), sem("x_in"), sem("weights_in")
        cleared_edges = sem("cleared_edges")
        tile_of_ready, signs_ready = sem("tile_of_ready"), sem("signs_ready")
        counts_ready, prefix_ready = sem("counts_ready"), sem("prefix_ready")
        ctile_ready, ctile_T, ctile_row, ctile_out = sem("ctile_ready"), sem("ctile_T"), sem("ctile_row"), sem("ctile_out")
        tile_row_in = sem("tile_row_in")
        bn_done = sem("bn_done")
        oh_ready, oh_free = sem("oh_ready"), sem("oh_free")
        std_in, std_out = sem("std_in"), sem("std_out")
        norm_ready = sem("norm_ready")
        xn_ready, t_ready, xnT_ready = sem("xn_ready"), sem("t_ready"), sem("xnT_ready")
        kv_ready, hq_ready, kvfm_ready, kv_done, proj_out = (
            sem("kv_ready"), sem("hq_ready"), sem("kvfm_ready"), sem("kv_done"), sem("proj_out"))
        sums_done = sem("sums_done")
        stage_ready, scat = sem("stage_ready"), [sem("scat0"), sem("scat1")]
        table_ready, table_out = sem("table_ready"), sem("table_out")
        wo_in, kvbd_ready = sem("wo_in"), sem("kvbd_ready")
        q_terms, q_ps, q_mixed, q_mixedT_ps, q_mixedT, q_out, q_added = (
            sem("q_terms"), sem("q_ps"), sem("q_mixed"), sem("q_mixedT_ps"), sem("q_mixedT"), sem("q_out"), sem("q_added"))
        raw_in, unpacked, unp_T, unp_out = sem("raw_in"), sem("unpacked"), sem("unp_T"), sem("unp_out")
        idx_ready, gath, onehot_ready, seg, added = (
            sem("idx_ready"), [[sem(f"gath{s}_{k}") for k in range(UNROLL // 2)] for s in range(BATCHES)], sem("onehot_ready"), sem("seg"), sem("added"))
        w1_in, w2_in, lnb_in, w1_now_ready, b1_ps, bias_in, bias_ready, bias_out = (
            [sem(f"w1_in{e}") for e in range(E)], sem("w2_in"), sem("lnb_in"), sem("w1_now_ready"), sem("b1_ps"), sem("bias_in"),
            sem("bias_ready"), sem("bias_out"))
        w1_scaled = sem("w1_scaled")
        x_done = sem("x_done")
        router_in, norm2_ready = sem("router_in"), sem("norm2_ready")
        x2_ready, x2T_ps, x2T_even, x2T_odd, logit_ps = (
            sem("x2_ready"), sem("x2T_ps"), sem("x2T_even"), sem("x2T_odd"), sem("logit_ps"))
        b_one_ready, b1_rows_ready, b1T_ps = sem("b_one_ready"), sem("b1_rows_ready"), sem("b1T_ps")
        pick_ready, gap_ready, gap_exp, ranks_ps, places_ready = (
            sem("pick_ready"), sem("gap_ready"), sem("gap_exp"), sem("ranks_ps"), sem("places_ready"))
        slot_e_ready, slot_e_out, slot_e_in = sem("slot_e_ready"), sem("slot_e_out"), sem("slot_e_in")
        xs_ready, xs_out = sem("xs_ready"), [sem(f"xs_out{s}") for s in range(4)]
        pc_ready, pc_used, tokens_ps, slots_ready, zero_ready = sem("pc_ready"), sem("pc_used"), sem("tokens_ps"), sem("slots_ready"), sem("zero_ready")
        ones3_ready = sem("ones3_ready")
        x_idx_ready = sem("x_idx_ready")
        xs_in, xsT_ps, xsT_ready = [sem(f"xs_in{s}") for s in range(4)], sem("xsT_ps"), sem("xsT_ready")
        y_bias_in = [sem("y_bias_in0"), sem("y_bias_in1")]
        hid_ps, hid_ready = sem("hid_ps"), sem("hid_ready")
        y_ps, y_ready, y_sent = sem("y_ps"), sem("y_ready"), [sem("y_sent0"), sem("y_sent1")]
        y_idx_ready, picks_in, o_ready, o_sent = (
            sem("y_idx_ready"), [sem(f"picks_in{k}") for k in range(len(OPARTS))], sem("o_ready"), sem("o_sent"))

        block = ctx.enter_context(nc.Block())

        @block.sync
        def _(sp):
            sp.dma_start(srcI[:, 0:FULL], src).then_inc(edges_in, 16)
            sp.dma_start(dstI[:, 0:FULL], dst).then_inc(edges_in, 16)
            sp.wait_ge(pads_set, 1)
            with nc.allow_non_contiguous_dma(reason="one edge per partition"):
                sp.dma_start(srcI[0:REST, FULL:FULL + 1], src_rest).then_inc(edges_in, 16)
                sp.dma_start(dstI[0:REST, FULL:FULL + 1], dst_rest).then_inc(edges_in, 16)
            sp.dma_start(xr[:, 0:NT - 1, :], x[0:(NT - 1) * P, :].rearrange("(t p) d -> p t d", p=P)).then_inc(x_in_s, 16)
            sp.dma_start(xr[0:LAST, NT - 1, :], x[(NT - 1) * P:N_NODES, :]).then_inc(x_in_s, 16)
            sp.dma_start(wkv_s, wkv.rearrange("(k p) n -> p k n", p=P)).then_inc(weights_in, 16)
            sp.dma_start(gw_s, gnn_w.rearrange("(k p) n -> p k n", p=P)).then_inc(weights_in, 16)
            sp.dma_start(wq_s, wq.rearrange("(k p) n -> p k n", p=P)).then_inc(weights_in, 16)
            sp.dma_start(bqc, bq).then_inc(weights_in, 16)
            sp.dma_start(bkv_row, bkv).then_inc(weights_in, 16)
            sp.dma_start(bo_row, bo).then_inc(weights_in, 16)
            sp.wait_ge(consts_ready, 1)
            sp.dma_start(edge_rows.rearrange("(p a) r -> p (a r)", p=P).rearrange("p (m z) -> p m z", z=D),
                         zeros.bitcast(I32).rearrange("p (m z) -> p m z", m=1).to_broadcast([P, CPAD * P // P // D, D])
                         ).then_inc(cleared_edges, 16)
            sp.wait_ge(ctile_row, 1)
            sp.dma_start(chunk_tiles.rearrange("(j p) -> j p", p=P), CT_row).then_inc(ctile_out, 16)
            for k in range(TPARTS):
                sp.wait_ge(table_ready, k + 1)
                ts_ = slice(k * TPART, (k + 1) * TPART)
                sp.dma_start(table.rearrange("(t p) d -> p t d", p=P)[:, ts_, :], acc[:, ts_, :]).then_inc(table_out, 16)
            sp.dma_start(wo_s, wo.rearrange("(k p) n -> p k n", p=P)).then_inc(wo_in, 16)
            for s in range(2):
                sp.wait_ge(scat[s], 16 * GR * ((NG + 1 - s) // 2))
            sp.wait_ge(kv_done, NT)
            sp.wait_ge(ctile_out, 16)
            sp.dma_start(raw3, edge_rows.rearrange("(j p a) r -> p j (a r)", p=P, a=RPC)).then_inc(raw_in, 16)
            sp.dma_start(tile_row, chunk_tiles.rearrange("(o n) -> o n", o=1)).then_inc(tile_row_in, 16)
            sp.wait_ge(q_added, NT)
            sp.dma_start(g_s, ln_gT.rearrange("(k p) e -> p k e", p=P)).then_inc(lnb_in, 16)
            sp.dma_start(b_s, ln_bT.rearrange("(k p) e -> p k e", p=P)).then_inc(lnb_in, 16)
            sp.dma_start(b1_s, b1).then_inc(lnb_in, 16)
            for e in range(E):
                if e:
                    sp.wait_ge(seg, (NT * BATCHES + 2 * e) * UNROLL)
                sp.dma_start(w1_s[:, e], w1.rearrange("e (k p) n -> p e k n", p=P)[:, e]).then_inc(w1_in[e], 16)
            sp.wait_ge(cleared_edges, 16)
            sp.wait_ge(added, BATCHES * STEPS)
            sp.dma_start(bias_f, b2).then_inc(bias_in, 16)
            sp.dma_start(wr_s, wr.rearrange("(k p) e -> p k e", p=P)).then_inc(router_in, 16)
            sp.dma_start(br_s, br.to_broadcast([P, E])).then_inc(router_in, 16)

            def store_group(g):
                for u in range(RG):
                    t, r = g * RG + u, RSLOT[u]
                    when(sp, tk_s, xs_ready, t + 1)
                    sp.dma_start(token_x[bass.ds(t * P, P), :], xs2[r]).then_inc(xs_out[r], 16)

            with sp.Fori(0, NT // RG) as g:
                store_group(g)
            sp.wait_ge(bias_ready, 1)
            sp.dma_start(bias_rows, bias_b).then_inc(bias_out, 16)
            sp.wait_ge(x_done, 1)
            sp.dma_start(W2A[:, :].rearrange("p (e c n) -> p e c n", e=E, c=KH),
                         w2.rearrange("e (c p) n -> p e c n", p=P)).then_inc(w2_in, 16)
            sp.wait_ge(slot_e_ready, 1)
            with nc.allow_non_contiguous_dma(reason="one expert number per partition"):
                sp.dma_start(slot_experts.rearrange("(p o) -> p o", o=1), slot_eI).then_inc(slot_e_out, 16)
            sp.wait_ge(slot_e_out, 16)
            sp.dma_start(expert_row, slot_experts.rearrange("(o p) -> o p", o=1)).then_inc(slot_e_in, 16)
            sp.wait_ge(slot_e_in, 16)

            def expert_of(t):
                return nc.sync.value_load(expert_row[0:1, bass.ds(t, 1)], min_val=0, max_val=E - 1)

            def load_y_bias(t, s):
                e = expert_of(t)
                when(sp, tk_s, y_ps, t - 1)
                sp.dma_start(y_bias[s], bias_rows[bass.ds(e, 1), :, :].rearrange("o s n -> (o s) n")).then_inc(y_bias_in[s], 16)

            for t in range(2):
                load_y_bias(t, t)
            with sp.Fori(0, (ST - 3) // 2) as i:
                for u in range(2):
                    load_y_bias(i * 2 + u + 2, u)
            load_y_bias(ST - 1, 0)
            sp.wait_ge(y_sent[0], 16 * (ST // 2 + 1))
            sp.wait_ge(y_sent[1], 16 * (ST // 2))

            def by_tile(rows, first, tiles_):
                a, b = tiles_.start, min(tiles_.stop, NT - 1)
                parts = [(slice(0, P), slice(a, b), rows[first + a * P:first + b * P, :])]
                if tiles_.stop == NT:
                    parts.append((slice(0, LAST), slice(b, NT), rows[first + b * P:first + b * P + LAST, :]))
                return parts

            for k, part in enumerate(OPARTS):
                for first, y in ((0, y_first), (NT * P, y_second)):
                    for p, t, rows in by_tile(pick_y, first, part):
                        sp.dma_start(y[p, t, :], rows.rearrange("(t p) d -> p t d", t=t.stop - t.start)).then_inc(picks_in[k], 16)
            for k, part in enumerate(OPARTS):
                sp.wait_ge(o_ready, k + 1)
                for p, t, rows in by_tile(out, 0, part):
                    sp.dma_start(rows.rearrange("(t p) d -> p t d", t=t.stop - t.start), y_first[p, t, :]).then_inc(o_sent, 16)
            sp.wait_ge(o_sent, 16 * (len(OPARTS) + 1))

        @block.gpsimd
        def _(pool):
            ch = Chain(pool, pool_steps)
            ch.add(pool.memset(zeros, 0.0))
            ch.sync()
            pool.sem_inc(consts_ready, 1)
            ch.add(pool.memset(ident, 0.0))
            ch.add(pool.memset(tri, 1.0))
            ch.add(pool.memset(ones, 1.0))
            ch.add(pool.memset(mask, 1.0))
            ch.add(pool.iota(iota, pattern=[[1, P]], base=0, channel_multiplier=0, allow_small_or_imprecise_dtypes=True))
            ch.add(pool.iota(pcol, pattern=[[0, 1]], base=0, channel_multiplier=1, allow_small_or_imprecise_dtypes=True))
            ch.add(pool.iota(junk, pattern=[[0, NT]], base=SLOTS, channel_multiplier=1, allow_small_or_imprecise_dtypes=True))
            ch.sync()
            ch.add(pool.affine_select(out=ident, in_=ident, compare_op=ALU.not_equal, fill=1.0, base=0,
                                      pattern=[[-1, P]], channel_multiplier=1))
            ch.add(pool.affine_select(out=tri, in_=tri, compare_op=ALU.is_gt, fill=0.0, base=0,
                                      pattern=[[1, P]], channel_multiplier=-1))
            ch.add(pool.affine_select(out=mask[:, NT - 1:NT], in_=mask[:, NT - 1:NT], compare_op=ALU.is_ge, fill=0.0,
                                      base=LAST - 1, pattern=[[0, 1]], channel_multiplier=-1))
            ch.sync()
            pool.sem_inc(consts_ready, 1)
            pool.wait_ge(cleared_edges, 16)

            def scatter_group(g, s):
                when(pool, tk_g, stage_ready, g + 1)
                for j in range(GR):
                    pool.indirect_dma_start(edge_rows, bass.IndirectOffsetOnAxis(ap=row_at[s][:, j:j + 1], axis=0),
                                            stage_raw[s][:, ROW * j:ROW * (j + 1)], None).then_inc(scat[s], 16)

            with pool.Fori(0, NG // 2) as i:
                for s in range(2):
                    scatter_group(i * 2 + s, s)
            scatter_group(NG - 1, 0)
            pool.wait_ge(table_out, 16 * TPARTS)

            def gather_batch(n, h):
                when(pool, tk_g, idx_ready, n + 1)
                for u in range(UNROLL):
                    if u % 2 == 0:
                        when(pool, tk_g, seg, (n - BATCHES) * UNROLL + u + 2)
                    pool.indirect_dma_start(G[h][:, u, :], None, table,
                                            bass.IndirectOffsetOnAxis(ap=idx_s[h][:, u:u + 1], axis=0)).then_inc(gath[h][u // 2], 16)

            for h in range(BATCHES):
                gather_batch(h, h)
            with pool.Fori(1, STEPS) as i:
                for h in range(BATCHES):
                    gather_batch(i * BATCHES + h, h)
            for s in range(4):
                pool.wait_ge(xs_out[s], 16 * RSLOT.count(s) * (NT // RG))

            def gather_x(t, s):
                when(pool, tk_g, x_idx_ready, t + 1)
                pool.indirect_dma_start(x_in[s], None, token_x,
                                        bass.IndirectOffsetOnAxis(ap=x_idx[s], axis=0)).then_inc(xs_in[s], 16)


            def scatter_y(t, s):
                when(pool, tk_g, y_idx_ready, t + 1)
                when(pool, tk_g, y_ready, t + 1)
                pool.indirect_dma_start(pick_y, bass.IndirectOffsetOnAxis(ap=y_idx[s], axis=0),
                                        y_out[s % 2], None).then_inc(y_sent[s % 2], 16)

            for t in range(5):
                gather_x(t, t % 4)
            with pool.Fori(0, ST // 4 - 1) as i:
                for s in range(4):
                    scatter_y(i * 4 + s, s)
                    gather_x(i * 4 + s + 5, (s + 1) % 4)
            for t in range(ST - 5, ST):
                scatter_y(t, t % 4)

        @block.vector
        def _(dve):
            ch = Chain(dve, dve_steps)

            def tt(o, a, b, op):
                return dve.tensor_tensor(o, a, b, op)

            def ts(o, a, s1, op0, s2=None, op1=ALU.bypass):
                return dve.tensor_scalar(o, a, s1, s2, op0, op1)

            def scan(o, a):
                return dve.tensor_tensor_scan(o, ones[:, 0:a.shape[1]], a, 0.0, ALU.mult, ALU.add)

            ch.add(dve.memset(xr[:, NT - 1, :], 0.0))
            ch.add(dve.memset(srcI[:, FULL:EC], PAD))
            ch.add(dve.memset(dstI[:, FULL:EC], PAD))
            ch.sync()
            dve.sem_inc(pads_set, 1)
            dve.wait_ge(edges_in, 64)
            dve.wait_ge(consts_ready, 2)
            ch.link(ts(packed, srcI, CODE, ALU.logical_shift_left))
            ch.link(tt(packed, packed, dstI, ALU.bitwise_or))
            ch.add(ts(workI[:, 0:EC], packed, MASK, ALU.bitwise_xor, FLAG, ALU.bitwise_or))
            ch.sync()
            ch.link(ts(packed, srcI, 7, ALU.logical_shift_right))
            ch.add(dve.tensor_copy(tile_of, packed))
            ch.add(ts(sign_bias, iota[:, CT_DVE:NT + 1], -1.0, ALU.mult, 0.5, ALU.add))
            ch.sync()
            dve.sem_inc(tile_of_ready, 1)
            ch.link(tt(packed, srcI, dstI, ALU.is_equal))
            ch.link(ts(srcI, dstI, 7, ALU.logical_shift_right))
            ch.add(dve.tensor_copy(hi_of, srcI))
            ch.link(ts(dstI, dstI, P - 1, ALU.bitwise_and))
            ch.link(dve.scalar_tensor_tensor(out=lo_of, in0=packed, scalar=float(2 * P), in1=dstI, op0=ALU.mult, op1=ALU.add))
            cnt, need, nrow, rows_before, rs, nch, cb, off, t0 = col[0:9]
            nI = small(19, 50, I32)

            with dve.Fori(0, CT_DVE // 7) as i:
                for u in range(7):
                    t = i * 7 + u
                    dve.tensor_scalar(eq_scratch[u % 2], tile_of, iota[:, bass.ds(t, 1)], None, ALU.is_equal, ALU.add,
                                      accum_out=cnt[:, bass.ds(t, 1)])
                    if u != 0:
                        dve.drain()
            dve.wait_ge(signs_ready, 1)
            ch.link(tt(cnt[:, CT_DVE:NT], signs[:, 0:NT - CT_DVE], signs[:, 1:NT - CT_DVE + 1], ALU.subtract))
            ch.link(ts(cnt[:, CT_DVE:NT], cnt[:, CT_DVE:NT], 0.5, ALU.mult))
            ch.link(ts(nI[:, 0:NT], cnt[:, 0:NT], float(ROW - 1), ALU.add))
            ch.link(ts(nI[:, 0:NT], nI[:, 0:NT], ROW.bit_length() - 1, ALU.logical_shift_right))
            ch.link(dve.tensor_copy(nrow[:, 0:NT], nI[:, 0:NT]))
            ch.add(dve.scalar_tensor_tensor(out=need[:, 0:NT], in0=nrow[:, 0:NT], scalar=float(ROW), in1=cnt[:, 0:NT],
                                            op0=ALU.mult, op1=ALU.subtract))
            ch.link(dve.reduce_sum(t0[:, 0:1], nrow[:, 0:NT], axis=AX.X))
            ch.link(ts(nrow[:, NT:NT + 1], t0[:, 0:1], -1.0, ALU.mult, float(SORTN // ROW), ALU.add))
            dve.sem_inc(counts_ready, 1)
            for j in range(ROW - 1):
                ch.add(ts(fill[:, :, j], need[:, 0:NT], float(j), ALU.is_gt))
            ch.add(ts(t0[:, 0:NT], iota[:, 0:NT], -1.0, ALU.mult, float(NT), ALU.add))
            ch.sync()
            ch.link(tt(fill, fill, t0[:, 0:NT].unsqueeze(2).to_broadcast([P, NT, ROW - 1]), ALU.mult))
            nf = (ROW - 1) * NT
            ch.add(ts(fill_flat[:, 0:nf], fill_flat[:, 0:nf], -1.0, ALU.mult, float(NT), ALU.add))
            ch.add(dve.memset(fill_flat[:, nf:NF], float(NT)))
            ch.sync()
            ch.link(ts(fillI, fill_flat, float(P * ((1 << CODE) + 1)), ALU.mult))
            ch.add(ts(workI[:, EC:SORTN], fillI, MASK, ALU.bitwise_xor, FLAG, ALU.bitwise_or))
            dve.wait_ge(prefix_ready, 1)
            ch.link(ts(nI, B[6][:, 64:64 + NT + 1], float(RPC - 1), ALU.add))
            ch.link(ts(nI, nI, RPC.bit_length() - 1, ALU.logical_shift_right))
            ch.link(dve.tensor_copy(nch, nI))
            ch.link(scan(cb, nch))
            ch.link(tt(cb, cb, nch, ALU.subtract))
            ch.link(scan(rs, nrow))
            ch.link(tt(rs, rs, nrow, ALU.subtract))
            ch.link(dve.scalar_tensor_tensor(out=off, in0=cb, scalar=float(RPC), in1=rs, op0=ALU.mult, op1=ALU.subtract))
            ch.link(tt(off, off, B[6][:, 0:NT + 1], ALU.add))

            def half_stats(st6):
                mean, var, dm = col[9], col[10], col[11]
                ch.add(tt(mean[:, 0:NT], st6[:, :, 1], st6[:, :, 4], ALU.add))
                ch.add(tt(dm[:, 0:NT], st6[:, :, 1], st6[:, :, 4], ALU.subtract))
                ch.add(tt(var[:, 0:NT], st6[:, :, 2], st6[:, :, 5], ALU.add))
                ch.sync()
                ch.add(ts(mean[:, 0:NT], mean[:, 0:NT], 0.5, ALU.mult))
                ch.add(tt(dm[:, 0:NT], dm[:, 0:NT], dm[:, 0:NT], ALU.mult))
                ch.add(ts(var[:, 0:NT], var[:, 0:NT], 1.0 / D, ALU.mult))
                ch.sync()
                ch.link(dve.scalar_tensor_tensor(out=var[:, 0:NT], in0=dm[:, 0:NT], scalar=0.25, in1=var[:, 0:NT],
                                                 op0=ALU.mult, op1=ALU.add))
                return mean, var

            def onehots(t, s):
                when(dve, tk_v, oh_free, t - 1)
                lo = lo_of[:, bass.ds(t * HB, HB)].unsqueeze(1).to_broadcast([P, P, HB])
                hi = hi_of[:, bass.ds(t * HB, HB)].unsqueeze(1).to_broadcast([P, NT, HB])
                tt(oh_lo[s], digits, lo, ALU.is_equal)
                tt(oh_hi[s], digits[:, 0:NT, :], hi, ALU.is_equal).then_inc(oh_ready, 1)

            ch.link(dve.tensor_copy(row_k, iota[:, 0:GR]))

            def sort_group(g, s, first, hist):
                for u in range(GSTEPS):
                    eight = sorted_g[:, 8 * u:8 * u + 8]
                    dve.max(eight, work)
                    dve.drain()
                    dve.match_replace(out=work, in_to_replace=eight, in_values=work, imm_value=0.0)
                    if u % 2 == 0 and u // 2 < hist:
                        onehots(first + u // 2, u // 2 % 2)
                    dve.drain()
                when(dve, tk_v, scat[s], (g - s) * (8 * GR))
                ts(stage_raw[s], sorted_i, MASK, ALU.bitwise_xor, MASK, ALU.bitwise_and)
                dve.drain()
                ts(row_tileI, stage_raw[s][:, ::ROW], CODE + 7, ALU.logical_shift_right)
                dve.drain()
                dve.tensor_copy(row_tile, row_tileI)
                dve.drain()
                tt(lookup, row_tile.unsqueeze(2).to_broadcast([P, GR, NT + 1]),
                   iota[:, 0:NT + 1].unsqueeze(1).to_broadcast([P, GR, NT + 1]), ALU.is_equal)
                dve.drain()
                tt(lookup, lookup, off.unsqueeze(1).to_broadcast([P, GR, NT + 1]), ALU.mult)
                dve.drain()
                dve.tensor_reduce(row_sum, lookup, axis=AX.X, op=ALU.add)
                dve.drain()
                tt(row_at[s], row_sum, row_k, ALU.add).then_inc(stage_ready, 1)
                dve.drain()
                ts(row_k, row_k, float(GR), ALU.add)
                dve.drain()

            sort_group(0, 0, 0, 0)
            ch.link(dve.tensor_copy(digits, iota.unsqueeze(2).to_broadcast([P, P, HB])))
            sort_group(1, 1, 0, 0)
            dve.wait_ge(x_in_s, 32)

            def stats_of(first, n, per):
                with dve.Fori(0, n // per) as i:
                    for u in range(per):
                        t = i * per + (first + u)
                        dve.bn_stats(stats_x[:, bass.ds(t, 1), :], xr[:, bass.ds(t, 1), :]).then_inc(bn_done, 1)

            stats_of(0, 24, 8)
            sort_group(2, 0, 0, 0)
            stats_of(24, NT - 24, 5)
            dve.wait_ge(bn_done, NT)
            mean, var = half_stats(stats_x)
            ch.link(ts(var[:, 0:NT], var[:, 0:NT], LN_EPS, ALU.add))
            dve.sem_inc(std_in, 1)
            dve.wait_ge(std_out, 1)
            ch.link(dve.reciprocal(rstd, col[12][:, 0:NT]))
            ch.link(dve.scalar_tensor_tensor(out=nmr, in0=mean[:, 0:NT], scalar=-1.0, in1=rstd, op0=ALU.mult, op1=ALU.mult))
            dve.sem_inc(norm_ready, 1)
            sort_group(3, 1, 0, 0)
            sort_group(4, 0, 0, HG)
            cgrid, ctile = col[9][:, 0:CG], col[10][:, 0:CG]
            ch.link(ts(cgrid, iota[:, 0:CG], float(P), ALU.mult, pcol, ALU.add))
            ch.link(tt(tile_cmp, cgrid.unsqueeze(2).to_broadcast([P, CG, NT]),
                       cb[:, 1:NT + 1].unsqueeze(1).to_broadcast([P, CG, NT]), ALU.is_ge))
            ch.link(dve.tensor_reduce(ctile, tile_cmp, axis=AX.X, op=ALU.add))
            ch.link(ts(ctile, ctile, float(D), ALU.mult))
            dve.sem_inc(ctile_ready, 1)
            with dve.Fori(2, 7) as i:
                for s in range(2):
                    sort_group(i * 2 + s + 1, 1 - s, (i * 2 + s - 3) * HG, HG)
            for t in range(NT - 1 - HG, NT):
                onehots(t, t % 2)
            dve.wait_ge(sums_done, 1)
            dve.wait_ge(ctile_T, 1)
            ch.link(dve.tensor_copy(CT_row, B[6][0:CG, 128:256]))
            dve.sem_inc(ctile_row, 1)
            ch.link(ts(col[9][:, 0:NT], B[5][:, 0:NT], 1.0, ALU.add))
            dve.sem_inc(std_in, 1)
            dve.wait_ge(std_out, 2)
            ch.link(dve.reciprocal(dinv, col[12][:, 0:NT]))
            ch.add(dve.memset(acc[:, NT, :], 0.0))
            for k in range(TPARTS):
                a = acc[:, k * TPART:(k + 1) * TPART, :]
                tt(a, a, dinv[:, k * TPART:(k + 1) * TPART].unsqueeze(2).to_broadcast([P, TPART, D]),
                   ALU.mult).then_inc(table_ready, 1)
            ch.link(dve.memset(head_mask, 0.0))
            for b in range(NH):
                ch.add(dve.memset(head_mask[b * DEPTH:(b + 1) * DEPTH, b * DEPTH:(b + 1) * DEPTH], 1.0))
            ch.sync()
            for g in range(KD):
                ch.add(tt(kv_ext[:, g, 0:P], B[3 + g][:, 0:P], head_mask, ALU.mult))
                ch.add(dve.tensor_copy(ksum[:, g:g + 1], B[3 + g][:, P:P + 1]))
            ch.sync()
            for g in range(KD):
                ch.add(ts(kv_ext[:, g, P:P + NH], head_mask[:, ::DEPTH], ksum[:, g:g + 1], ALU.mult))
            ch.sync()
            dve.sem_inc(kvbd_ready, 1)

            def divide(t):
                when(dve, tk_v, q_ps, t + 1)
                when(dve, tk_v, q_mixedT_ps, t)
                res = B[5][:, :].rearrange("p (g n) -> p g n", g=KD)
                den = q_den.rearrange("p (g h) -> p g h", g=KD)
                ts(den, res[:, :, P:P + NH], 1e-6, ALU.add)
                dve.drain()
                dve.reciprocal(q_den, q_den)
                dve.drain()
                tt(mixed.rearrange("p (g h d) -> p g h d", g=KD, h=NH), res[:, :, 0:P].rearrange("p g (h d) -> p g h d", h=NH),
                   den.unsqueeze(3).to_broadcast([P, KD, NH, DEPTH]), ALU.mult).then_inc(q_mixed, 1)

            def add_attention(t):
                when(dve, tk_v, q_out, t + 1)
                xt = xr[:, bass.ds(t, 1), :].rearrange("p o d -> p (o d)")
                tt(xt, xt, B[7][:, 0:D], ALU.add).then_inc(q_added, 1)

            dve.wait_ge(raw_in, 16)
            ch.add(ts(src_u, raw, CODE, ALU.logical_shift_right))
            ch.add(ts(dst_u, raw, (1 << CODE) - 1, ALU.bitwise_and))
            ch.sync()
            ch.link(tt(same_f, src_u, dst_u, ALU.is_equal))
            ch.add(ts(dst_f, dst_u, float(NT * P - 1), ALU.min))
            ch.link(ts(raw, src_u, P - 1, ALU.bitwise_and))
            ch.link(dve.scalar_tensor_tensor(out=lo_f, in0=same_f, scalar=float(2 * P), in1=raw, op0=ALU.mult, op1=ALU.add))
            dve.sem_inc(unpacked, 1)
            for k in range(4):
                dve.wait_ge(unp_T, k + 1)
                n = min(512, CHUNKS - 512 * (k % 2))
                to = (dst_T, lo_neg)[k // 2][:, 512 * (k % 2):512 * (k % 2) + n]
                ch.add(dve.tensor_copy(to, B[k][:, 0:n]) if k < 2 else ts(to, B[k][:, 0:n], -1.0, ALU.mult))
            ch.sync()
            dve.sem_inc(unp_out, 1)
            dve.wait_ge(tile_row_in, 16)

            def places(n):
                return nc.values_load_multi_w_load_instructions(
                    tile_row[0:1, bass.ds(n * UNROLL, 2 * UNROLL)], engines=[mybir.EngineType.DVE], min_val=0,
                    max_val=NT * D)[1]

            def add_sums(n, h, at):
                when(dve, tk_v, seg, (n + 1) * UNROLL)
                for u in range(UNROLL):
                    a = ACC[:, bass.ds(at[u], D)]
                    tt(a, a, B[h % 2 * 2 + u // 2][:, (u % 2) * D:(u % 2 + 1) * D], ALU.add)
                    dve.drain()
                dve.sem_inc(added, 1)

            def shift_columns():
                dve.wait_ge(lnb_in, 48)
                dve.memset(b_one_flat, 0.0)
                dve.drain()
                for k in range(KD):
                    for e in range(E):
                        dve.tensor_copy(b_one[:, k, e, e:e + 1], b_s[:, k, e:e + 1])
                dve.drain()
                dve.sem_inc(b_one_ready, 1)

            def add_step(i):
                at = places(i * BATCHES)
                add_sums(i * BATCHES, 0, at[:UNROLL])
                if not isinstance(i, int) or i < NT:
                    divide(i)
                add_sums(i * BATCHES + 1, 1, at[UNROLL:])
                at = places(i * BATCHES + 2)
                if not isinstance(i, int) or i > 0:
                    add_attention(i - 1)
                add_sums(i * BATCHES + 2, 2, at[:UNROLL])
                add_sums(i * BATCHES + 3, 3, at[UNROLL:])

            def add_batches(i):
                for h in range(0, BATCHES, 2):
                    at = places(i * BATCHES + h)
                    add_sums(i * BATCHES + h, h, at[:UNROLL])
                    add_sums(i * BATCHES + h + 1, h + 1, at[UNROLL:])

            add_step(0)
            with dve.Fori(1, NT) as i:
                add_step(i)
            add_step(NT)
            add_batches(NT + 1)
            shift_columns()
            with dve.Fori(NT + 2, STEPS) as i:
                add_batches(i)
            dve.wait_ge(b1_ps, 1)
            for n in range(2):
                last = dve.tensor_copy(b1_rows[n], B[5 + n][0:E, :])
            last.then_inc(b1_rows_ready, 1)
            dve.wait_ge(q_added, NT)

            def residual(t):
                a = acc[:, bass.ds(t, 1), :].rearrange("p o d -> p (o d)")
                xt = xr[:, bass.ds(t, 1), :].rearrange("p o d -> p (o d)")
                return dve.scalar_tensor_tensor(out=a, in0=a, scalar=dinv[:, bass.ds(t, 1)], in1=xt, op0=ALU.mult, op1=ALU.add)

            def residuals(g, us):
                for u in us:
                    residual(g * RG + u)

            def statistics(g, us):
                for u in us:
                    t = g * RG + u
                    dve.bn_stats(stats2[:, bass.ds(t, 1), :], acc[:, bass.ds(t, 1), :])

            def norms(g):
                def part(a):
                    return a[:, bass.ds(g * RG, RG)]
                st6 = stats2[:, bass.ds(g * RG, RG), :]
                sums, dm, var, r2, std, root = (col[k][:, 0:RG] for k in range(8, 14))
                stt = dve.scalar_tensor_tensor
                tt(sums, st6[:, :, 1], st6[:, :, 4], ALU.add)
                tt(dm, st6[:, :, 1], st6[:, :, 4], ALU.subtract)
                tt(var, st6[:, :, 2], st6[:, :, 5], ALU.add)
                dve.drain()
                stt(out=dm, in0=dm, scalar=0.25, in1=dm, op0=ALU.mult, op1=ALU.mult)
                dve.drain()
                stt(out=var, in0=var, scalar=1.0 / D, in1=dm, op0=ALU.mult, op1=ALU.add)
                dve.drain()
                ts(root, var, LN_EPS, ALU.add).then_inc(std_in, 1)
                when(dve, tk_v, std_out, g * 2 + 3)
                dve.reciprocal(part(rstd), std)
                dve.drain()
                stt(out=part(nmr), in0=sums, scalar=-0.5, in1=part(rstd), op0=ALU.mult, op1=ALU.mult)
                tt(r2, part(rstd), part(rstd), ALU.mult)
                dve.drain()
                tt(r2, r2, var, ALU.mult)
                dve.drain()
                ts(root, r2, LN_EPS, ALU.add).then_inc(std_in, 1)
                when(dve, tk_v, std_out, g * 2 + 4)
                dve.reciprocal(r2, std)
                dve.drain()
                tt(part(rstd2), r2, part(rstd), ALU.mult)
                tt(part(nmr2), r2, part(nmr), ALU.mult).then_inc(norm2_ready, 1)
                dve.drain()

            def transposed_x2(g, u):
                t, r = g * RG + u, RSLOT[u]
                when(dve, tk_v, x2T_ps, t + 1)
                when(dve, tk_v, logit_ps, t - RLAG[u] + 1)
                dve.tensor_copy(x2T[r], B[r][:, 0:D].rearrange("p (g n) -> p g n", g=KD)).then_inc(x2T_even, 1)

            def group(g, last=False):
                if not last:
                    residuals(g + 1, range(4))
                transposed_x2(g, 0)
                if not last:
                    residuals(g + 1, range(4, RG))
                    dve.drain()
                    statistics(g + 1, range(2))
                transposed_x2(g, 2)
                if not last:
                    statistics(g + 1, range(2, RG))
                    dve.drain()
                transposed_x2(g, 4)
                if not last:
                    norms(g + 1)
                transposed_x2(g, 6)

            residuals(0, range(RG))
            dve.drain()
            statistics(0, range(RG))
            dve.drain()
            norms(0)
            group(0)
            dve.wait_ge(b1T_ps, 1)
            ch.link(tt(hid_bias.rearrange("p (e c) -> p e c", e=E), B[7][:, 0:E * KH].rearrange("p (c e) -> p e c", e=E),
                       b1_s.rearrange("p (e c) -> p e c", e=E), ALU.add))
            dve.wait_ge(bias_in, 16)
            ch.link(dve.tensor_copy(bias_b[:, 0, :], bias_f))
            ch.link(tt(bias_r, bias_f, bias_b[:, 0, :], ALU.subtract))
            ch.link(dve.tensor_copy(bias_b[:, 1, :], bias_r))
            ch.link(tt(bias_r, bias_r, bias_b[:, 1, :], ALU.subtract))
            ch.link(dve.tensor_copy(bias_b[:, 2, :], bias_r))
            dve.sem_inc(bias_ready, 1)
            with dve.Fori(1, NT // RG - 1) as g:
                group(g)
            dve.sem_inc(x_done, 1)
            group(NT // RG - 1, True)
            dve.wait_ge(logit_ps, NT)
            dve.wait_ge(router_in, 32)
            dve.wait_ge(bias_out, 16)
            full = [P, NT, E]
            ch.link(tt(logits, B[4][:, 0:NE].rearrange("p (t e) -> p t e", e=E), br_s.unsqueeze(1).to_broadcast(full), ALU.add))
            ch.add(ts(slot_e, iota[:, 0:E], -float(E), ALU.add))
            ch.sync()
            ch.link(dve.tensor_copy(expert_m8, slot_e.unsqueeze(1).to_broadcast(full)))
            best, which = col[9][:, 0:NT], col[10][:, 0:NT]
            second = col[11][:, 0:NT]
            for s in range(4):
                dve.wait_ge(xs_out[s], 16 * RSLOT.count(s) * (NT // RG))
            for k, (top, pick) in enumerate(((best, pick0), (second, pick1))):
                ch.link(dve.tensor_reduce(top, logits, axis=AX.X, op=ALU.max))
                ch.link(tt(tmp, logits, top.unsqueeze(2).to_broadcast(full), ALU.is_equal))
                ch.link(tt(tmp, tmp, expert_m8, ALU.mult))
                ch.link(dve.tensor_reduce(which, tmp, axis=AX.X, op=ALU.min))
                ch.link(tt(pick, expert_m8, which.unsqueeze(2).to_broadcast(full), ALU.is_equal))
                if k == 0:
                    ch.link(dve.scalar_tensor_tensor(out=logits, in0=pick, scalar=-3e38, in1=logits, op0=ALU.mult, op1=ALU.add))
            ch.link(tt(both, pick0, pick1, ALU.add))
            ch.link(tt(both, both, mask.unsqueeze(2).to_broadcast(full), ALU.mult))
            dve.sem_inc(pick_ready, 1)
            ch.link(tt(second, second, best, ALU.subtract))
            dve.sem_inc(gap_ready, 1)
            dve.wait_ge(ranks_ps, 1)
            fl = lambda a: a.rearrange("p t e -> p (t e)")
            ch.add(dve.tensor_copy(fl(rank), B[2][:, 0:NE]))
            ch.add(dve.tensor_copy(fl(totals), B[3][:, 0:NE]))
            ch.sync()
            for e in range(E):
                ch.add(scan(runs[:, :, e], totals[:, :, e]))
            ch.sync()
            ch.link(dve.tensor_copy(exp_tot, runs[:, NT - 1, :]))
            ch.add(tt(runs, runs, totals, ALU.subtract))
            ch.sync()
            ch.link(tt(rank, rank, runs, ALU.add))
            ch.link(ts(expI, exp_tot, float(P - 1), ALU.add))
            ch.link(ts(expI, expI, 7, ALU.logical_shift_right))
            ch.link(dve.tensor_copy(exp_tiles, expI))
            ch.link(scan(exp_i, exp_tiles))
            ch.link(tt(exp_base, exp_i, exp_tiles, ALU.subtract))
            ch.link(ts(slot_e[:, 0:E - 1], exp_i[:, 0:E - 1], pcol, ALU.is_le))
            ch.link(dve.reduce_sum(exp_tot[:, 0:1], slot_e[:, 0:E - 1], axis=AX.X))
            ch.link(dve.tensor_copy(slot_eI, exp_tot[:, 0:1]))
            dve.sem_inc(slot_e_ready, 1)
            ch.link(ts(exp_base, exp_base, float(P), ALU.mult))
            ch.link(tt(rank, rank, exp_base.unsqueeze(1).to_broadcast(full), ALU.add))
            inv = col[12][:, 0:NT]
            ch.link(ts(inv, mask, -1.0, ALU.mult, 1.0, ALU.add))
            ch.link(tt(junk, junk, inv, ALU.mult))
            for c, pick in enumerate((pick0, pick1)):
                pf = col[13][:, 0:NT]
                ch.link(tt(tmp, rank, pick, ALU.mult))
                ch.link(dve.tensor_reduce(pf, tmp, axis=AX.X, op=ALU.add))
                ch.link(tt(pf, pf, mask, ALU.mult))
                ch.link(tt(pf, pf, junk, ALU.add))
                if c:
                    ch.link(dve.scalar_tensor_tensor(out=pf, in0=inv, scalar=float(P), in1=pf, op0=ALU.mult, op1=ALU.add))
                ch.link(dve.tensor_copy(slotI[:, c * NT:(c + 1) * NT], pf))
            ch.add(dve.tensor_copy(pick_col, iota[:, 0:PICKS]))
            ch.add(ts(row_1, pcol, 1.0, ALU.add))
            ch.add(ts(dump_row, pcol, float(PICKS * P + 1), ALU.add))
            ch.add(dve.memset(zero_row, 0.0))
            ch.sync()
            dve.sem_inc(zero_ready, 1)
            ch.add(ts(digitI, slotI, P - 1, ALU.bitwise_and))
            ch.add(dve.tensor_copy(pc_digits, iota.unsqueeze(2).to_broadcast([P, P, PC])))
            ch.sync()
            ch.link(dve.tensor_copy(slot_at, digitI))
            ch.link(ts(digitI, slotI, 7, ALU.logical_shift_right))
            ch.link(dve.tensor_copy(slot_tile, digitI))

            def slot_digits(g, s):
                def cols(a, rows):
                    return a[:, bass.ds(g * PC, PC)].unsqueeze(1).to_broadcast([P, rows, PC])
                tt(pc_at[s], pc_digits, cols(slot_at, P), ALU.is_equal)
                tt(pc_tile, pc_digits[:, 0:ST, :], cols(slot_tile, ST), ALU.is_equal)
                dve.drain()
                when(dve, tk_v, pc_used, g)
                tt(pc_tokens[:, 0:ST, :], pc_tile, cols(pick_col, ST), ALU.mult)
                ts(pc_tokens[:, ST:2 * ST, :], pc_tile, row_1, ALU.mult)
                dve.drain()
                dve.sem_inc(pc_ready, 1)

            dve.wait_ge(slot_e_out, 16)
            slot_digits(0, 0)
            with dve.Fori(0, PICKS // PC // 2) as i:
                slot_digits(i * 2 + 1, 1)
                slot_digits(i * 2 + 2, 0)
            dve.wait_ge(tokens_ps, 1)
            ch.link(ts(row_f, B[5][:, 0:ST], float(P), ALU.mult))
            ch.link(tt(row_f, row_f, B[5][:, ST:2 * ST], ALU.add))
            ch.add(dve.memset(parity[:, 0:ST:2], 0.0))
            ch.add(dve.memset(parity[:, 1:ST:2], float(P)))
            ch.link(ts(unused, row_f, 0.0, ALU.is_equal))
            ch.add(dve.scalar_tensor_tensor(out=unused_at, in0=parity, scalar=dump_row, in1=unused, op0=ALU.add, op1=ALU.mult))
            ch.add(ts(row_f, row_f, -1.0, ALU.add))
            ch.sync()
            ch.link(tt(row_f, row_f, unused_at, ALU.add))
            ch.add(dve.tensor_copy(slot_row, row_f))
            ch.add(ts(tok_f, row_f, float(NT * P), ALU.is_ge, -float(NT * P), ALU.mult))
            ch.sync()
            ch.link(tt(tok_f, tok_f, row_f, ALU.add))
            ch.link(ts(tok_f, tok_f, float(NT * P - 1), ALU.min))
            ch.link(dve.tensor_copy(slot_token, tok_f))
            dve.sem_inc(slots_ready, 1)
            dve.wait_ge(gap_exp, 1)
            ch.link(ts(gate0, gate1, 1.0, ALU.add))
            ch.link(dve.reciprocal(gate0, gate0))
            ch.link(tt(gate1, gate1, gate0, ALU.mult))
            ch.link(dve.memset(ones3, 1.0))
            dve.sem_inc(ones3_ready, 1)
            def load_w1(t):
                e = nc.vector.value_load(expert_row[0:1, bass.ds(t, 1)], min_val=0, max_val=E - 1)
                when(dve, tk_v, hid_ps, t)
                dve.tensor_copy(w1_now, W1A[:, bass.ds(e * (KD * H), KD * H)].rearrange("p (k n) -> p k n", k=KD)
                                ).then_inc(w1_now_ready, 1)

            def inputs(t, s):
                when(dve, tk_v, xsT_ps, t + 1)
                when(dve, tk_v, hid_ps, t - 1)
                dve.tensor_copy(x_inT[s], B[6][:, s * D:(s + 1) * D].rearrange("p (g n) -> p g n", g=KD)).then_inc(xsT_ready, 1)

            def outputs(t, s):
                when(dve, tk_v, y_ps, t + 1)
                when(dve, tk_v, y_sent[s], (t - s) * 8)
                dve.tensor_copy(y_out[s], B[7][:, 0:D]).then_inc(y_ready, 1)

            def step(t, s):
                if not isinstance(t, int) or t + 2 < ST:
                    load_w1(t + 2)
                    inputs(t + 2, s)
                outputs(t, s)

            dve.wait_ge(slot_e_in, 16)
            dve.wait_ge(w1_scaled, 1)
            load_w1(0)
            inputs(0, 0)
            load_w1(1)
            inputs(1, 1)
            for t in range(3):
                step(t, t % 2)
            with dve.Fori(1, ST // 2 - 1) as i:
                step(i * 2 + 1, 1)
                step(i * 2 + 2, 0)
            for t in range(ST - 2, ST):
                step(t, t % 2)

            def weigh(t, y, gate, onto):
                return dve.scalar_tensor_tensor(out=y_first[:, t, :], in0=y[:, t, :], scalar=gate[:, t:t + 1], in1=onto[:, t, :],
                                                op0=ALU.mult, op1=ALU.add)

            for k, part in enumerate(OPARTS):
                dve.wait_ge(picks_in[k], 32 if part.stop < NT else 64)
                for t in range(part.start, part.stop):
                    weigh(t, y_first, gate0, acc)
                dve.drain()
                for t in range(part.start, part.stop):
                    last = weigh(t, y_second, gate1, y_first)
                last.then_inc(o_ready, 1)

        @block.scalar
        def _(act):
            ch = Chain(act, act_steps)

            def cp(o, i, fn=ACT.Copy, **kw):
                return nc.scalar.activation(o, i, fn, **kw)

            act.wait_ge(tile_of_ready, 1)
            for k in range(NT - CT_DVE + 1):
                cp(sign_scratch[k % 2], tile_of, ACT.Sign, bias=sign_bias[:, k:k + 1], accum_out=signs[:, k:k + 1])
                if k:
                    act.drain()
            act.sem_inc(signs_ready, 1)
            act.wait_ge(std_in, 1)
            cp(col[12][:, 0:NT], col[10][:, 0:NT], ACT.Sqrt).then_inc(std_out, 1)
            act.wait_ge(norm_ready, 1)
            act.wait_ge(weights_in, 96)

            def normalize(t, s):
                when(act, tk_a, t_ready, t - 1)
                xt = xr[:, bass.ds(t, 1), :].rearrange("p o d -> p (o d)")
                cp(xn[s], xt, ACT.Identity, scale=rstd[:, bass.ds(t, 1)], bias=nmr[:, bass.ds(t, 1)]).then_inc(xn_ready, 1)

            def transposed(t, s):
                when(act, tk_a, t_ready, t + 1)
                when(act, tk_a, hq_ready, t - 1)
                cp(xnT[s], B[0][:, s * D:(s + 1) * D].rearrange("p (g n) -> p g n", g=KD)).then_inc(xnT_ready, 1)

            def keys_values(t):
                when(act, tk_a, kv_ready, t + 1)
                when(act, tk_a, kv_done, t)
                cp(ka, B[1][:, 0:D], ACT.Relu, scale=-1.0)
                cp(kc, B[1][:, 0:D], ACT.Relu)
                act.drain()
                cp(kb, ka, ACT.Exp, scale=-1.0)
                m = mask[:, bass.ds(t, 1)]
                cp(vbuf[:, :, 0:P], B[1][:, D:2 * D].rearrange("p (g n) -> p g n", g=KD), scale=m)
                cp(vbuf[:, 0, P:P + 1], m)
                cp(vbuf[:, 1, P:P + 1], m)
                act.drain()
                act.sem_inc(kvfm_ready, 1)

            def features_queries(t):
                when(act, tk_a, hq_ready, t + 1)
                cp(acc[:, bass.ds(t, 1), :].rearrange("p o d -> p (o d)"), B[2][:, 0:D])
                for g in range(KD):
                    last = cp(q_all[:, g, bass.ds(t * P, P)], B[2][:, D + g * P:D + (g + 1) * P], ACT.Identity,
                              bias=bqc[:, g:g + 1])
                last.then_inc(proj_out, 1)

            def project(t, s):
                normalize(t + 1, 1 - s)
                keys_values(t)
                transposed(t + 1, 1 - s)
                features_queries(t)

            normalize(0, 0)
            transposed(0, 0)
            for t in range(2):
                project(t, t)
            with act.Fori(1, NT // 2) as i:
                for s in range(2):
                    project(i * 2 + s, s)
            keys_values(NT - 1)
            features_queries(NT - 1)
            act.wait_ge(std_in, 2)
            cp(col[12][:, 0:NT], col[9][:, 0:NT], ACT.Sqrt).then_inc(std_out, 1)

            act.wait_ge(wo_in, 16)

            def query_terms(t, part):
                qt = q_all[:, :, bass.ds(t * P, P)]
                g3 = lambda a: a.rearrange("p (g n) -> p g n", g=KD)
                if part == 0:
                    when(act, tk_a, q_ps, t)
                    cp(g3(q_neg), qt, ACT.Relu, scale=-1.0)
                elif part == 1:
                    cp(g3(q_relu), qt, ACT.Relu)
                else:
                    act.drain()
                    cp(q_exp, q_neg, ACT.Exp, scale=-1.0).then_inc(q_terms, 1)

            def transposed_mix(t):
                when(act, tk_a, q_mixedT_ps, t + 1)
                when(act, tk_a, q_out, t)
                cp(mixedT, B[4][:, 0:D].rearrange("p (g n) -> p g n", g=KD)).then_inc(q_mixedT, 1)

            def indices(n, h):
                for half in gath[h]:
                    when(act, tk_a, half, (n - h) * (32 // BATCHES))
                act.copy(idx_s[h], dst_T[:, bass.ds(n * UNROLL, UNROLL)]).then_inc(idx_ready, 1)

            def onehots(n, h):
                when(act, tk_a, seg, (n - BATCHES + 1) * UNROLL)
                for u in range(UNROLL):
                    cp(OH[h][:, u, :], iota, ACT.Abs, bias=lo_neg[:, bass.ds(n * UNROLL + u, 1)])
                act.drain()
                cp(OH[h], OH[h], ACT.Relu, scale=-1.0, bias=ones[:, 0:1]).then_inc(onehot_ready, 1)

            def index_step(i):
                for h in range(BATCHES):
                    if h == 3 and (not isinstance(i, int) or i > 0):
                        transposed_mix(i - 1)
                    indices(i * BATCHES + h, h)
                    if h < 3 and (not isinstance(i, int) or i < NT):
                        query_terms(i, h)
                    onehots(i * BATCHES + h, h)

            act.wait_ge(unp_out, 1)
            index_step(0)
            with act.Fori(1, NT) as i:
                index_step(i)
            index_step(NT)
            with act.Fori(NT + 1, STEPS) as i:
                for h in range(BATCHES):
                    indices(i * BATCHES + h, h)
                    onehots(i * BATCHES + h, h)

            def transposed_x2(g, u):
                t, r = g * RG + u, RSLOT[u]
                when(act, tk_a, x2T_ps, t + 1)
                when(act, tk_a, logit_ps, t - RLAG[u] + 1)
                cp(x2T[r], B[r][:, 0:D].rearrange("p (g n) -> p g n", g=KD)).then_inc(x2T_odd, 1)

            def root(k):
                when(act, tk_a, std_in, k + 3)
                cp(col[12][:, 0:RG], col[13][:, 0:RG], ACT.Sqrt).then_inc(std_out, 1)

            root(0)
            root(1)

            def norm_group(g, last=False):
                when(act, tk_a, norm2_ready, g + 1)
                for u in range(RG):
                    t, r = g * RG + u, RSLOT[u]
                    when(act, tk_a, x2T_ps, t - RLAG[u] + 1)
                    xt = acc[:, bass.ds(t, 1), :].rearrange("p o d -> p (o d)")
                    cp(x2[r], xt, ACT.Identity, scale=rstd[:, bass.ds(t, 1)], bias=nmr[:, bass.ds(t, 1)]).then_inc(x2_ready, 1)
                    when(act, tk_a, xs_out[r], (g * RSLOT.count(r) + u // 4) * 16)
                    cp(xs2[r], xt, ACT.Identity, scale=rstd2[:, bass.ds(t, 1)], bias=nmr2[:, bass.ds(t, 1)]).then_inc(xs_ready, 1)
                    if u % 2 == 0 and u > 0:
                        transposed_x2(g, u - 1)
                    if u in (4, 5) and not last:
                        root((g + 1) * 2 + u - 4)

            norm_group(0)
            with act.Fori(1, NT // RG - 1) as g:
                norm_group(g)
            norm_group(NT // RG - 1, True)
            act.wait_ge(gap_ready, 1)
            cp(gate1, col[11][:, 0:NT], ACT.Exp).then_inc(gap_exp, 1)
            act.wait_ge(b1_ps, 1)
            act.wait_ge(lnb_in, 48)
            for e in range(E):
                for k in range(KD):
                    last = cp(w1_s[:, e, k, :], w1_s[:, e, k, :], scale=g_s[:, k, e:e + 1])
            last.then_inc(w1_scaled, 1)
            act.wait_ge(slot_e_in, 16)

            def expert(t, s):
                e = nc.scalar.value_load(expert_row[0:1, bass.ds(t, 1)], min_val=0, max_val=E - 1)
                when(act, tk_a, hid_ps, t + 1)
                when(act, tk_a, y_ps, t - 1)
                for c in range(KH):
                    last = cp(hidT[s][:, c, :], B[2 * s + c // 4][:, c % 4 * P:(c % 4 + 1) * P], ACT.Gelu,
                              bias=hid_bias[:, bass.ds(e * KH + c, 1)])
                last.then_inc(hid_ready, 1)

            def index(t, s):
                when(act, tk_a, xsT_ps, t - 3)
                act.copy(x_idx[s], slot_token[:, bass.ds(t, 1)]).then_inc(x_idx_ready, 1)

            def y_index(t, s):
                when(act, tk_a, y_sent[s % 2], (t - s % 2) * 8 - 16)
                act.copy(y_idx[s], slot_row[:, bass.ds(t, 1)]).then_inc(y_idx_ready, 1)

            act.wait_ge(slots_ready, 1)
            for t in range(4):
                index(t, t)
            index(4, 0)
            for t in range(4):
                expert(t, t % 2)
                y_index(t, t)
                index(t + 5, (t + 1) % 4)
            with act.Fori(1, ST // 4 - 1) as i:
                for s in range(4):
                    expert(i * 4 + s, s % 2)
                    y_index(i * 4 + s, s)
                    index(i * 4 + s + 5, (s + 1) % 4)
            for t in range(ST - 5, ST):
                expert(t, t % 2)
                y_index(t, t % 4)

        @block.tensor
        def _(pe):
            mm = nc.tensor.matmul
            pe.wait_ge(consts_ready, 2)
            pe.wait_ge(counts_ready, 1)
            mm(B[6][:, 0:NT + 1], tri, col[2], start=True, stop=True)
            mm(B[6][:, 64:64 + NT + 1], ones, col[2], start=True, stop=True).then_inc(prefix_ready, 1)
            pe.wait_ge(weights_in, 96)
            zb = zeros.bitcast(BF16)
            mm(B[3][:, 0:P + 1], zeros[:, 0:P], zeros[:, 0:P + 1], start=True, stop=False)
            mm(B[4][:, 0:P + 1], zeros[:, 0:P], zeros[:, 0:P + 1], start=True, stop=False)
            mm(B[5][:, 0:NT], zb[:, 0:P], zb[:, 0:NT], start=True, stop=False)

            def transpose_x(t, s):
                when(pe, tk_t, xn_ready, t + 1)
                when(pe, tk_t, xnT_ready, t - 1)
                for k in range(KD):
                    last = nc.tensor.transpose(B[0][:, s * D + k * P:s * D + (k + 1) * P], xn[s][:, k * P:(k + 1) * P], ident)
                last.then_inc(t_ready, 1)

            def keys_values(t, s):
                when(pe, tk_t, xnT_ready, t + 1)
                when(pe, tk_t, kvfm_ready, t)
                mm(B[1][:, :], ones[0:1, :], bkv_row, start=True, stop=False)
                for k in range(KD):
                    last = mm(B[1][:, :], xnT[s][:, k, :], wkv_s[:, k, :], start=False, stop=k == KD - 1)
                last.then_inc(kv_ready, 1)

            def features_queries(t, s):
                when(pe, tk_t, proj_out, t)
                for k in range(KD):
                    mm(B[2][:, 0:D], xnT[s][:, k, :], gw_s[:, k, :], start=k == 0, stop=k == KD - 1)
                for g in range(KD):
                    for k in range(KD):
                        last = mm(B[2][:, D + g * P:D + (g + 1) * P], wq_s[:, k, g * P:(g + 1) * P], xnT[s][:, k, :],
                                  start=k == 0, stop=k == KD - 1)
                last.then_inc(hq_ready, 1)

            def sum_kv(t):
                when(pe, tk_t, kvfm_ready, t + 1)
                for g in range(KD):
                    for kk in (kb, kc):
                        last = mm(B[3 + g][:, 0:P + 1], kk[:, g * P:(g + 1) * P], vbuf[:, g, :], start=False, stop=False)
                last.then_inc(kv_done, 1)

            def project(t, s):
                keys_values(t, s)
                features_queries(t, s)
                if not isinstance(t, int) or t + 1 < NT:
                    transpose_x(t + 1, 1 - s)
                sum_kv(t)
                if not isinstance(t, int) or t >= HG:
                    histogram(t - HG, s)

            def histogram(t, s):
                when(pe, tk_t, oh_ready, t + 1)
                for b in range(HB):
                    last = mm(B[5][:, 0:NT], oh_lo[s][:, :, b], oh_hi[s][:, :, b], start=False, stop=False)
                last.then_inc(oh_free, 1)

            transpose_x(0, 0)
            for t in range(HG):
                project(t, t % 2)
            with pe.Fori(HG // 2, NT // 2) as i:
                for s in range(2):
                    project(i * 2 + s, s)
            project(NT - 1, 0)
            for t in range(NT - HG, NT):
                histogram(t, t % 2)
            mm(B[3][:, 0:P + 1], zeros[:, 0:P], zeros[:, 0:P + 1], start=False, stop=True)
            mm(B[4][:, 0:P + 1], zeros[:, 0:P], zeros[:, 0:P + 1], start=False, stop=True)
            mm(B[5][:, 0:NT], zb[:, 0:P], zb[:, 0:NT], start=False, stop=True).then_inc(sums_done, 1)
            pe.wait_ge(ctile_ready, 1)
            nc.tensor.transpose(B[6][0:CG, 128:256], col[10][:, 0:CG], ident).then_inc(ctile_T, 1)
            pe.wait_ge(unpacked, 1)
            for k in range(4):
                f = (dst_f, lo_f)[k // 2]
                for j in range(4):
                    c = (k % 2) * 4 + j
                    last = nc.tensor.transpose(B[k][:, j * P:(j + 1) * P], f[:, c * P:(c + 1) * P], ident)
                last.then_inc(unp_T, 1)
            pe.wait_ge(unp_out, 1)
            pe.wait_ge(kvbd_ready, 1)
            pe.wait_ge(wo_in, 16)

            def query_products(t):
                when(pe, tk_t, q_terms, t + 1)
                for g in range(KD):
                    for k, term in enumerate((q_exp, q_relu)):
                        last = mm(B[5][:, g * D:g * D + P + NH], term[:, g * P:(g + 1) * P], kv_ext[:, g, :],
                                  start=k == 0, stop=k == 1)
                last.then_inc(q_ps, 1)

            def transpose_mix(t):
                when(pe, tk_t, q_mixed, t + 1)
                for g in range(KD):
                    last = nc.tensor.transpose(B[4][:, g * P:(g + 1) * P], mixed[:, g * P:(g + 1) * P], ident)
                last.then_inc(q_mixedT_ps, 1)

            def mix_out(t):
                when(pe, tk_t, q_mixedT, t + 1)
                when(pe, tk_t, q_added, t)
                mm(B[7][:, 0:D], ones[0:1, :], bo_row, start=True, stop=False)
                for g in range(KD):
                    last = mm(B[7][:, 0:D], mixedT[:, g, :], wo_s[:, g, :], start=False, stop=g == KD - 1)
                last.then_inc(q_out, 1)

            def sum_chunks(n, h):
                when(pe, tk_t, onehot_ready, n + 1)
                when(pe, tk_t, added, n - 1)
                for u in range(UNROLL):
                    if u % 2 == 0:
                        when(pe, tk_t, gath[h][u // 2], (n - h) * (32 // BATCHES) + 32)
                    mm(B[h % 2 * 2 + u // 2][:, (u % 2) * D:(u % 2 + 1) * D], OH[h][:, u, :], G[h][:, u, :],
                       start=True, stop=True).then_inc(seg, 1)

            def sum_step(i):
                attend = not isinstance(i, int) or i < NT
                sum_chunks(i * BATCHES, 0)
                if attend:
                    query_products(i)
                sum_chunks(i * BATCHES + 1, 1)
                if not isinstance(i, int) or i > 0:
                    mix_out(i - 1)
                sum_chunks(i * BATCHES + 2, 2)
                if attend:
                    transpose_mix(i)
                sum_chunks(i * BATCHES + 3, 3)

            sum_step(0)
            with pe.Fori(1, NT) as i:
                sum_step(i)
            sum_step(NT)
            for h in range(BATCHES):
                sum_chunks((NT + 1) * BATCHES + h, h)
            pe.wait_ge(b_one_ready, 1)
            for n in range((NT + 2) * BATCHES, STEPS * BATCHES):
                sum_chunks(n, n % BATCHES)
                e, half = divmod(n - (STEPS * BATCHES - 2 * E), 2)
                if e >= 0:
                    pe.wait_ge(w1_in[e], 16)
                    for k in range(KD):
                        last = mm(B[5 + half][0:E, :], b_one[:, k, e, :], w1_s[:, e, k, half * 512:(half + 1) * 512],
                                  start=e == 0 and k == 0, stop=e == E - 1 and k == KD - 1)
            last.then_inc(b1_ps, 1)
            pe.wait_ge(b1_rows_ready, 1)
            for c in range(KH):
                last = nc.tensor.transpose(B[7][:, c * E:(c + 1) * E], b1_rows[c // 4][:, c % 4 * P:(c % 4 + 1) * P],
                                           ident[0:E, 0:E])
            last.then_inc(b1T_ps, 1)
            pe.wait_ge(router_in, 32)

            def transpose_x2(t, u):
                r = RSLOT[u]
                when(pe, tk_t, x2_ready, t + 1)
                for k in range(KD):
                    last = nc.tensor.transpose(B[r][:, k * P:(k + 1) * P], x2[r][:, k * P:(k + 1) * P], ident)
                last.then_inc(x2T_ps, 1)

            def route_group(g, last_group=False):
                for u in range(RG):
                    t, r = g * RG + u, RSLOT[u]
                    if not last_group or u + 2 < RG:
                        transpose_x2(t + 2, (u + 2) % RG)
                    if u % 2 == 0:
                        when(pe, tk_t, x2T_even, g * ((RG + 1) // 2) + u // 2 + 1)
                    else:
                        when(pe, tk_t, x2T_odd, g * (RG // 2) + u // 2 + 1)
                    for k in range(KD):
                        last = mm(B[4][:, bass.ds(t * E, E)], x2T[r][:, k, :], wr_s[:, k, :], start=k == 0, stop=k == KD - 1)
                    last.then_inc(logit_ps, 1)

            transpose_x2(0, 0)
            transpose_x2(1, 1)
            with pe.Fori(0, NT // RG - 1) as g:
                route_group(g)
            route_group(NT // RG - 1, True)
            pe.wait_ge(pick_ready, 1)
            flat = both.rearrange("p t e -> p (t e)")
            mm(B[2][:, 0:NE], tri, flat, start=True, stop=True)
            mm(B[3][:, 0:NE], ones, flat, start=True, stop=True).then_inc(ranks_ps, 1)

            def slot_tokens(g, s):
                when(pe, tk_t, pc_ready, g + 1)
                for c in range(PC):
                    last = mm(B[5][:, 0:2 * ST], pc_at[s][:, :, c], pc_tokens[:, :, c], start=False, stop=False)
                last.then_inc(pc_used, 1)

            pe.wait_ge(zero_ready, 1)
            mm(B[5][:, 0:2 * ST], zero_row[:, 0:P], zero_row[:, 0:2 * ST], start=True, stop=False)
            slot_tokens(0, 0)
            with pe.Fori(0, PICKS // PC // 2) as i:
                slot_tokens(i * 2 + 1, 1)
                slot_tokens(i * 2 + 2, 0)
            mm(B[5][:, 0:2 * ST], zero_row[:, 0:P], zero_row[:, 0:2 * ST], start=False, stop=True).then_inc(tokens_ps, 1)
            pe.wait_ge(slot_e_in, 16)
            pe.wait_ge(ones3_ready, 1)
            pe.wait_ge(w1_scaled, 1)
            pe.wait_ge(w2_in, 16)
            pe.wait_ge(bias_out, 16)

            def expert_of(t):
                return nc.tensor.value_load(expert_row[0:1, bass.ds(t, 1)], min_val=0, max_val=E - 1)

            def inputs(t, s):
                when(pe, tk_t, xs_in[s], (t - s) * 4 + 16)
                when(pe, tk_t, xsT_ready, t - 1)
                for k in range(KD):
                    last = nc.tensor.transpose(B[6][:, s % 2 * D + k * P:s % 2 * D + (k + 1) * P],
                                               x_in[s][:, k * P:(k + 1) * P], ident)
                last.then_inc(xsT_ps, 1)

            def first_product(t, s):
                when(pe, tk_t, xsT_ready, t + 1)
                when(pe, tk_t, w1_now_ready, t + 1)
                when(pe, tk_t, hid_ready, t - 1)
                for c in range(KH):
                    for k in range(KD):
                        last = mm(B[2 * s + c // 4][:, c % 4 * P:(c % 4 + 1) * P], w1_now[:, k, c * P:(c + 1) * P],
                                  x_inT[s][:, k, :], start=k == 0, stop=k == KD - 1)
                last.then_inc(hid_ps, 1)

            def second_product(t, s):
                e = expert_of(t)
                when(pe, tk_t, y_ready, t)
                when(pe, tk_t, y_bias_in[s], (t - s) * 8 + 16)
                mm(B[7][:, 0:D], ones3, y_bias[s], start=True, stop=False)
                when(pe, tk_t, hid_ready, t + 1)
                for k in range(KH):
                    last = mm(B[7][:, 0:D], hidT[s][:, k, :], W2A[:, bass.ds(e * (KH * D) + k * D, D)],
                              start=False, stop=k == KH - 1)
                last.then_inc(y_ps, 1)

            def step(t, s):
                if not isinstance(t, int) or t + 1 < ST:
                    first_product(t + 1, (s + 1) % 2)
                if not isinstance(t, int) or t + 2 < ST:
                    inputs(t + 2, (s + 2) % 4)
                second_product(t, s % 2)

            inputs(0, 0)
            first_product(0, 0)
            inputs(1, 1)
            step(0, 0)
            with pe.Fori(0, ST // 4 - 1) as i:
                for u in range(4):
                    step(i * 4 + 1 + u, (1 + u) % 4)
            for t in range(ST - 4, ST):
                step(t, t % 4)


def kernel(x, src, dst, L0_gnn_W, L0_mix_wq, L0_mix_bq, L0_mix_wk, L0_mix_bk, L0_mix_wv, L0_mix_bv, L0_mix_wo,
           L0_mix_bo, L0_ffn_Wr, L0_ffn_br, L0_ffn_ln_g, L0_ffn_ln_b, L0_ffn_W1, L0_ffn_b1, L0_ffn_W2, L0_ffn_b2):
    import numpy as np
    import concourse.bacc as bacc
    from concourse.bass_utils import run_bass_kernel_spmd

    src, dst = np.asarray(src), np.asarray(dst)
    n = P * FULL
    arrays = {
        "x": x, "src": src[:n].reshape(P, FULL), "dst": dst[:n].reshape(P, FULL),
        "src_rest": src[n:].reshape(REST, 1), "dst_rest": dst[n:].reshape(REST, 1),
        "gnn_w": L0_gnn_W, "wq": L0_mix_wq, "bq": np.asarray(L0_mix_bq).reshape(KD, P).T,
        "wkv": np.concatenate([np.asarray(L0_mix_wk), np.asarray(L0_mix_wv)], axis=1),
        "bkv": np.concatenate([np.asarray(L0_mix_bk), np.asarray(L0_mix_bv)]).reshape(1, 2 * D),
        "wo": L0_mix_wo, "bo": np.asarray(L0_mix_bo).reshape(1, D), "wr": L0_ffn_Wr,
        "br": np.asarray(L0_ffn_br).reshape(1, E), "ln_gT": np.asarray(L0_ffn_ln_g).T, "ln_bT": np.asarray(L0_ffn_ln_b).T,
        "w1": L0_ffn_W1, "b1": np.asarray(L0_ffn_b1).reshape(E * KH, P).T, "w2": L0_ffn_W2, "b2": L0_ffn_b2,
    }
    arrays = {"in_" + k: np.ascontiguousarray(a) for k, a in arrays.items()}
    nc = bacc.Bacc("TRN2", target_bir_lowering=False, num_devices=1)
    args = [nc.dram_tensor(k, a.shape, mybir.dt.from_np(a.dtype), kind="ExternalInput").ap() for k, a in arrays.items()]
    out = nc.dram_tensor("out_dram", (N_NODES, D), F32, kind="ExternalOutput").ap()
    gps_layer(nc, *args, out)
    r = run_bass_kernel_spmd(nc, [arrays], core_ids=[0])
    return r.results[0]["out_dram"]
```
